# Optimizing a Trainium2 kernel written in Bass

```python
import numpy as np
import jax
import jax.numpy as jnp

def _softmax(x, axis=-1):
    return jax.nn.softmax(x, axis=axis)

def _gelu(x):
    return jax.nn.gelu(x, approximate=True)

def _silu(x):
    return jax.nn.silu(x)

def _sigmoid(x):
    return jax.nn.sigmoid(x)

def _layernorm(x, axis=-1, eps=1e-05):
    m = jnp.mean(x, axis=axis, keepdims=True)
    v = jnp.var(x, axis=axis, keepdims=True)
    return (x - m) / jnp.sqrt(v + eps)

def _scatter_add(tgt, idx, src, axis=0):
    return tgt.at[idx].add(src)

def _segment_sum(src, seg, n):
    return jax.ops.segment_sum(src, seg, n)
kernel_name = 'mk_decoder_preln_d1_seqx_r4_683c66'

def setup_inputs(seed: int=0):
    np.random.seed(seed)
    _w = jnp.asarray

    def _rec_inputs():
        import jax
        import jax.numpy as jnp
        _rk = jax.random.key(seed)
        x = 7.22e-05 + 1 * jax.random.normal(jax.random.fold_in(_rk, 1), (32, 128, 256), jnp.float32)
        _lenS = 128 - jax.random.randint(jax.random.fold_in(_rk, 7), (32,), 0, max(1, 128 // 4) + 1, jnp.int32)
        _lenS2 = 128 - jax.random.randint(jax.random.fold_in(_rk, 8), (32,), 0, max(1, 128 // 4) + 1, jnp.int32)
        _ctx_1024P = jax.random.normal(jax.random.fold_in(_rk, 11), (32, 16, 256), jnp.float32)
        _ctx_1024c = jax.random.dirichlet(jax.random.fold_in(_rk, 511), 0.3 * jnp.ones((16,), jnp.float32), (32, 128))
        _ctx_1024t = jnp.einsum('bsk,bkd->bsd', _ctx_1024c, _ctx_1024P)
        _ctx_1024t = _ctx_1024t * jax.lax.rsqrt(jnp.mean(jnp.square(_ctx_1024t)) + 1e-12) * 0.953939
        ctx_1024 = 4.13588e-05 + 0.999923 * (_ctx_1024t + 0.3 * jax.random.normal(jax.random.fold_in(_rk, 611), (32, 128, 256), jnp.float32))
        return (x, ctx_1024)
    x, ctx_1024 = _rec_inputs()

    def _L0_attn_setup():
        import jax, jax.numpy as jnp
        import numpy as np
        EPS = 1e-06
        NUM_HEADS = 16

        def _phi(x):
            return jax.nn.elu(x) + 1.0
        key = jax.random.key(seed)
        ks = jax.random.split(key, 5)
        B, S, D = (2, 512, 256)
        scale = 1.0 / np.sqrt(D)
        return {'x': jax.random.normal(ks[0], (B, S, D), dtype=jnp.float32), 'Wq': jax.random.normal(ks[1], (D, D), dtype=jnp.float32) * scale, 'bq': jnp.zeros((D,), dtype=jnp.float32), 'Wk': jax.random.normal(ks[2], (D, D), dtype=jnp.float32) * scale, 'bk': jnp.zeros((D,), dtype=jnp.float32), 'Wv': jax.random.normal(ks[3], (D, D), dtype=jnp.float32) * scale, 'bv': jnp.zeros((D,), dtype=jnp.float32), 'Wo': jax.random.normal(ks[4], (D, D), dtype=jnp.float32) * scale, 'bo': jnp.zeros((D,), dtype=jnp.float32)}
    _L0_attn_all = _L0_attn_setup()
    _L0_attn_in = {k: v for k, v in _L0_attn_all.items() if k in ('Wq', 'bq', 'Wk', 'bk', 'Wv', 'bv', 'Wo', 'bo')}
    del _L0_attn_all

    def _L0_xattn_setup():
        import jax, jax.numpy as jnp
        import numpy as np
        EMBED_DIM = 256
        NUM_HEADS = 16
        HEAD_DIM = EMBED_DIM // NUM_HEADS

        def _xavier_uniform(key, out_dim, in_dim):
            limit = jnp.sqrt(6.0 / (in_dim + out_dim)).astype(jnp.float32)
            return jax.random.uniform(key, (out_dim, in_dim), jnp.float32, -limit, limit)
        key = jax.random.key(seed)
        ks = jax.random.split(key, 6)
        B, S, D = (4, 512, EMBED_DIM)
        return {'query': jax.random.normal(ks[0], (B, S, D), jnp.float32), 'key': jax.random.normal(ks[1], (B, S, D), jnp.float32), 'value': jax.random.normal(ks[2], (B, S, D), jnp.float32), 'Wq': _xavier_uniform(ks[3], D, D), 'Wk': _xavier_uniform(ks[4], D, D), 'Wv': _xavier_uniform(ks[5], D, D)}
    _L0_xattn_all = _L0_xattn_setup()
    _L0_xattn_in = {k: v for k, v in _L0_xattn_all.items() if k in ('Wq', 'Wk', 'Wv')}
    del _L0_xattn_all

    def _L0_ffn_setup():
        import jax, jax.numpy as jnp
        import numpy as np
        D_IN, D_HID = (256, 1024)

        def _ternary(key, shape):
            return jax.random.randint(key, shape, -1, 2).astype(jnp.float32)

        def _tlin(x, w, s):
            return jnp.einsum('bsi,oi->bso', x, w) * s
        key = jax.random.key(seed)
        ks = jax.random.split(key, 12)
        inv = lambda fan: 1.0 / np.sqrt(fan).astype(np.float32)
        return {'x': jax.random.normal(ks[0], (4, 512, D_IN), dtype=jnp.float32), 'w1_w': _ternary(ks[1], (D_HID, D_IN)), 'w1_s': jax.random.uniform(ks[2], (D_HID,), dtype=jnp.float32) * inv(D_IN), 'w2_w': _ternary(ks[3], (D_HID, D_IN)), 'w2_s': jax.random.uniform(ks[4], (D_HID,), dtype=jnp.float32) * inv(D_IN), 'h1_w': _ternary(ks[5], (D_HID, D_HID)), 'h1_s': jax.random.uniform(ks[6], (D_HID,), dtype=jnp.float32) * inv(D_HID), 'h2_w': _ternary(ks[7], (D_HID, D_HID)), 'h2_s': jax.random.uniform(ks[8], (D_HID,), dtype=jnp.float32) * inv(D_HID), 'w3_w': _ternary(ks[9], (D_IN, D_HID)), 'w3_s': jax.random.uniform(ks[10], (D_IN,), dtype=jnp.float32) * inv(D_HID)}
    _L0_ffn_all = _L0_ffn_setup()
    _L0_ffn_in = {k: v for k, v in _L0_ffn_all.items() if k in ('w1_w', 'w1_s', 'w2_w', 'w2_s', 'h1_w', 'h1_s', 'h2_w', 'h2_s', 'w3_w', 'w3_s')}
    del _L0_ffn_all
    return {'x': x, 'ctx_1024': ctx_1024, 'L0_attn_Wq': _L0_attn_in['Wq'], 'L0_attn_bq': _L0_attn_in['bq'], 'L0_attn_Wk': _L0_attn_in['Wk'], 'L0_attn_bk': _L0_attn_in['bk'], 'L0_attn_Wv': _L0_attn_in['Wv'], 'L0_attn_bv': _L0_attn_in['bv'], 'L0_attn_Wo': _L0_attn_in['Wo'], 'L0_attn_bo': _L0_attn_in['bo'], 'L0_xattn_Wq': _L0_xattn_in['Wq'], 'L0_xattn_Wk': _L0_xattn_in['Wk'], 'L0_xattn_Wv': _L0_xattn_in['Wv'], 'L0_ffn_w1_w': _L0_ffn_in['w1_w'], 'L0_ffn_w1_s': _L0_ffn_in['w1_s'], 'L0_ffn_w2_w': _L0_ffn_in['w2_w'], 'L0_ffn_w2_s': _L0_ffn_in['w2_s'], 'L0_ffn_h1_w': _L0_ffn_in['h1_w'], 'L0_ffn_h1_s': _L0_ffn_in['h1_s'], 'L0_ffn_h2_w': _L0_ffn_in['h2_w'], 'L0_ffn_h2_s': _L0_ffn_in['h2_s'], 'L0_ffn_w3_w': _L0_ffn_in['w3_w'], 'L0_ffn_w3_s': _L0_ffn_in['w3_s']}

def reference(x, ctx_1024, L0_attn_Wq, L0_attn_bq, L0_attn_Wk, L0_attn_bk, L0_attn_Wv, L0_attn_bv, L0_attn_Wo, L0_attn_bo, L0_xattn_Wq, L0_xattn_Wk, L0_xattn_Wv, L0_ffn_w1_w, L0_ffn_w1_s, L0_ffn_w2_w, L0_ffn_w2_s, L0_ffn_h1_w, L0_ffn_h1_s, L0_ffn_h2_w, L0_ffn_h2_s, L0_ffn_w3_w, L0_ffn_w3_s):
    import jax
    import jax.numpy as jnp

    def _L0_attn_ref(x, Wq, bq, Wk, bk, Wv, bv, Wo, bo):
        import jax, jax.numpy as jnp
        import numpy as np
        EPS = 1e-06
        NUM_HEADS = 16

        def _phi(x):
            return jax.nn.elu(x) + 1.0
        B, S, D = x.shape
        H = NUM_HEADS
        hd = D // H
        q = (x @ Wq.T + bq).reshape(B, S, H, hd).transpose(0, 2, 1, 3)
        k = (x @ Wk.T + bk).reshape(B, S, H, hd).transpose(0, 2, 1, 3)
        v = (x @ Wv.T + bv).reshape(B, S, H, hd).transpose(0, 2, 1, 3)
        q = _phi(q)
        k = _phi(k)
        kv_cum = jnp.cumsum(k[..., :, None] * v[..., None, :], axis=2)
        k_cum = jnp.cumsum(k, axis=2)
        num = jnp.einsum('bhsd,bhsde->bhse', q, kv_cum)
        den = jnp.einsum('bhsd,bhsd->bhs', q, k_cum)
        out = num / (den[..., None] + EPS)
        out = out.transpose(0, 2, 1, 3).reshape(B, S, D)
        return out @ Wo.T + bo

    def _L0_xattn_ref(query, key, value, Wq, Wk, Wv):
        import jax, jax.numpy as jnp
        import numpy as np
        EMBED_DIM = 256
        NUM_HEADS = 16
        HEAD_DIM = EMBED_DIM // NUM_HEADS

        def _xavier_uniform(key, out_dim, in_dim):
            limit = jnp.sqrt(6.0 / (in_dim + out_dim)).astype(jnp.float32)
            return jax.random.uniform(key, (out_dim, in_dim), jnp.float32, -limit, limit)
        B, S, _ = query.shape
        H, Dh = (NUM_HEADS, HEAD_DIM)
        q = (query @ Wq.T).reshape(B, S, H, Dh).transpose(0, 2, 1, 3)
        k = (key @ Wk.T).reshape(B, S, H, Dh).transpose(0, 2, 1, 3)
        v = (value @ Wv.T).reshape(B, S, H, Dh).transpose(0, 2, 1, 3)
        scale = 1.0 / jnp.sqrt(jnp.asarray(Dh, q.dtype))
        logits = jnp.einsum('bhqd,bhkd->bhqk', q, k) * scale
        attn = jax.nn.softmax(logits, axis=-1)
        out = jnp.einsum('bhqk,bhkd->bhqd', attn, v)
        out = out.transpose(0, 2, 1, 3).reshape(B, S, H * Dh)
        return out

    def _L0_ffn_ref(x, w1_w, w1_s, w2_w, w2_s, h1_w, h1_s, h2_w, h2_s, w3_w, w3_s):
        import jax, jax.numpy as jnp
        import numpy as np
        D_IN, D_HID = (256, 1024)

        def _ternary(key, shape):
            return jax.random.randint(key, shape, -1, 2).astype(jnp.float32)

        def _tlin(x, w, s):
            return jnp.einsum('bsi,oi->bso', x, w) * s
        h = jax.nn.silu(_tlin(x, w1_w, w1_s)) * _tlin(x, w2_w, w2_s)
        h = jax.nn.gelu(_tlin(h, h1_w, h1_s), approximate=False)
        h = jax.nn.gelu(_tlin(h, h2_w, h2_s), approximate=False)
        return _tlin(h, w3_w, w3_s)
    x = x + _L0_attn_ref(_layernorm(x, axis=-1), L0_attn_Wq, L0_attn_bq, L0_attn_Wk, L0_attn_bk, L0_attn_Wv, L0_attn_bv, L0_attn_Wo, L0_attn_bo)
    x = x + _L0_xattn_ref(_layernorm(x, axis=-1), ctx_1024, ctx_1024, L0_xattn_Wq, L0_xattn_Wk, L0_xattn_Wv)
    x = x + _L0_ffn_ref(_layernorm(x, axis=-1), L0_ffn_w1_w, L0_ffn_w1_s, L0_ffn_w2_w, L0_ffn_w2_s, L0_ffn_h1_w, L0_ffn_h1_s, L0_ffn_h2_w, L0_ffn_h2_s, L0_ffn_w3_w, L0_ffn_w3_s)
    return x

_drawn_inputs = setup_inputs


def setup_inputs(seed=0):
    import zlib

    import numpy as np

    out = dict(_drawn_inputs(seed))
    spreads = {'L0_attn_bq': (0.0, 0.1),
     'L0_attn_bk': (0.0, 0.1),
     'L0_attn_bv': (0.0, 0.1),
     'L0_attn_bo': (0.0, 0.1)}
    factors = {}
    for name, (base, spread) in spreads.items():
        noise = np.random.default_rng([zlib.crc32(name.encode()), seed]).standard_normal(out[name].shape)
        drawn = base * np.exp(spread * noise) if base else spread * noise
        out[name] = jnp.asarray(drawn.astype(out[name].dtype))
    for name, factor in factors.items():
        out[name] = (out[name] * factor).astype(out[name].dtype)
    return out
```

```python
import concourse.bass as bass
from concourse import mybir
from contextlib import ExitStack


def decoder_layer_program(nc, x, ctxT, wqT, wkT, wvT, woT, bq, bk, bv, bo, xqT, xkT, xvT,
                          w12, h1, h2, w3, s1, s2, sh1, sh2, s3, consts, outT):
    F32, F32R, BF16, I32 = mybir.dt.float32, mybir.dt.float32r, mybir.dt.bfloat16, mybir.dt.int32
    ALU, ACT, AX = mybir.AluOpType, mybir.ActivationFunctionType, mybir.AxisListType

    P = 128
    B, S, D = x.shape
    H, HD = 16, 16
    HID = s1.shape[0]
    C = D // P
    GB = 4
    T = GB * S
    G = B // GB
    KH = HID // P
    LN_EPS, ATT_EPS, SCALE = 1e-5, 1e-6, HD ** -0.5
    NU = 4 * GB

    x2T_d = nc.dram_tensor("x2T_scratch", [D, B * S], F32, kind="Internal").ap()
    xnT_d = nc.dram_tensor("xn3T_scratch", [D, B * S], F32, kind="Internal").ap()

    def tokens(ap, g):
        v = ap.rearrange("(c p) t -> p c t", p=P)
        if isinstance(g, int):
            return v[:, :, g * T:(g + 1) * T]
        return v[:, :, bass.ds(g * T, T)]

    outer = ExitStack()

    def sem(name):
        return outer.enter_context(nc.semaphore(name))

    with outer:
        flag = outer.enter_context(nc.sbuf_tensor("inexact_flag", [1, 1], I32))
        flag_ready = sem("flag_ready")
        stored = sem("scratch_stored")

        ctx = ExitStack()
        with ctx:
            def sb(name, shape, dt=F32):
                return ctx.enter_context(nc.sbuf_tensor(name, shape, dt))

            wq, wk, wv, wo = (sb(n, [P, C, D]) for n in ("wq", "wk", "wv", "wo"))
            xwq, xwk, xwv = (sb(n, [P, C, D]) for n in ("xwq", "xwk", "xwv"))
            NC_ = consts.shape[1]
            cst = sb("cst", [P, NC_])
            ident = cst[:, 0:128]
            causal = cst[:, 128:256]
            headmask = cst[:, 320:324]
            selcol = cst[:, 324:340]
            bqc, bkc, bq1, bk1 = (sb(n, [P, C]) for n in ("bqc", "bkc", "bq1", "bk1"))
            bvb, bob = sb("bvb", [P, D]), sb("bob", [P, D])
            onepad = sb("onepad", [P, 64])
            identb = sb("identb", [P, P], BF16)
            sel = sb("sel", [P, H, P], BF16)
            unused = sb("unused", [P, 1])
            mhalf, eps = sb("mhalf", [P, 1]), sb("eps", [P, 1])

            x_in = sb("x_in", [P, GB, D])
            xn1 = sb("xn1", [P, GB, D])
            xn1T = sb("xn1T", [P, C, T])
            xb = sb("xb", [P, GB, D])
            x1 = sb("x1", [P, GB, D])
            xn2 = sb("xn2", [P, GB, D])
            xn2T = sb("xn2T", [P, C, T])
            x2 = sb("x2", [P, GB, D])
            xn3 = sb("xn3", [P, GB, D])
            x2T = sb("x2T", [P, C, T])
            xn3T = sb("xn3T", [P, C, T])
            ctxs = sb("ctxs", [P, C, T])
            stats = sb("stats", [P, 3, GB, 6])
            mv = sb("mv", [P, 3, GB, 2])
            ve = sb("ve", [P, 3, GB])
            rstd = sb("rstd", [P, 3, GB])

            ex = sb("ex", [P, 2, T])
            q = sb("q", [P, C, T])
            k = sb("k", [P, C, T])
            qm = sb("qm", [P, C, 4, T])
            v = sb("v", [P, GB, H // 2, 64])
            xqr = sb("xqr", [P, C, T], F32R)
            xqm = sb("xqm", [P, C, 4, T])
            xk = sb("xk", [P, C, T])
            xkm = sb("xkm", [P, C, 4, T], F32R)
            xv = sb("xv", [P, GB, H // 2, 64])
            NA = 8
            att = sb("att", [P, NA, 4, S])
            den = sb("den", [P, 2, D])
            rec = sb("rec", [P, 2, D])
            oT = sb("oT", [P, 2, C, S])
            oxT = sb("oxT", [P, 2, C, S])
            mx = sb("mx", [P, 2, H])
            nshift = sb("nshift", [P, 2, 2, H], BF16)
            shiftT = sb("shiftT", [P, 2, S], BF16)
            NX = 2 * C * P + 2 * KH * P + C * P
            wbits = sb("weight_bits", [P, NX], I32)
            low = sb("low_bits", [P, G + 1])

            bank = [ctx.enter_context(nc.psum_tensor(f"bank{n}", [P, 512], F32)) for n in range(8)]
            pb, sbk, ob = bank[0:4], bank[4:6], bank[6:8]

            weights = sem("weights_loaded")
            const_ready = sem("const_ready")
            act_const = sem("act_const")
            x_loaded, ctx_loaded = sem("x_loaded"), sem("ctx_loaded")
            bn_done = sem("bn_stats_done")
            LNS = [dict((w, sem(f"ln{n + 1}_{w}")) for w in ("mean_var", "ve", "rstd", "xn", "turned", "xnT"))
                   for n in range(3)]
            xb_done = sem("xb_done")
            qk_psum, qk_exp, qk_min, qk_done = sem("qk_psum"), sem("qk_exp"), sem("qk_min"), sem("qk_done")
            qm_done = sem("qm_done")
            v_psum, v_done = sem("v_psum"), sem("v_done")
            lin_s, lin_a = sem("lin_scores"), sem("lin_masked")
            av_done = sem("av_done")
            den_done, rec_done = sem("lin_den"), sem("rec_done")
            lin_o, wo_psum, x1_done = sem("lin_o"), sem("wo_psum"), sem("x1_done")
            xq_psum, xqr_done, xqm_done = sem("xq_psum"), sem("xqr_done"), sem("xqm_done")
            xk_psum, xk_done, xkm_done = sem("xk_psum"), sem("xk_done"), sem("xkm_done")
            xv_psum, xv_done = sem("xv_psum"), sem("xv_done")
            max_psum, max_done = sem("max_psum"), sem("max_done")
            sh_hi, sh_lo = sem("shift_hi"), sem("shift_lo")
            sh_psum, sh_done = sem("shift_turned"), sem("shift_done")
            x_s, x_e = sem("x_scores"), sem("x_exp")
            x_rec, x_o, ox_psum, x2_done = sem("x_rec"), sem("x_o"), sem("ox_turned"), sem("x2_done")
            x2T_psum, x2T_done = sem("x2T_psum"), sem("x2T_done")
            LN1, LN2, LN3 = LNS
            wbits_loaded, wbits_read, low_done, low_psum = (
                sem(n) for n in ("wbits_loaded", "wbits_read", "low_done", "low_psum"))

            tail = ["ox3", "x2T0", "x2T1", "xn3T0", "xn3T1"]
            ahead = ["ln1T0", "ln1T1", "q0", "q1", "k0", "k1", "v0", "v1"]
            cross = ["ln2T0", "ln2T1", "xq0", "xq1", "xk0", "xk1", "xv0", "xv1",
                     "sh0", "sh1", "sh2", "ox0", "sh3", "ox1", "ox2"]
            linear = ["wo0", "wo1", "wo2"] + ahead[:2] + ["wo3"] + ahead[2:]
            lists = {
                "start": ahead,
                "first": linear + cross,
                "mid": tail + linear + cross,
                "last": tail + ["wo0", "wo1", "wo2", "wo3"] + cross,
                "end": tail,
            }
            before = {"first": "start", "mid": "first", "last": "mid", "end": "last"}
            assert lists["first"][-4:] == lists["mid"][-4:] == lists["last"][-4:] and len(lists["mid"]) % 4 == 0
            begin = {"start": 0, "first": len(ahead)}
            begin["mid"] = begin["first"] + len(lists["first"])
            begin["last"] = begin["mid"] + (G - 2) * len(lists["mid"])
            begin["end"] = begin["last"] + len(lists["last"])

            freed = {"ox": (x2_done, GB), "x2T": (x2T_done, C), "xn3T": (LN3["xnT"], C),
                     "ln1T": (LN1["xnT"], C), "q": (qk_done, 2 * C), "k": (qk_done, 2 * C), "v": (v_done, 2),
                     "ln2T": (LN2["xnT"], C), "xq": (xqm_done, 4 * C), "xk": (xk_done, C), "xv": (xv_done, 2),
                     "wo": (x1_done, GB), "sh": (sh_done, GB)}

            def pbank(kind, use):
                return pb[(begin[kind] + lists[kind].index(use)) % 4]

            def wait_pbank(eng, kind, i, use):
                pos = lists[kind].index(use) - 4
                if pos < 0 and kind == "start":
                    return
                turn = i
                if pos < 0:
                    turn = i if kind == "first" else i - 1
                    kind = before[kind]
                prev = lists[kind][pos]
                name, n = prev[:-1], int(prev[-1])
                s, per = freed[name]
                group = 0 if kind == "start" else turn - 1 if prev in tail else turn + 1 if prev in ahead else turn
                at = {"k": C + n, "xq": 4 * n + 3}.get(name, n)
                eng.wait_ge(s, per * group + at + 1)

            s_order = [("lin", n) for n in range(NU)] + [("max", n) for n in range(8)]
            for n in range(NU):
                s_order.append(("exp", n))
                if n + 8 < NU:
                    s_order.append(("max", n + 8))
            s_freed = {"lin": lin_a, "max": max_done, "exp": x_e}

            def sbank(part, n):
                return sbk[s_order.index((part, n)) % 2]

            def wait_sbank(eng, i, part, n):
                pos = s_order.index((part, n)) - 2
                part, n = s_order[pos]
                j = i - 1 if pos < 0 else i
                if not (isinstance(j, int) and j < 0):
                    eng.wait_ge(s_freed[part], NU * j + n + 1)

            def wait_obank(eng, i, part, b):
                pos = GB * part + b - 2
                j = i - 1 if pos < 0 else i
                if not (isinstance(j, int) and j < 0):
                    eng.wait_ge([lin_o, x_o][pos // GB % 2], GB * j + pos % GB + 1)

            def att_slot(part, n):
                return att[:, (NU * part + n) % NA, :, :]

            def wait_att(eng, i, part, n):
                value = NU * i + (NU * part + n - NA) // 2 + 1
                if not (isinstance(value, int) and value <= 0):
                    eng.wait_ge(av_done, value)

            def head_columns(vt, b0, nb):
                return vt[:, b0:b0 + nb, :, :].rearrange("p b r (z d) -> p (b r) z d", d=HD)[:, :, 0::3, :]

            def each_group(eng, body):
                body("first", 0)
                with eng.Fori(1, G - 1) as i:
                    body("mid", i)
                body("last", G - 1)

            def unit(n):
                return n // 4, n // 2 % 2, 64 * (n % 2)

            block = ctx.enter_context(nc.Block())

            @block.sync
            def _(eng):
                x_v = x.rearrange("(g b) s d -> g s b d", b=GB)

                def load_x(g):
                    src = x_v[g] if isinstance(g, int) else x_v[bass.ds(g, 1)].rearrange("g s b d -> (g s) b d")
                    eng.dma_start(x_in[:, :, :], src).then_inc(x_loaded, 16)

                def load_bits(g):
                    if not (isinstance(g, int) and g == 0):
                        eng.wait_ge(wbits_read, g)
                    at = 0
                    for w in (w12.rearrange("p m z k o -> p m (z k o)"), h1.rearrange("p m k o -> p m (k o)"),
                              h2.rearrange("p m k o -> p m (k o)"),
                              w3.rearrange("p m (k2 k) o -> p (m k2) (k o)", k2=G // C)):
                        n = w.shape[2]
                        src = w[:, g, :] if isinstance(g, int) else w[:, bass.ds(g, 1), :].rearrange("p m n -> p (m n)")
                        eng.dma_start(wbits[:, at:at + n], src.bitcast(I32)).then_inc(wbits_loaded, 16)
                        at += n
                    assert at == NX

                load_x(0)
                eng.dma_start(cst[:, :], consts).then_inc(weights, 16)
                for dst, src in ((wq, wqT), (wk, wkT), (wv, wvT), (wo, woT), (xwq, xqT), (xwk, xkT), (xwv, xvT)):
                    eng.dma_start(dst[:, :, :], src.rearrange("(c p) o -> p c o", p=P)).then_inc(weights, 16)
                with nc.allow_non_contiguous_dma(reason="biases, once"):
                    eng.dma_start(bqc[:, :], bq.rearrange("(c p) -> p c", p=P)).then_inc(weights, 16)
                    eng.dma_start(bkc[:, :], bk.rearrange("(c p) -> p c", p=P)).then_inc(weights, 16)
                eng.dma_start(bvb[:, :], bv.partition_broadcast(P)).then_inc(weights, 16)
                eng.dma_start(bob[:, :], bo.partition_broadcast(P)).then_inc(weights, 16)
                eng.dma_start(ctxs[:, :, :], tokens(ctxT, 0)).then_inc(ctx_loaded, 16)

                def store(g):
                    eng.wait_ge(x2T_done, C * g + C)
                    eng.dma_start(tokens(x2T_d, g), x2T[:, :, :]).then_inc(stored, 16)
                    eng.wait_ge(LN3["xnT"], C * g + C)
                    eng.dma_start(tokens(xnT_d, g), xn3T[:, :, :]).then_inc(stored, 16)

                def body(kind, i):
                    if kind != "last":
                        eng.wait_ge(xb_done, i + 1)
                        eng.wait_ge(LN1["xn"], GB * i + GB)
                        load_x(i + 1)
                    load_bits(i)
                    if kind != "first":
                        store(i - 1)
                    if kind != "last":
                        eng.wait_ge(xk_psum, C * i + C)
                        eng.wait_ge(xv_psum, 2 * i + 2)
                        eng.dma_start(ctxs[:, :, :], tokens(ctxT, i + 1)).then_inc(ctx_loaded, 16)

                each_group(eng, body)
                store(G - 1)
                eng.wait_ge(stored, 32 * G)

            NW = 16 * 12

            @block.gpsimd
            def _(eng):
                eng.memset(v[:, :, :, :], 0.0).then_inc(const_ready, 1)
                eng.memset(xv[:, :, :, :], 0.0).then_inc(const_ready, 1)
                eng.memset(shiftT[:, :, :], 0.0).then_inc(const_ready, 1)
                eng.memset(mhalf[:, :], -0.5).then_inc(const_ready, 1)
                eng.memset(eps[:, :], LN_EPS).then_inc(const_ready, 1)
                eng.wait_ge(const_ready, 5)
                eng.wait_ge(weights, NW)

                def ln_rstd(ln, n, g, b):
                    eng.wait_ge(ln["mean_var"], GB * g + b + 1)
                    eng.tensor_tensor(ve[:, n, b:b + 1], mv[:, n, b, 1:2], eps[:, 0:1], ALU.add).then_inc(ln["ve"], 1)
                    eng.wait_ge(ln["ve"], GB * g + b + 1)
                    eng.tensor_tensor(rstd[:, n, b:b + 1], ve[:, n, b:b + 1], mhalf[:, 0:1], ALU.pow)\
                       .then_inc(ln["rstd"], 1)

                def residual_bias(g):
                    eng.wait_ge(x_loaded, 16 * g + 16)
                    if not (isinstance(g, int) and g == 0):
                        eng.wait_ge(x1_done, GB * g)
                    eng.tensor_tensor(xb[:, :, :], x_in[:, :, :],
                                      bob[:, :].rearrange("p (o d) -> p o d", o=1).broadcast_to([P, GB, D]),
                                      ALU.add).then_inc(xb_done, 1)

                for b in range(GB):
                    ln_rstd(LN1, 0, 0, b)
                residual_bias(0)

                def body(kind, i):
                    if kind != "first":
                        ln_rstd(LN3, 2, i - 1, 3)
                    for b in range(GB):
                        if kind != "last":
                            ln_rstd(LN1, 0, i + 1, b)
                        if b >= 1:
                            ln_rstd(LN2, 1, i, b - 1)
                    ln_rstd(LN2, 1, i, 3)
                    if kind != "last":
                        residual_bias(i + 1)
                    for b in range(3):
                        ln_rstd(LN3, 2, i, b)

                each_group(eng, body)
                ln_rstd(LN3, 2, G - 1, 3)

            @block.scalar
            def _(eng):
                eng.wait_ge(weights, NW)
                eng.preload_act_table(ACT.Exp)
                eng.activation(identb[:, :], ident, ACT.Copy).then_inc(act_const, 1)
                eng.activation(sel[:, :, :], selcol.rearrange("p (h o) -> p h o", o=1).broadcast_to([P, H, P]),
                               ACT.Copy).then_inc(act_const, 1)
                eng.activation(onepad[:, :], cst[:, 256:320], ACT.Copy).then_inc(act_const, 1)

                def turned(kind, i, g, ln, name, dst, last_use, per):
                    for c in range(C):
                        eng.wait_ge(ln["turned"], C * g + c + 1)
                        if c == 0 and not (isinstance(g, int) and g == 0):
                            eng.wait_ge(last_use, per * g)
                        eng.activation(dst[:, c, :], pbank(kind, f"{name}{c}")[:, :], ACT.Copy)\
                           .then_inc(ln["xnT"], 1)

                def qk_exp_(kind, g):
                    for n, (t, use) in enumerate((t, f"{t}{c}") for t in "qk" for c in range(C)):
                        c = n % C
                        eng.wait_ge(qk_psum, 2 * C * g + n + 1)
                        if not (isinstance(g, int) and g == 0 and n < 2):
                            eng.wait_ge(qk_done, 2 * C * g + n - 1)
                        eng.activation(ex[:, n % 2, :], pbank(kind, use)[:, :], ACT.Exp,
                                       bias=(bqc if t == "q" else bkc)[:, c:c + 1]).then_inc(qk_exp, 1)

                def q_heads(g):
                    for c in range(C):
                        eng.wait_ge(qk_done, 2 * C * g + c + 1)
                        if c == 0 and not (isinstance(g, int) and g == 0):
                            eng.wait_ge(lin_s, NU * g)
                        for j in range(4):
                            eng.activation(qm[:, c, j, :], q[:, c, :], ACT.Copy, scale=headmask[:, j:j + 1])\
                               .then_inc(qm_done, 1)

                def lin_den(i, b):
                    eng.wait_ge(av_done, NU * i + 2 * b + 2)
                    if not (isinstance(i, int) and i == 0 and b < 2):
                        eng.wait_ge(rec_done, GB * i + b - 1)
                    eng.activation(den[:, b % 2, :], ob[b % 2][:, 2 * S:4 * S], ACT.Copy, bias=ATT_EPS)\
                       .then_inc(den_done, 1)

                def xq_heads(kind, i):
                    for c in range(C):
                        eng.wait_ge(xq_psum, C * i + c + 1)
                        if c == 0 and not (isinstance(i, int) and i == 0):
                            eng.wait_ge(x_s, NU * i)
                        eng.wait_ge(xqr_done, C * i + c + 1)
                        for j in range(4):
                            eng.activation(xqm[:, c, j, :], pbank(kind, f"xq{c}")[:, :], ACT.Copy,
                                           scale=headmask[:, j:j + 1]).then_inc(xqm_done, 1)

                def xk_out(kind, i):
                    for c in range(C):
                        eng.wait_ge(xk_psum, C * i + c + 1)
                        if c == 0 and not (isinstance(i, int) and i == 0):
                            eng.wait_ge(x_s, NU * i)
                            eng.wait_ge(xkm_done, 4 * C * i)
                        eng.activation(xk[:, c, :], pbank(kind, f"xk{c}")[:, :], ACT.Copy).then_inc(xk_done, 1)

                def xv_out(kind, i):
                    for n in range(2):
                        eng.wait_ge(xv_psum, 2 * i + n + 1)
                        if n == 0 and not (isinstance(i, int) and i == 0):
                            eng.wait_ge(av_done, NU * i)
                        if n == 0 and isinstance(i, int) and i == 0:
                            eng.wait_ge(const_ready, 5)
                        eng.activation(head_columns(xv, 2 * n, 2),
                                       pbank(kind, f"xv{n}")[:, :].rearrange("p (r z d) -> p r z d", z=2, d=HD),
                                       ACT.Copy).then_inc(xv_done, 1)

                def shift_out(kind, i, b):
                    eng.wait_ge(sh_psum, GB * i + b + 1)
                    if not (isinstance(i, int) and i == 0 and b < 2):
                        eng.wait_ge(x_s, NU * i + 4 * (b - 1))
                    eng.activation(shiftT[0:32, b % 2, :],
                                   pbank(kind, f"sh{b}")[0:32, 0:S // 2].bitcast(BF16), ACT.Copy)\
                       .then_inc(sh_done, 1)

                def exponentials(i, n):
                    eng.wait_ge(x_s, NU * i + n + 1)
                    wait_att(eng, i, 1, n)
                    eng.activation(att_slot(1, n),
                                   sbank("exp", n)[:, :].rearrange("p (j s) -> p j s", j=4), ACT.Exp, scale=SCALE)\
                       .then_inc(x_e, 1)

                def x2_out(kind, i, g):
                    for c in range(C):
                        eng.wait_ge(x2T_psum, C * g + c + 1)
                        if c == 0 and not (isinstance(g, int) and g == 0):
                            eng.wait_ge(stored, 32 * g)
                        eng.activation(x2T[:, c, :], pbank(kind, f"x2T{c}")[:, :], ACT.Copy).then_inc(x2T_done, 1)
                    turned(kind, i, g, LN3, "xn3T", xn3T, stored, 32)

                turned("start", 0, 0, LN1, "ln1T", xn1T, v_psum, 2)
                qk_exp_("start", 0)
                q_heads(0)

                def body(kind, i):
                    for b in range(3):
                        lin_den(i, b)
                        if b == 0 and kind != "first":
                            x2_out(kind, i, i - 1)
                    if kind != "last":
                        turned(kind, i, i + 1, LN1, "ln1T", xn1T, v_psum, 2)
                    lin_den(i, 3)
                    if kind != "last":
                        qk_exp_(kind, i + 1)
                        q_heads(i + 1)
                    turned(kind, i, i, LN2, "ln2T", xn2T, xq_psum, C)
                    xq_heads(kind, i)
                    xk_out(kind, i)
                    xv_out(kind, i)
                    shift_out(kind, i, 0)
                    for n in range(NU):
                        exponentials(i, n)
                        if n % 4 == 3 and n < NU - 1:
                            shift_out(kind, i, n // 4 + 1)

                each_group(eng, body)
                x2_out("end", G, G - 1)

            @block.vector
            def _(eng):
                eng.wait_ge(weights, NW)
                eng.tensor_scalar(bq1[:, :], bqc[:, :], 1.0, None, ALU.add).then_inc(bn_done, 1)
                eng.tensor_scalar(bk1[:, :], bkc[:, :], 1.0, None, ALU.add).then_inc(bn_done, 1)
                eng.wait_ge(bn_done, 2)

                def mean_var(ln, n, src, g, b, count):
                    eng.bn_stats(stats[:, n, b, :], src[:, b, :]).then_inc(bn_done, 1)
                    eng.wait_ge(bn_done, count)
                    eng.memset(unused[0:1, :], 0.0)
                    eng.bn_aggr(mv[:, n, b, :], stats[:, n, b, :]).then_inc(ln["mean_var"], 1)

                def normalise(ln, n, dst, src, g, b, per, last):
                    eng.wait_ge(ln["rstd"], GB * g + b + 1)
                    if b == 0 and not (isinstance(g, int) and g == 0):
                        eng.wait_ge(last, per * g)
                    eng.tensor_scalar(dst[:, b, :], src[:, b, :], mv[:, n, b, 0:1], rstd[:, n, b:b + 1],
                                      ALU.subtract, ALU.mult).then_inc(ln["xn"], 1)

                def ln1(g, b, count):
                    if b == 0:
                        eng.wait_ge(x_loaded, 16 * g + 16)
                    mean_var(LN1, 0, x_in, g, b, count)

                def qk_out(kind, g):
                    for n in range(2 * C):
                        t, c = "qk"[n // C], n % C
                        eng.wait_ge(qk_exp, 2 * C * g + n + 1)
                        eng.tensor_scalar(ex[:, n % 2, :], ex[:, n % 2, :], 1.0, None, ALU.min).then_inc(qk_min, 1)
                        eng.wait_ge(qk_min, 2 * C * g + n + 1)
                        if not (isinstance(g, int) and g == 0):
                            if n == 0:
                                eng.wait_ge(qm_done, 4 * C * g)
                            if n == C:
                                eng.wait_ge(lin_s, NU * g)
                        eng.scalar_tensor_tensor((q if t == "q" else k)[:, c, :], pbank(kind, f"{t}{c}")[:, :],
                                                 (bq1 if t == "q" else bk1)[:, c:c + 1], ex[:, n % 2, :],
                                                 ALU.add, ALU.max).then_inc(qk_done, 1)

                def v_out(kind, g):
                    for n in range(2):
                        eng.wait_ge(v_psum, 2 * g + n + 1)
                        if n == 0:
                            if isinstance(g, int) and g == 0:
                                eng.wait_ge(const_ready, 5)
                            else:
                                eng.wait_ge(av_done, NU * g - NU // 2)
                        for b in range(2):
                            i_ = eng.tensor_tensor(
                                head_columns(v, 2 * n + b, 1),
                                pbank(kind, f"v{n}")[:, b * D:(b + 1) * D].rearrange("p (r z d) -> p r z d", z=2, d=HD),
                                bvb[:, :].rearrange("p (r z d) -> p r z d", z=2, d=HD), ALU.add)
                        i_.then_inc(v_done, 1)

                def masked(i, n):
                    eng.wait_ge(lin_s, NU * i + n + 1)
                    wait_att(eng, i, 0, n)
                    eng.tensor_tensor(att_slot(0, n), sbank("lin", n)[:, :].rearrange("p (j s) -> p j s", j=4),
                                      causal.rearrange("p (o s) -> p o s", o=1).broadcast_to([P, 4, S]), ALU.mult)\
                       .then_inc(lin_a, 1)

                def lin_out(i, b):
                    eng.wait_ge(den_done, GB * i + b + 1)
                    eng.reciprocal(rec[:, b % 2, :], den[:, b % 2, :]).then_inc(rec_done, 1)
                    eng.wait_ge(rec_done, GB * i + b + 1)
                    if not (isinstance(i, int) and i == 0 and b < 2):
                        eng.wait_ge(wo_psum, GB * i + b - 1)
                    eng.tensor_tensor(oT[:, b % 2, :, :], ob[b % 2][:, 0:2 * S].rearrange("p (c s) -> p c s", c=C),
                                      rec[:, b % 2, :].rearrange("p (c s) -> p c s", c=C), ALU.mult)\
                       .then_inc(lin_o, 1)

                def residual1(kind, i, b, count):
                    eng.wait_ge(wo_psum, GB * i + b + 1)
                    eng.wait_ge(xb_done, i + 1)
                    eng.tensor_tensor(x1[:, b, :], pbank(kind, f"wo{b}")[:, 0:D], xb[:, b, :], ALU.add)\
                       .then_inc(x1_done, 1)
                    eng.wait_ge(x1_done, GB * i + b + 1)
                    mean_var(LN2, 1, x1, i, b, count)

                def xq_out(kind, i):
                    for c in range(C):
                        eng.wait_ge(xq_psum, C * i + c + 1)
                        if c == 0 and not (isinstance(i, int) and i == 0):
                            eng.wait_ge(max_psum, NU * i)
                        eng.tensor_copy(xqr[:, c, :], pbank(kind, f"xq{c}")[:, :]).then_inc(xqr_done, 1)

                def xk_heads(i):
                    for c in range(C):
                        eng.wait_ge(xk_done, C * i + c + 1)
                        for j in range(4):
                            eng.tensor_scalar(xkm[:, c, j, :], xk[:, c, :], headmask[:, j:j + 1], None, ALU.mult)\
                               .then_inc(xkm_done, 1)

                def maximum(i, n):
                    b, c, row = unit(n)
                    h = 8 * c + 4 * (row // 64)
                    eng.wait_ge(max_psum, NU * i + n + 1)
                    eng.tensor_reduce(mx[:, b % 2, h:h + 4], sbank("max", n)[:, :].rearrange("p (j t) -> p j t", j=4),
                                      AX.X, ALU.max).then_inc(max_done, 1)

                def shift(i, b):
                    eng.wait_ge(max_done, NU * i + 4 * b + 4)
                    if not (isinstance(i, int) and i == 0 and b < 2):
                        eng.wait_ge(sh_psum, GB * i + b - 1)
                    eng.tensor_scalar(nshift[:, b % 2, 0, :], mx[:, b % 2, :], -1.0, None, ALU.mult).then_inc(sh_hi, 1)
                    eng.wait_ge(sh_hi, GB * i + b + 1)
                    eng.scalar_tensor_tensor(nshift[:, b % 2, 1, :], mx[:, b % 2, :], -1.0, nshift[:, b % 2, 0, :],
                                             ALU.mult, ALU.subtract).then_inc(sh_lo, 1)

                def x_out(i, b):
                    eng.wait_ge(av_done, NU * i + NU // 2 + 2 * b + 2)
                    eng.reciprocal(rec[:, b % 2, :], ob[b % 2][:, 2 * S:4 * S]).then_inc(x_rec, 1)
                    eng.wait_ge(x_rec, GB * i + b + 1)
                    if not (isinstance(i, int) and i == 0 and b < 2):
                        eng.wait_ge(ox_psum, GB * i + b - 1)
                    eng.tensor_tensor(oxT[:, b % 2, :, :], ob[b % 2][:, 0:2 * S].rearrange("p (c s) -> p c s", c=C),
                                      rec[:, b % 2, :].rearrange("p (c s) -> p c s", c=C), ALU.mult)\
                       .then_inc(x_o, 1)

                def residual2(kind, i, g, b, count):
                    eng.wait_ge(ox_psum, GB * g + b + 1)
                    if b == 0 and not (isinstance(g, int) and g == 0):
                        eng.wait_ge(x2T_psum, C * g)
                    eng.tensor_tensor(x2[:, b, :], pbank(kind, f"ox{b}")[:, 0:D], x1[:, b, :], ALU.add)\
                       .then_inc(x2_done, 1)
                    eng.wait_ge(x2_done, GB * g + b + 1)
                    mean_var(LN3, 2, x2, g, b, count)

                def low_bits_of(i):
                    eng.wait_ge(wbits_loaded, 64 * i + 64)
                    eng.tensor_scalar(wbits[:, :], wbits[:, :], 0xFFF, None, ALU.bitwise_and).then_inc(low_done, 1)
                    eng.wait_ge(low_done, i + 1)
                    out = low[:, i:i + 1] if isinstance(i, int) else low[:, bass.ds(i, 1)]
                    eng.tensor_reduce(out, wbits[:, :], AX.X, ALU.max).then_inc(wbits_read, 1)

                for b in range(GB):
                    ln1(0, b, 2 + b + 1)
                for b in range(GB):
                    normalise(LN1, 0, xn1, x_in, 0, b, C, LN1["turned"])
                qk_out("start", 0)
                v_out("start", 0)

                def body(kind, i):
                    done = [6 if kind == "first" else 6 + 12 * i - 1]

                    def count():
                        done[0] = done[0] + 1
                        return done[0]

                    for n in range(NU):
                        masked(i, n)
                        if kind != "first" and n == 2:
                            residual2(kind, i, i - 1, 3, count())
                        if kind != "first" and n == 4:
                            normalise(LN3, 2, xn3, x2, i - 1, 3, C, LN3["turned"])
                        if kind != "last" and n % 4 == 3:
                            ln1(i + 1, n // 4, count())
                        if kind != "last" and n % 4 == 1 and n > 4:
                            normalise(LN1, 0, xn1, x_in, i + 1, n // 4 - 1, C, LN1["turned"])
                        if n % 4 == 2 and n > 4:
                            lin_out(i, n // 4 - 1)
                        if n % 4 == 1 and n > 8:
                            residual1(kind, i, n // 4 - 2, count())
                        if n % 4 == 3 and n > 8:
                            normalise(LN2, 1, xn2, x1, i, n // 4 - 2, C, LN2["turned"])
                    if kind != "last":
                        normalise(LN1, 0, xn1, x_in, i + 1, 3, C, LN1["turned"])
                    lin_out(i, 3)
                    residual1(kind, i, 2, count())
                    residual1(kind, i, 3, count())
                    normalise(LN2, 1, xn2, x1, i, 2, C, LN2["turned"])
                    normalise(LN2, 1, xn2, x1, i, 3, C, LN2["turned"])
                    if kind != "last":
                        qk_out(kind, i + 1)
                        v_out(kind, i + 1)
                    low_bits_of(i)
                    xq_out(kind, i)
                    xk_heads(i)
                    for n in range(8):
                        maximum(i, n)
                        if n % 4 == 3:
                            shift(i, n // 4)
                    for n in range(NU):
                        if n + 8 < NU:
                            maximum(i, n + 8)
                            if n % 4 == 3:
                                shift(i, n // 4 + 2)
                        if n % 4 == 1 and n > 4:
                            x_out(i, n // 4 - 1)
                        if n % 4 == 3 and n > 4:
                            residual2(kind, i, i, n // 4 - 1, count())
                        if n % 4 == 1 and n > 8:
                            normalise(LN3, 2, xn3, x2, i, n // 4 - 2, C, LN3["turned"])
                    x_out(i, 3)
                    normalise(LN3, 2, xn3, x2, i, 2, C, LN3["turned"])

                each_group(eng, body)
                residual2("end", G, G - 1, 3, 2 + 12 * G)
                normalise(LN3, 2, xn3, x2, G - 1, 3, C, LN3["turned"])

                eng.wait_ge(wbits_read, G)
                eng.tensor_reduce(low[:, G:G + 1], low[:, 0:G], AX.X, ALU.max).then_inc(low_done, 1)
                eng.wait_ge(low_psum, 1)
                eng.tensor_scalar(flag[:, :], sbk[0][0:1, 0:1], 1.0, None, ALU.min).then_inc(flag_ready, 1)

            @block.tensor
            def _(eng):
                eng.wait_ge(weights, NW)
                eng.wait_ge(act_const, 3)
                eng.wait_ge(const_ready, 5)

                def turn(kind, i, g, src, name, ready, done):
                    eng.wait_ge(ready, GB * g + GB)
                    for c in range(C):
                        wait_pbank(eng, kind, i, f"{name}{c}")
                        for b in range(GB):
                            mm = eng.transpose(pbank(kind, f"{name}{c}")[:, b * S:(b + 1) * S],
                                               src[:, b, c * P:(c + 1) * P], ident)
                        mm.then_inc(done, 1)

                def project(kind, i, name, w, src, done):
                    for m in range(C):
                        wait_pbank(eng, kind, i, f"{name}{m}")
                        for c in range(C):
                            mm = eng.matmul(pbank(kind, f"{name}{m}")[:, :], w[:, c, m * P:(m + 1) * P], src[:, c, :],
                                            start=(c == 0), stop=(c == C - 1))
                        mm.then_inc(done, 1)

                def values(kind, i, name, w, src, done):
                    for n in range(2):
                        wait_pbank(eng, kind, i, f"{name}{n}")
                        for b in (2 * n, 2 * n + 1):
                            for c in range(C):
                                mm = eng.matmul(pbank(kind, f"{name}{n}")[:, b % 2 * D:b % 2 * D + D],
                                                src[:, c, b * S:(b + 1) * S], w[:, c, :],
                                                start=(c == 0), stop=(c == C - 1))
                        mm.then_inc(done, 1)

                def lin_scores(i, n):
                    b, c, row = unit(n)
                    if n == 0:
                        eng.wait_ge(qm_done, 4 * C * i + 4 * C)
                        eng.wait_ge(qk_done, 2 * C * i + 2 * C)
                    wait_sbank(eng, i, "lin", n)
                    eng.matmul(sbank("lin", n)[:, :].rearrange("p (j s) -> p j s", j=4),
                               k[row:row + 64, c, b * S:(b + 1) * S], qm[row:row + 64, c, :, b * S:(b + 1) * S],
                               start=True, stop=True).then_inc(lin_s, 1)

                def outputs(i, part, m, vt, ready):
                    b, c = m // 2, m % 2
                    eng.wait_ge(ready, NU * i + 2 * m + 2)
                    if c == 0:
                        wait_obank(eng, i, part, b)
                    o_ = ob[b % 2]
                    for at, num in ((c * S, True), ((C + c) * S, False)):
                        for z in range(2):
                            for r in range(4):
                                u = 2 * m + r // 2
                                w = vt[:, b, 4 * c + r, 32 * z:32 * z + 32] if num else onepad[:, 32 * z:32 * z + 32]
                                mm = eng.matmul(o_[32 * r:32 * r + 32, at:at + S], w,
                                                att_slot(part, u)[:, 2 * (r % 2) + z, :], start=(z == 0), stop=(z == 1),
                                                tile_position=(0, 32 * r))
                    mm.then_inc(av_done, 1)

                def out_project(kind, i, b):
                    eng.wait_ge(lin_o, GB * i + b + 1)
                    wait_pbank(eng, kind, i, f"wo{b}")
                    for c in range(C):
                        mm = eng.matmul(pbank(kind, f"wo{b}")[:, 0:D], oT[:, b % 2, c, :], wo[:, c, :],
                                        start=(c == 0), stop=(c == C - 1))
                    mm.then_inc(wo_psum, 1)

                def max_scores(i, n):
                    b, c, row = unit(n)
                    if n == 0:
                        eng.wait_ge(xqr_done, C * i + C)
                        eng.wait_ge(xkm_done, 4 * C * i + 4 * C)
                    wait_sbank(eng, i, "max", n)
                    eng.matmul(sbank("max", n)[:, :].rearrange("p (j t) -> p j t", j=4),
                               xqr[row:row + 64, c, b * S:(b + 1) * S], xkm[row:row + 64, c, :, b * S:(b + 1) * S],
                               start=True, stop=True).then_inc(max_psum, 1)

                def turn_shift(kind, i, b):
                    eng.wait_ge(sh_lo, GB * i + b + 1)
                    wait_pbank(eng, kind, i, f"sh{b}")
                    eng.transpose(pbank(kind, f"sh{b}")[0:32, 0:S // 2].bitcast(BF16),
                                  nshift[:, b % 2, :, :].rearrange("p a h -> p (a h)"), identb[:, :]).then_inc(sh_psum, 1)

                def x_scores(i, n):
                    b, c, row = unit(n)
                    if n == 0:
                        eng.wait_ge(xqm_done, 4 * C * i + 4 * C)
                    if n % 4 == 0:
                        eng.wait_ge(sh_done, GB * i + b + 1)
                    wait_sbank(eng, i, "exp", n)
                    s_ = sbank("exp", n)
                    eng.matmul(s_[:, :].rearrange("p (j s) -> p j s", j=4),
                               xk[row:row + 64, c, b * S:(b + 1) * S], xqm[row:row + 64, c, :, b * S:(b + 1) * S],
                               start=True, stop=False)
                    for j in range(4):
                        mm = eng.matmul(s_[:, j * S:(j + 1) * S], sel[:, 8 * c + row // 16 + j, :], shiftT[:, b % 2, :],
                                        start=False, stop=(j == 3))
                    mm.then_inc(x_s, 1)

                def turn_output(kind, i, g, b):
                    eng.wait_ge(x_o, GB * g + b + 1)
                    wait_pbank(eng, kind, i, f"ox{b}")
                    for c in range(C):
                        mm = eng.transpose(pbank(kind, f"ox{b}")[:, c * P:(c + 1) * P], oxT[:, b % 2, c, :], ident)
                    mm.then_inc(ox_psum, 1)

                def qkv(kind, i, g):
                    eng.wait_ge(LN1["xnT"], C * g + C)
                    project(kind, i, "q", wq, xn1T, qk_psum)
                    project(kind, i, "k", wk, xn1T, qk_psum)
                    values(kind, i, "v", wv, xn1T, v_psum)

                turn("start", 0, 0, xn1, "ln1T", LN1["xn"], LN1["turned"])
                qkv("start", 0, 0)

                def body(kind, i):
                    for n in range(NU + 2):
                        if n < NU:
                            lin_scores(i, n)
                        if n == 0:
                            eng.wait_ge(v_done, 2 * i + 2)
                        if n % 2 == 1 and n > 2:
                            outputs(i, 0, (n - 3) // 2, v, lin_a)
                        if kind != "first" and n == 1:
                            turn_output(kind, i, i - 1, 3)
                        if kind != "first" and n == 6:
                            turn(kind, i, i - 1, x2, "x2T", x2_done, x2T_psum)
                            turn(kind, i, i - 1, xn3, "xn3T", LN3["xn"], LN3["turned"])
                        if n % 4 == 0 and n > 4:
                            out_project(kind, i, n // 4 - 2)
                    if kind != "last":
                        turn(kind, i, i + 1, xn1, "ln1T", LN1["xn"], LN1["turned"])
                    out_project(kind, i, 3)
                    if kind != "last":
                        qkv(kind, i, i + 1)
                    turn(kind, i, i, xn2, "ln2T", LN2["xn"], LN2["turned"])
                    eng.wait_ge(LN2["xnT"], C * i + C)
                    project(kind, i, "xq", xwq, xn2T, xq_psum)
                    eng.wait_ge(ctx_loaded, 16 * i + 16)
                    project(kind, i, "xk", xwk, ctxs, xk_psum)
                    values(kind, i, "xv", xwv, ctxs, xv_psum)
                    for n in range(8):
                        max_scores(i, n)
                    turn_shift(kind, i, 0)
                    eng.wait_ge(xv_done, 2 * i + 2)
                    for n in range(NU):
                        x_scores(i, n)
                        if n + 8 < NU:
                            max_scores(i, n + 8)
                        if n % 2 == 1 and n > 2:
                            outputs(i, 1, (n - 3) // 2, xv, x_e)
                        if n % 4 == 3 and n < NU - 1:
                            turn_shift(kind, i, n // 4 + 1)
                        if n % 4 == 3 and n > 4:
                            turn_output(kind, i, i, n // 4 - 1)
                    outputs(i, 1, NU // 2 - 1, xv, x_e)

                each_group(eng, body)
                turn_output("end", G, G - 1, 3)
                turn("end", G, G - 1, x2, "x2T", x2_done, x2T_psum)
                turn("end", G, G - 1, xn3, "xn3T", LN3["xn"], LN3["turned"])
                eng.wait_ge(low_done, G + 1)
                eng.matmul(sbk[0][0:1, 0:1], low[:, G:G + 1], causal[:, P - 1:P], start=True, stop=True).then_inc(low_psum, 1)

        ctx = ExitStack()
        with ctx:
            base = (nc.sbuf_base + 31) // 32 * 32

            def sb(name, shape, dt=F32):
                return ctx.enter_context(nc.sbuf_tensor(name, shape, dt))

            FA = nc.alloc_sbuf_tensor_at("general_hidden_a", [P, KH, T], F32, offset=base)
            FB = nc.alloc_sbuf_tensor_at("general_hidden_b", [P, KH, T], F32, offset=base + KH * T * 4)
            FW = nc.alloc_sbuf_tensor_at("general_weights", [P, 2, KH, P], F32, offset=base + 2 * KH * T * 4)
            w12r = sb("w12_r", [P, KH, 2, C, P], F32R)
            h1r = sb("h1_r", [P, KH, KH, P], F32R)
            h2r = sb("h2_r", [P, KH, KH, P], F32R)
            w3r = sb("w3_r", [P, C, KH, P], F32R)
            HA = sb("hidden_a", [P, 2, KH, T], F32R)
            HB = sb("hidden_b", [P, 2, KH, T], F32R)
            xin = sb("ffn_in", [P, C, T])
            xhl = sb("ffn_in_parts", [P, 2, C, T], F32R)
            res = sb("ffn_residual", [P, C, T])
            gate = sb("gate", [P, T])
            full = sb("hidden_full", [P, 2, T])
            s1c, s2c, sh1c, sh2c = (sb(n, [P, KH]) for n in ("s1c", "s2c", "sh1c", "sh2c"))
            s3c, s1h, s12 = sb("s3c", [P, C]), sb("s1h", [P, KH]), sb("s12", [P, KH])

            bank = [ctx.enter_context(nc.psum_tensor(f"ffn_bank{n}", [P, T], F32)) for n in range(8)]
            scales, s1h_done, s12_done = sem("scales_loaded"), sem("s1h_done"), sem("s12_done")
            w_loaded = {n: sem(f"{n}_loaded") for n in ("w12a", "w12b", "h1a", "h1b", "h2", "w3")}
            in_loaded, res_loaded = sem("ffn_in_loaded"), sem("residual_loaded")
            hi_done, in_done = sem("in_hi"), sem("in_parts")
            gate_psum, gate_act, gate_mul, gate_full = (sem(n) for n in ("gate_psum", "gate_act", "gate_mul", "gate_full"))
            gate_hi, gate_lo = sem("gate_hi"), sem("gate_lo")
            h_psum, h_full, h_hi, h_lo = sem("h_psum"), sem("h_full"), sem("h_hi"), sem("h_lo")
            o_psum, o_done, o_stored = sem("o_psum"), sem("o_done"), sem("o_stored")
            g_loaded = [sem(f"general_weights_loaded{n}") for n in range(2)]
            out_t = sb("out_tile", [P, C, T])

            def some(n):
                return not isinstance(n, int) or n > 0

            def exact_gpsimd(eng):
                half = KH // 2
                for dst, src, s in ((w12r[:, 0:half], w12[:, 0:half], "w12a"), (w12r[:, half:KH], w12[:, half:KH], "w12b"),
                                    (h1r[:, 0:half], h1[:, 0:half], "h1a"), (h1r[:, half:KH], h1[:, half:KH], "h1b"),
                                    (h2r[:, :], h2[:, :], "h2"), (w3r[:, :], w3[:, :], "w3")):
                    eng.dma_start(dst, src).then_inc(w_loaded[s], 16)

            def exact_sync(eng):
                eng.dma_start(xin[:, :, :], tokens(xnT_d, 0)).then_inc(in_loaded, 16)
                eng.dma_start(res[:, :, :], tokens(x2T_d, 0)).then_inc(res_loaded, 16)
                with nc.allow_non_contiguous_dma(reason="scales, once"):
                    for dst, src in ((s1c, s1), (s2c, s2), (sh1c, sh1), (sh2c, sh2), (s3c, s3)):
                        eng.dma_start(dst[:, :], src.rearrange("(c p) -> p c", p=P)).then_inc(scales, 16)

                def store(i):
                    eng.wait_ge(o_done, C * i + C)
                    eng.dma_start(tokens(outT, i), out_t[:, :, :]).then_inc(o_stored, 16)

                with eng.Fori(1, G) as i:
                    eng.wait_ge(in_done, i)
                    eng.dma_start(xin[:, :, :], tokens(xnT_d, i)).then_inc(in_loaded, 16)
                    store(i - 1)
                    eng.dma_start(res[:, :, :], tokens(x2T_d, i)).then_inc(res_loaded, 16)
                store(G - 1)
                eng.wait_ge(o_stored, 16 * G)

            def exact_scalar(eng):
                eng.wait_ge(scales, 16 * 5)
                eng.preload_act_table(ACT.Gelu)
                eng.activation(s1h[:, :], s1c[:, :], ACT.Copy, scale=0.5).then_inc(s1h_done, 1)
                eng.wait_ge(s1h_done, 1)

                def split_in(i):
                    eng.wait_ge(in_loaded, 16 * i + 16)
                    if some(i):
                        eng.wait_ge(gate_psum, KH * i)
                    eng.activation(xhl[:, 0, :, :], xin[:, :, :], ACT.Copy).then_inc(hi_done, 1)

                def gates(i, m):
                    eng.wait_ge(gate_psum, KH * i + m + 1)
                    if some(KH * i + m):
                        eng.wait_ge(gate_mul, KH * i + m)
                    eng.activation(gate[:, :], bank[2 * m % 4][:, :], ACT.Tanh, scale=s1h[:, m:m + 1])\
                       .then_inc(gate_act, 1)

                def gate_round(i, m):
                    eng.wait_ge(gate_full, KH * i + m + 1)
                    if m == 0 and some(i):
                        eng.wait_ge(o_psum, C * i)
                    eng.activation(HA[:, 0, m, :], full[:, m % 2, :], ACT.Copy).then_inc(gate_hi, 1)

                def hidden(i, n):
                    m, layer = n % KH, n // KH
                    src, dst, sc = bank[4 + n % 4], (HB, HA)[layer], (sh1c, sh2c)[layer][:, m:m + 1]
                    eng.wait_ge(h_psum, 2 * KH * i + n + 1)
                    if n >= 2:
                        eng.wait_ge(h_lo, 2 * KH * i + n - 1)
                    else:
                        eng.wait_ge(gate_lo, KH * i + KH - 1 + n)
                    eng.activation(full[:, n % 2, :], src[:, :], ACT.Gelu, scale=sc).then_inc(h_full, 1)
                    if n == 0 and some(i):
                        eng.wait_ge(h_psum, 2 * KH * i)
                    eng.activation(dst[:, 0, m, :], src[:, :], ACT.Gelu, scale=sc).then_inc(h_hi, 1)

                split_in(0)

                def body(i, last=False):
                    for m in range(KH):
                        gates(i, m)
                        if m >= 1:
                            gate_round(i, m - 1)
                    gate_round(i, KH - 1)
                    for n in range(2 * KH):
                        hidden(i, n)
                        if n == 2 and not last:
                            split_in(i + 1)

                body(0)
                with eng.Fori(1, G - 1) as i:
                    body(i)
                body(G - 1, last=True)

            def exact_vector(eng):
                eng.wait_ge(scales, 16 * 5)
                eng.scalar_tensor_tensor(s12[:, :], s1c[:, :], 0.5, s2c[:, :], ALU.mult, ALU.mult).then_inc(s12_done, 1)
                eng.wait_ge(s12_done, 1)

                def rest_in(i):
                    eng.wait_ge(hi_done, i + 1)
                    eng.tensor_tensor(xhl[:, 1, :, :], xin[:, :, :], xhl[:, 0, :, :].bitcast(F32), ALU.subtract)\
                       .then_inc(in_done, 1)

                def gated(i, m):
                    eng.wait_ge(gate_act, KH * i + m + 1)
                    f = full[:, m % 2, :]
                    if m < 2:
                        if some(i):
                            eng.wait_ge(h_lo, 2 * KH * i)
                    else:
                        eng.wait_ge(gate_lo, KH * i + m - 1)
                    eng.scalar_tensor_tensor(f, gate[:, :], 1.0, bank[2 * m % 4][:, :], ALU.add, ALU.mult)\
                       .then_inc(gate_mul, 1)
                    eng.wait_ge(gate_mul, KH * i + m + 1)
                    eng.scalar_tensor_tensor(f, bank[2 * m % 4 + 1][:, :], s12[:, m:m + 1], f, ALU.mult, ALU.mult)\
                       .then_inc(gate_full, 1)

                def gate_rest(i, m):
                    eng.wait_ge(gate_hi, KH * i + m + 1)
                    eng.tensor_tensor(HA[:, 1, m, :], full[:, m % 2, :], HA[:, 0, m, :].bitcast(F32), ALU.subtract)\
                       .then_inc(gate_lo, 1)

                def hidden_rest(i, n):
                    m, dst = n % KH, (HB, HA)[n // KH]
                    eng.wait_ge(h_hi, 2 * KH * i + n + 1)
                    eng.tensor_tensor(dst[:, 1, m, :], full[:, n % 2, :], dst[:, 0, m, :].bitcast(F32), ALU.subtract)\
                       .then_inc(h_lo, 1)

                def output(i, c):
                    eng.wait_ge(o_psum, C * i + c + 1)
                    eng.wait_ge(res_loaded, 16 * i + 16)
                    if c == 0 and some(i):
                        eng.wait_ge(o_stored, 16 * i)
                    eng.scalar_tensor_tensor(out_t[:, c, :], bank[c][:, :], s3c[:, c:c + 1], res[:, c, :],
                                             ALU.mult, ALU.add).then_inc(o_done, 1)

                rest_in(0)

                def body(i, last=False):
                    for m in range(KH):
                        gated(i, m)
                        if m >= 1:
                            gate_rest(i, m - 1)
                    gate_rest(i, KH - 1)
                    for n in range(2 * KH):
                        hidden_rest(i, n)
                        if n == 2 and not last:
                            rest_in(i + 1)
                    for c in range(C):
                        output(i, c)

                body(0)
                with eng.Fori(1, G - 1) as i:
                    body(i)
                body(G - 1, last=True)

            def exact_tensor(eng):
                def products(out, w, src, n):
                    for kk in range(n):
                        for part in range(2):
                            mm = eng.matmul(out[:, :], w(kk), src[:, part, kk, :],
                                            start=(kk == 0 and part == 0), stop=(kk == n - 1 and part == 1))
                    return mm

                def body(i):
                    eng.wait_ge(in_done, i + 1)
                    for m in range(KH):
                        if m == 0:
                            eng.wait_ge(w_loaded["w12a"], 16)
                            if some(i):
                                eng.wait_ge(o_done, C * i)
                        if m == KH // 2:
                            eng.wait_ge(w_loaded["w12b"], 16)
                        if m >= 2:
                            eng.wait_ge(gate_full, KH * i + m - 1)
                        for z in range(2):
                            mm = products(bank[2 * m % 4 + z], lambda kk: w12r[:, m, z, kk, :], xhl, C)
                        mm.then_inc(gate_psum, 1)
                    for n in range(2 * KH):
                        m, w, src = n % KH, (h1r, h2r)[n // KH], (HA, HB)[n // KH]
                        if n == 0:
                            eng.wait_ge(w_loaded["h1a"], 16)
                        if n == KH // 2:
                            eng.wait_ge(w_loaded["h1b"], 16)
                        if n == KH:
                            eng.wait_ge(w_loaded["h2"], 16)
                        if some(2 * KH * i + n - 3):
                            eng.wait_ge(h_hi, 2 * KH * i + n - 3)
                        for kk in range(KH):
                            if m == 0:
                                if n == 0:
                                    eng.wait_ge(gate_lo, KH * i + kk + 1)
                                else:
                                    eng.wait_ge(h_lo, 2 * KH * i + kk + 1)
                            for part in range(2):
                                mm = eng.matmul(bank[4 + n % 4][:, :], w[:, m, kk, :], src[:, part, kk, :],
                                                start=(kk == 0 and part == 0), stop=(kk == KH - 1 and part == 1))
                        mm.then_inc(h_psum, 1)
                    eng.wait_ge(w_loaded["w3"], 16)
                    eng.wait_ge(gate_full, KH * i + KH - 1)
                    for c in range(C):
                        for kk in range(KH):
                            if c == 0:
                                eng.wait_ge(h_lo, 2 * KH * i + KH + kk + 1)
                            for part in range(2):
                                mm = eng.matmul(bank[c][:, :], w3r[:, c, kk, :], HA[:, part, kk, :],
                                                start=(kk == 0 and part == 0), stop=(kk == KH - 1 and part == 1))
                        mm.then_inc(o_psum, 1)

                body(0)
                with eng.Fori(1, G) as i:
                    body(i)

            NT = KH + 2 * KH + C

            def general_sync(eng):
                def body(i):
                    if some(i):
                        eng.wait_ge(o_done, C * i)
                    eng.dma_start(xin[:, :, :], tokens(xnT_d, i)).then_inc(in_loaded, 16)
                    eng.dma_start(res[:, :, :], tokens(x2T_d, i)).then_inc(res_loaded, 16)
                    for j in range(NT):
                        used = j - 2
                        if 0 <= used < KH:
                            eng.wait_ge(gate_psum, KH * i + used + 1)
                        elif KH <= used < 3 * KH:
                            eng.wait_ge(h_psum, 2 * KH * i + used - KH + 1)
                        if j < KH:
                            src = w12[:, j].rearrange("p z k o -> p (z k) o")
                        elif j < 2 * KH:
                            src = h1[:, j - KH]
                        elif j < 3 * KH:
                            src = h2[:, j - 2 * KH]
                        else:
                            src = w3[:, j - 3 * KH]
                        eng.dma_start(FW[:, j % 2, 0:src.shape[1], :], src).then_inc(g_loaded[j % 2], 16)
                    eng.wait_ge(o_done, C * i + C)
                    eng.dma_start(tokens(outT, i), out_t[:, :, :]).then_inc(o_stored, 16)

                with nc.allow_non_contiguous_dma(reason="scales, once"):
                    for dst, src in ((s1c, s1), (s2c, s2), (sh1c, sh1), (sh2c, sh2), (s3c, s3)):
                        eng.dma_start(dst[:, :], src.rearrange("(c p) -> p c", p=P)).then_inc(scales, 16)
                body(0)
                with eng.Fori(1, G) as i:
                    body(i)
                eng.wait_ge(o_stored, 16 * G)

            def general_scalar(eng):
                eng.wait_ge(scales, 16 * 5)
                eng.activation(s1h[:, :], s1c[:, :], ACT.Copy, scale=0.5).then_inc(s1h_done, 1)
                eng.wait_ge(s1h_done, 1)

                def body(i):
                    for m in range(KH):
                        eng.wait_ge(gate_psum, KH * i + m + 1)
                        if some(KH * i + m):
                            eng.wait_ge(gate_mul, KH * i + m)
                        eng.activation(gate[:, :], bank[2 * m % 4][:, :], ACT.Tanh, scale=s1h[:, m:m + 1])\
                           .then_inc(gate_act, 1)
                    for n in range(2 * KH):
                        m, dst, sc = n % KH, (FB, FA)[n // KH], (sh1c, sh2c)[n // KH]
                        eng.wait_ge(h_psum, 2 * KH * i + n + 1)
                        eng.activation(dst[:, m, :], bank[4 + n % 4][:, :], ACT.Gelu, scale=sc[:, m:m + 1])\
                           .then_inc(h_full, 1)

                body(0)
                with eng.Fori(1, G) as i:
                    body(i)

            def general_vector(eng):
                eng.wait_ge(scales, 16 * 5)
                eng.scalar_tensor_tensor(s12[:, :], s1c[:, :], 0.5, s2c[:, :], ALU.mult, ALU.mult).then_inc(s12_done, 1)
                eng.wait_ge(s12_done, 1)

                def body(i):
                    for m in range(KH):
                        eng.wait_ge(gate_act, KH * i + m + 1)
                        eng.scalar_tensor_tensor(FA[:, m, :], gate[:, :], 1.0, bank[2 * m % 4][:, :], ALU.add, ALU.mult)\
                           .then_inc(gate_mul, 1)
                        eng.wait_ge(gate_mul, KH * i + m + 1)
                        eng.scalar_tensor_tensor(FA[:, m, :], bank[2 * m % 4 + 1][:, :], s12[:, m:m + 1], FA[:, m, :],
                                                 ALU.mult, ALU.mult).then_inc(gate_full, 1)
                    eng.wait_ge(res_loaded, 16 * i + 16)
                    if some(i):
                        eng.wait_ge(o_stored, 16 * i)
                    for c in range(C):
                        eng.wait_ge(o_psum, C * i + c + 1)
                        eng.scalar_tensor_tensor(out_t[:, c, :], bank[c][:, :], s3c[:, c:c + 1], res[:, c, :],
                                                 ALU.mult, ALU.add).then_inc(o_done, 1)

                body(0)
                with eng.Fori(1, G) as i:
                    body(i)

            def general_tensor(eng):
                def body(i):
                    eng.wait_ge(in_loaded, 16 * i + 16)
                    for j in range(NT):
                        eng.wait_ge(g_loaded[j % 2], 16 * (NT // 2 * i + j // 2) + 16)
                        if j < KH:
                            if j == 0 and some(i):
                                eng.wait_ge(o_done, C * i)
                            if j >= 2:
                                eng.wait_ge(gate_full, KH * i + j - 1)
                            for z in range(2):
                                for kk in range(C):
                                    mm = eng.matmul(bank[2 * j % 4 + z][:, :], FW[:, j % 2, C * z + kk, :], xin[:, kk, :],
                                                    start=(kk == 0), stop=(kk == C - 1))
                            mm.then_inc(gate_psum, 1)
                        elif j < 3 * KH:
                            n = j - KH
                            if n == 0:
                                eng.wait_ge(gate_full, KH * i + KH)
                            if n == KH:
                                eng.wait_ge(h_full, 2 * KH * i + KH)
                            if some(2 * KH * i + n - 3):
                                eng.wait_ge(h_full, 2 * KH * i + n - 3)
                            for kk in range(KH):
                                mm = eng.matmul(bank[4 + n % 4][:, :], FW[:, j % 2, kk, :], (FA, FB)[n // KH][:, kk, :],
                                                start=(kk == 0), stop=(kk == KH - 1))
                            mm.then_inc(h_psum, 1)
                        else:
                            c = j - 3 * KH
                            if c == 0:
                                eng.wait_ge(h_full, 2 * KH * i + 2 * KH)
                            for kk in range(KH):
                                mm = eng.matmul(bank[c][:, :], FW[:, j % 2, kk, :], FA[:, kk, :],
                                                start=(kk == 0), stop=(kk == KH - 1))
                            mm.then_inc(o_psum, 1)

                body(0)
                with eng.Fori(1, G) as i:
                    body(i)

            block = ctx.enter_context(nc.Block())

            def inexact(eng):
                eng.wait_ge(flag_ready, 1)
                return eng.value_load(flag[0:1, 0:1], min_val=0, max_val=1) != 0

            @block.gpsimd
            def _(eng):
                with eng.If(inexact(eng)):
                    pass
                with eng.Else():
                    exact_gpsimd(eng)

            @block.sync
            def _(eng):
                with eng.If(inexact(eng)):
                    general_sync(eng)
                with eng.Else():
                    exact_sync(eng)

            @block.scalar
            def _(eng):
                with eng.If(inexact(eng)):
                    general_scalar(eng)
                with eng.Else():
                    exact_scalar(eng)

            @block.vector
            def _(eng):
                with eng.If(inexact(eng)):
                    general_vector(eng)
                with eng.Else():
                    exact_vector(eng)

            @block.tensor
            def _(eng):
                with eng.If(inexact(eng)):
                    general_tensor(eng)
                with eng.Else():
                    exact_tensor(eng)


_INS = ["x", "ctxT", "wqT", "wkT", "wvT", "woT", "bq", "bk", "bv", "bo", "xqT", "xkT", "xvT",
        "w12", "h1", "h2", "w3", "s1", "s2", "sh1", "sh2", "s3", "consts"]


def constants():
    import numpy as np
    c = np.zeros((128, 340), np.float32)
    c[:, 0:128] = np.eye(128)
    c[:, 128:256] = np.triu(np.ones((128, 128)))
    c[:, 256:272] = 1.0
    c[:, 304:320] = 1.0
    for j in range(4):
        c[:, 320 + j] = np.arange(128) // 16 % 4 == j
    for h in range(16):
        c[[h, 16 + h], 324 + h] = 1.0
    return c


def kernel(**inputs):
    import numpy as np
    import concourse.bacc as bacc
    from concourse.bass_utils import run_bass_kernel_spmd

    a = {n: np.asarray(v) for n, v in inputs.items()}
    B, S, D = a["x"].shape

    def turned(w):
        return np.ascontiguousarray(np.transpose(w))

    def by_tile(w, columns):
        o, i = w.shape
        return np.ascontiguousarray(np.transpose(w.reshape(o // columns, columns, i // 128, 128), (3, 0, 2, 1)))

    w1, w2 = by_tile(a["L0_ffn_w1_w"], 128), by_tile(a["L0_ffn_w2_w"], 128)
    arrays = {
        "x": np.ascontiguousarray(a["x"]),
        "ctxT": turned(a["ctx_1024"].reshape(B * S, D)),
        "wqT": turned(a["L0_attn_Wq"]), "wkT": turned(a["L0_attn_Wk"]),
        "wvT": turned(a["L0_attn_Wv"]), "woT": turned(a["L0_attn_Wo"]),
        "bq": a["L0_attn_bq"], "bk": a["L0_attn_bk"], "bv": a["L0_attn_bv"], "bo": a["L0_attn_bo"],
        "xqT": turned(a["L0_xattn_Wq"]), "xkT": turned(a["L0_xattn_Wk"]), "xvT": turned(a["L0_xattn_Wv"]),
        "w12": np.ascontiguousarray(np.stack([w1, w2], axis=2)),
        "h1": by_tile(a["L0_ffn_h1_w"], 128), "h2": by_tile(a["L0_ffn_h2_w"], 128),
        "w3": by_tile(a["L0_ffn_w3_w"], 128),
        "s1": a["L0_ffn_w1_s"], "s2": a["L0_ffn_w2_s"],
        "sh1": a["L0_ffn_h1_s"], "sh2": a["L0_ffn_h2_s"], "s3": a["L0_ffn_w3_s"],
        "consts": constants(),
    }
    nc = bacc.Bacc("TRN2", target_bir_lowering=False, num_devices=1)
    args = [nc.dram_tensor(f"in_{n}", arrays[n].shape, mybir.dt.from_np(arrays[n].dtype), kind="ExternalInput").ap()
            for n in _INS]
    out = nc.dram_tensor("out_T", (D, B * S), mybir.dt.float32, kind="ExternalOutput").ap()
    decoder_layer_program(nc, *args, out)
    r = run_bass_kernel_spmd(nc, [{f"in_{n}": arrays[n] for n in _INS}], core_ids=[0])
    return np.ascontiguousarray(np.transpose(r.results[0]["out_T"])).reshape(B, S, D)
```

```python
import concourse.bass as bass
from concourse import mybir
from contextlib import ExitStack


def decoder_layer_program(nc, x, ctxT, wqT, wkT, wvT, woT, bq, bk, bv, bo, xqT, xkT, xvT,
                          w12, h1, h2, w3, s1, s2, sh1, sh2, s3, consts, outT):
    F32, F32R, BF16, I32 = mybir.dt.float32, mybir.dt.float32r, mybir.dt.bfloat16, mybir.dt.int32
    ALU, ACT, AX = mybir.AluOpType, mybir.ActivationFunctionType, mybir.AxisListType

    P = 128
    B, S, D = x.shape
    H, HD = 16, 16
    HID = s1.shape[0]
    C = D // P
    GB = 4
    T = GB * S
    G = B // GB
    KH = HID // P
    LN_EPS, ATT_EPS, SCALE = 1e-5, 1e-6, HD ** -0.5
    NU = 4 * GB

    x2T_d = nc.dram_tensor("x2T_scratch", [D, B * S], F32, kind="Internal").ap()
    xnT_d = nc.dram_tensor("xn3T_scratch", [D, B * S], F32, kind="Internal").ap()

    parts_d = nc.dram_tensor("parts_scratch", [4, 3, D, T], BF16, kind="Internal").ap()

    def tokens(ap, g):
        v = ap.rearrange("(c p) t -> p c t", p=P)
        if isinstance(g, int):
            return v[:, :, g * T:(g + 1) * T]
        return v[:, :, bass.ds(g * T, T)]

    outer = ExitStack()

    def sem(name):
        return outer.enter_context(nc.semaphore(name))

    with outer:
        flag = outer.enter_context(nc.sbuf_tensor("inexact_flag", [1, 1], I32))
        flag_ready = sem("flag_ready")
        stored = sem("scratch_stored")

        ctx = ExitStack()
        with ctx:
            def sb(name, shape, dt=F32):
                return ctx.enter_context(nc.sbuf_tensor(name, shape, dt))

            wq, wk, wv, wo = (sb(n, [P, C, D]) for n in ("wq", "wk", "wv", "wo"))
            xwq, xwk, xwv = (sb(n, [P, C, D]) for n in ("xwq", "xwk", "xwv"))
            NC_ = consts.shape[1]
            cst = sb("cst", [P, NC_])
            ident = cst[:, 0:128]
            causal = cst[:, 128:256]
            bqc, bkc, bq1, bk1 = (sb(n, [P, C]) for n in ("bqc", "bkc", "bq1", "bk1"))
            bvb, bob = sb("bvb", [P, D]), sb("bob", [P, D])
            identb = sb("identb", [P, P], BF16)
            unused = sb("unused", [P, 1])
            mhalf, eps = sb("mhalf", [P, 1]), sb("eps", [P, 1])

            x_in = sb("x_in", [P, GB, D])
            xn1 = sb("xn1", [P, GB, D])
            xn1T = sb("xn1T", [P, C, T])
            xb = sb("xb", [P, GB, D])
            x1 = sb("x1", [P, GB, D])
            xn2 = sb("xn2", [P, GB, D])
            xn2T = sb("xn2T", [P, C, T])
            x2 = sb("x2", [P, GB, D])
            xn3 = sb("xn3", [P, GB, D])
            x2T = sb("x2T", [P, C, T])
            xn3T = sb("xn3T", [P, C, T])
            ctxs = sb("ctxs", [P, C, T])
            stats = sb("stats", [P, 3, GB, 6])
            mv = sb("mv", [P, 3, GB, 2])
            ve = sb("ve", [P, 3, GB])
            rstd = sb("rstd", [P, 3, GB])

            ex = sb("ex", [P, 2, T])
            qf = sb("qf", [P, C, T])
            kf = sb("kf", [P, C, T])
            qp = sb("qp", [P, 3, C, T], BF16)
            kp = sb("kp", [P, 3, C, T], BF16)
            Q_PARTS, K_PARTS = (0, 1, 2, 0, 1, 0), (0, 0, 0, 1, 1, 2)
            KR = HD * len(Q_PARTS)
            qs, ks = sb("qs", [KR, H, T], BF16), sb("ks", [KR, H, T], BF16)
            xqs, xks = sb("xqs", [KR + 2, H, T], BF16), sb("xks", [KR + 2, H, T], BF16)
            v = sb("v", [P, GB, H, 2 * HD])
            xv = sb("xv", [P, GB, H, 2 * HD])
            NA = 4
            att = sb("att", [P, 2, NA, 4, S])
            sums = sb("sums", [P, 2, 4, S])
            denom = sb("denom", [P, 2, H])
            rec = sb("rec", [P, 2, H])
            o = sb("o", [P, 2, D])
            oT = sb("oT", [P, 2, C, S])
            mx = sb("mx", [P, 2, H])
            nshift = sb("nshift", [P, 2, 2, H], BF16)
            shiftT = sb("shiftT", [32, 2, S], BF16)
            NX = 2 * C * P + 2 * KH * P + C * P
            wbits = sb("weight_bits", [P, NX], I32)
            NB = 4
            assert NX % NB == 0
            low = sb("low_bits", [P, NB * G + 1])

            bank = [ctx.enter_context(nc.psum_tensor(f"bank{n}", [P, 512], F32)) for n in range(8)]
            NP = 3
            pb, lin_bank, sbk, ob = bank[0:NP], bank[3], bank[4:6], bank[6:8]

            weights = sem("weights_loaded")
            const_ready = sem("const_ready")
            act_const = sem("act_const")
            x_loaded, ctx_loaded = sem("x_loaded"), sem("ctx_loaded")
            bias_ready = sem("bias_ready")
            LNS = [dict((w, sem(f"ln{n + 1}_{w}")) for w in ("stats", "mean_var", "ve", "rstd", "xn", "turned", "xnT"))
                   for n in range(3)]
            xb_done = sem("xb_done")
            qk_psum, qk_exp, qk_min, qk_done = sem("qk_psum"), sem("qk_exp"), sem("qk_min"), sem("qk_done")
            PART = {n: [sem(f"{n}_{w}") for w in ("part1", "rest", "part2", "part3", "parts_stored", "rows_loaded")]
                    for n in ("q", "k", "xq", "xk")}
            v_psum, v_done = sem("v_psum"), sem("v_done")
            lin_s, lin_c, lin_a = sem("lin_scores"), sem("lin_scores_out"), sem("lin_masked")
            av_done, sums_done, turned_sums, den_done, rec_done, divided = (
                [sem(f"{which}_{w}") for which in ("lin", "x")]
                for w in ("sums", "sums_out", "sums_turned", "denominator", "reciprocal", "divided"))
            on_turned, oT_done, wo_psum, x1_done = sem("o_turned"), sem("oT_done"), sem("wo_psum"), sem("x1_done")
            kept = sem("x1_kept")
            xq_psum, xk_psum = sem("xq_psum"), sem("xk_psum")
            xv_psum, xv_done = sem("xv_psum"), sem("xv_done")
            max_psum, max_done = sem("max_psum"), sem("max_done")
            sh_hi, sh_lo = sem("shift_hi"), sem("shift_lo")
            sh_psum, sh_done = sem("shift_turned"), sem("shift_done")
            sh_rows = [sem(f"shift_rows{n}") for n in range(2)]
            x_s, x_e = sem("x_scores"), sem("x_exp")
            x2_done = sem("x2_done")
            x2T_psum, x2T_done = sem("x2T_psum"), sem("x2T_done")
            LN1, LN2, LN3 = LNS
            wbits_loaded, wbits_read, low_done, low_psum = (
                sem(n) for n in ("wbits_loaded", "wbits_read", "low_done", "low_psum"))

            streams = {"start": "Q", "fill": "LQ", "first": "LQX", "mid": "TLQX", "drain": "TLX", "last": "TX", "end": "T"}

            plan = [("Q", "load_x", 0, dict(sync=0)), ("X", "load_bits", 0, dict(sync=0)), ("L", "load_ctx", 0, dict(sync=0)),
                    ("X", "keep_x1", 0, dict(scalar=5.1)),
                    ("Q", "q_split", 0, dict(scalar=13.6, vector=14)),
                    ("Q", "q_split2", 0, dict(scalar=14.6, gpsimd=14.8, sync=15)), ("Q", "q_rows", 0, dict(sync=16)),
                    ("Q", "k_split", 0, dict(scalar=17.6, vector=18)),
                    ("Q", "k_split2", 0, dict(scalar=18.6, gpsimd=18.8, sync=19)), ("Q", "k_rows", 0, dict(sync=19.2)),
                    ("Q", "xb", 0, dict(gpsimd=24)),
                    ("L", "xk_split2", 0, dict(scalar=23.6, gpsimd=23.8, sync=24)), ("L", "xk_rows", 0, dict(sync=26.2)),
                    ("L", "xq_split2", 0, dict(scalar=27.6, gpsimd=27.8, sync=28)), ("L", "xq_rows", 0, dict(sync=28.2))]
            for n in range(NU):
                plan += [("L", "lin_scores", n, dict(tensor=n, scalar=n + .1, gpsimd=n + .3)), ("L", "lin_sums", n, dict(tensor=n + 2)),
                         ("X", "max_scores", n, dict(tensor=n + 3.2, vector=n + 3.5)),
                         ("X", "x_scores", n, dict(tensor=n + 10.3, scalar=n + 10.4)),
                         ("X", "x_sums", n, dict(tensor=n + 12.3))]
            for b in range(GB):
                at = 4 * b
                plan += [("L", "lin_sums_out", b, dict(scalar=at + 5.6)),
                         ("L", "lin_divide", b, dict(tensor=at + 6.5, vector=at + 7.2)),
                         ("L", "lin_turn", b, dict(tensor=at + 8.3, scalar=at + 8.6)),
                         ("L", "out_project", b, dict(tensor=at + 9.3, vector=at + 10.2, gpsimd=at + 10.3)),
                         ("L", "ln2", b, dict(vector=at + 11.5)),
                         ("Q", "ln1_stats", b, dict(vector=b + 4, gpsimd=b + 4.2)), ("Q", "ln1", b, dict(vector=b + 5.5)),
                         ("X", "shift", b, dict(vector=at + 6.6, tensor=at + 7.4, scalar=at + 7.6)),
                         ("X", "x_sums_out", b, dict(scalar=at + 15.6)),
                         ("X", "x_divide", b, dict(tensor=at + 16.6, vector=at + 17.2, gpsimd=at + 17.3)),
                         ("T", "ln3", b, dict(vector=.8)) if b == 3 else ("X", "ln3", b, dict(vector=at + 18.5)),
                         ("T", "x2T", b, dict(tensor=1.6 + .7 * b, scalar=1.8 + .7 * b, sync=1.9 + .7 * b))]
            for n in range(NB):
                plan += [("X", "low_bits", n, dict(vector=21 + 1.5 * n))]
            for c in range(C):
                plan += [("Q", "ln1T", c, dict(tensor=9.6 + c, scalar=9.9 + c)),
                         ("Q", "q", c, dict(tensor=11.5 + c, scalar=12 + c, vector=12.3 + c)),
                         ("Q", "k", c, dict(tensor=15.5 + c, scalar=16 + c, vector=16.3 + c)),
                         ("Q", "v", c, dict(tensor=18.5 + c, vector=19.3 + c)),
                         ("L", "xk", c, dict(tensor=21 + c, scalar=21.6 + c, vector=22 + c)),
                         ("L", "ln2T", c, dict(tensor=24.5 + .4 * c, scalar=24.7 + .4 * c)),
                         ("L", "xq", c, dict(tensor=25.5 + c, scalar=26 + c, vector=26.4 + c)),
                         ("L", "xv", c, dict(tensor=27.5 + c, scalar=28 + c))]

            def steps(kind, engine):
                mine = [(slots[engine], step, n) for stream, step, n, slots in plan
                        if stream in streams[kind] and engine in slots]
                return [(step, n) for _, step, n in sorted(mine, key=lambda entry: entry[0])]

            def each_turn(eng, body):
                body("start", -2)
                body("fill", -1)
                body("first", 0)
                with eng.Fori(1, G - 2) as i:
                    body("mid", i)
                body("drain", G - 2)
                body("last", G - 1)
                body("end", G)

            in_banks = {"lin_divide": "sl", "lin_turn": "on", "out_project": "wo", "shift": "sh", "x_divide": "sx",
                        **{name: name for name in ("x2T", "xk", "ln1T", "q", "k", "v", "ln2T", "xq", "xv")}}
            freed = {"sx": (0, divided[1], GB), "x2T": (-1, x2T_done, 2 * C),
                     "ln1T": (2, LN1["xnT"], C), "q": (2, qk_done, 2 * C), "k": (2, qk_done, 2 * C), "v": (2, v_done, 2),
                     "ln2T": (1, LN2["xnT"], C), "xq": (1, PART["xq"][1], C), "xk": (1, PART["xk"][1], C),
                     "xv": (1, xv_done, 2), "sl": (1, divided[0], GB), "on": (1, oT_done, GB), "wo": (1, x1_done, GB),
                     "sh": (0, sh_done, GB)}

            def bank_uses(kind):
                uses = []
                for step, n in steps(kind, "tensor"):
                    if step in in_banks:
                        uses.append(f"{in_banks[step]}{n}")
                    if (step, n) == ("x2T", 3):
                        uses += [None] * PAD
                return uses

            PAD = 0
            PAD = -len(bank_uses("mid")) % NP
            lists = {kind: bank_uses(kind) for kind in streams}
            kinds = list(streams)
            before = dict(zip(kinds[1:], kinds[:-1]))
            assert lists["first"][-2 * NP:] == lists["mid"][-2 * NP:] and len(lists["mid"]) % NP == 0
            begin = {kind: sum(len(lists[k]) for k in kinds[:at]) for at, kind in enumerate(kinds)}

            def pbank(kind, use):
                return pb[(begin[kind] + lists[kind].index(use)) % NP]

            def wait_pbank(eng, kind, i, use):
                pos, turn, prev = lists[kind].index(use), i, None
                while prev is None:
                    pos -= NP
                    while pos < 0:
                        if kind == "start":
                            return
                        kind, turn = before[kind], turn - 1
                        pos += len(lists[kind])
                    prev = lists[kind][pos]
                name, n = prev[:-1], int(prev[-1])
                ahead, s, per = freed[name]
                eng.wait_ge(s, per * (turn + ahead) + (C + n if name == "k" else n) + 1)

            s_order = [step for step in steps("mid", "tensor") if step[0] in ("max_scores", "x_scores")]
            assert len(s_order) % 2 == 0
            s_freed = {"max_scores": max_done, "x_scores": x_e}

            def sbank(step, n):
                return sbk[s_order.index((step, n)) % 2]

            def wait_sbank(eng, i, step, n):
                pos = s_order.index((step, n)) - 2
                step, n = s_order[pos]
                j = i - 1 if pos < 0 else i
                if not (isinstance(j, int) and j < 0):
                    eng.wait_ge(s_freed[step], NU * j + n + 1)

            def wait_count(eng, s, count):
                if not (isinstance(count, int) and count <= 0):
                    eng.wait_ge(s, count)

            def before_in_buffer(name, g):
                last = isinstance(g, int) and g == G - 1
                return ("x" + name, g - 1) if name in "qk" else (name[1], g + 1 if last else g + 2)

            def free_rest(eng, name, g):
                prev, count = before_in_buffer(name, g)
                if not (isinstance(count, int) and count <= 0):
                    eng.wait_ge(PART[prev][3], count)

            def heads(t, first, n, width):
                return t[:, first * width:(first + n) * width].rearrange("p (h d) -> p h d", d=width)

            block = ctx.enter_context(nc.Block())

            @block.sync
            def _(eng):
                x_v = x.rearrange("(g b) s d -> g s b d", b=GB)

                def load_x(g):
                    src = x_v[g] if isinstance(g, int) else x_v[bass.ds(g, 1)].rearrange("g s b d -> (g s) b d")
                    eng.dma_start(x_in[:, :, :], src).then_inc(x_loaded, 16)

                def load_bits(g):
                    wait_count(eng, wbits_read, NB * g)
                    at = 0
                    for w in (w12.rearrange("p m z k o -> p m (z k o)"), h1.rearrange("p m k o -> p m (k o)"),
                              h2.rearrange("p m k o -> p m (k o)"),
                              w3.rearrange("p m (k2 k) o -> p (m k2) (k o)", k2=G // C)):
                        n = w.shape[2]
                        src = w[:, g, :] if isinstance(g, int) else w[:, bass.ds(g, 1), :].rearrange("p m n -> p (m n)")
                        eng.dma_start(wbits[:, at:at + n], src.bitcast(I32)).then_inc(wbits_loaded, 16)
                        at += n
                    assert at == NX

                load_x(0)
                eng.dma_start(cst[:, :], consts).then_inc(weights, 16)
                for dst, src in ((wq, wqT), (wk, wkT), (wv, wvT), (wo, woT), (xwq, xqT), (xwk, xkT), (xwv, xvT)):
                    eng.dma_start(dst[:, :, :], src.rearrange("(c p) o -> p c o", p=P)).then_inc(weights, 16)
                with nc.allow_non_contiguous_dma(reason="biases, once"):
                    eng.dma_start(bqc[:, :], bq.rearrange("(c p) -> p c", p=P)).then_inc(weights, 16)
                    eng.dma_start(bkc[:, :], bk.rearrange("(c p) -> p c", p=P)).then_inc(weights, 16)
                eng.dma_start(bvb[:, :], bv.partition_broadcast(P)).then_inc(weights, 16)
                eng.dma_start(bob[:, :], bo.partition_broadcast(P)).then_inc(weights, 16)
                eng.dma_start(ctxs[:, :, :], tokens(ctxT, 0)).then_inc(ctx_loaded, 16)

                def store_parts(name, g, parts):
                    at = ("q", "k", "xq", "xk").index(name)
                    _, _, _, part3, stored_, _ = PART[name]
                    eng.wait_ge(part3, g + 1)
                    eng.dma_start(parts_d[at].rearrange("j (c p) t -> p j c t", p=P), parts[:, :, :, :]).then_inc(stored_, 16)

                def load_rows(name, g, rows, order, last):
                    at = ("q", "k", "xq", "xk").index(name)
                    _, _, _, _, stored_, loaded = PART[name]
                    eng.wait_ge(stored_, 16 * g + 16)
                    wait_count(eng, last, NU * g)
                    for j, part in enumerate(order):
                        eng.dma_start(rows[HD * j:HD * (j + 1), :, :], parts_d[at, part].rearrange("(h d) t -> d h t", d=HD))\
                           .then_inc(loaded, 16)

                def body(kind, i):
                    for step, n in steps(kind, "sync"):
                        if step == "load_x" and kind != "start":
                            eng.wait_ge(xb_done, i + 2)
                            load_x(i + 2)
                        elif step == "load_bits":
                            load_bits(i)
                        elif step == "x2T" and n % C == C - 1:
                            eng.wait_ge(x2T_done, 2 * C * (i - 1) + n + 1)
                            dst, src = ((x2T_d, x2T), (xnT_d, xn3T))[n // C]
                            eng.dma_start(tokens(dst, i - 1), src[:, :, :]).then_inc(stored, 16)
                        elif step == "xk_split2":
                            store_parts("xk", i + 1, kp)
                        elif step == "xk_rows":
                            load_rows("xk", i + 1, xks, K_PARTS, x_s)
                        elif step == "xq_split2":
                            store_parts("xq", i + 1, qp)
                        elif step == "xq_rows":
                            load_rows("xq", i + 1, xqs, Q_PARTS, x_s)
                        elif step == "q_split2":
                            store_parts("q", i + 2, qp)
                        elif step == "q_rows":
                            load_rows("q", i + 2, qs, Q_PARTS, lin_s)
                        elif step == "k_split2":
                            store_parts("k", i + 2, kp)
                        elif step == "k_rows":
                            load_rows("k", i + 2, ks, K_PARTS, lin_s)
                        elif step == "load_ctx" and kind != "fill":
                            eng.wait_ge(xv_psum, 2 * (i + 1))
                            eng.dma_start(ctxs[:, :, :], tokens(ctxT, i + 1)).then_inc(ctx_loaded, 16)

                each_turn(eng, body)
                eng.wait_ge(stored, 32 * G)

            NW = 16 * 12

            @block.gpsimd
            def _(eng):
                eng.memset(v[:, :, :, :], 1.0).then_inc(const_ready, 1)
                eng.memset(xv[:, :, :, :], 1.0).then_inc(const_ready, 1)
                eng.memset(mhalf[:, :], -0.5).then_inc(const_ready, 1)
                eng.memset(eps[:, :], LN_EPS).then_inc(const_ready, 1)
                eng.wait_ge(const_ready, 5)
                eng.wait_ge(weights, NW)

                def ln_rstd(ln, n, g, b):
                    eng.wait_ge(ln["mean_var"], GB * g + b + 1)
                    eng.tensor_tensor(ve[:, n, b:b + 1], mv[:, n, b, 1:2], eps[:, 0:1], ALU.add).then_inc(ln["ve"], 1)
                    eng.wait_ge(ln["ve"], GB * g + b + 1)
                    eng.tensor_tensor(rstd[:, n, b:b + 1], ve[:, n, b:b + 1], mhalf[:, 0:1], ALU.pow)\
                       .then_inc(ln["rstd"], 1)

                def masked(g, n):
                    eng.wait_ge(lin_c, NU * g + n + 1)
                    slot = att[:, 0, n % NA, :, :]
                    eng.tensor_tensor(slot, slot, causal.rearrange("p (o s) -> p o s", o=1).broadcast_to([P, 4, S]), ALU.mult)\
                       .then_inc(lin_a, 1)

                def residual_bias(g):
                    eng.wait_ge(x_loaded, 16 * g + 16)
                    if not (isinstance(g, int) and g == 0):
                        eng.wait_ge(x1_done, GB * g)
                    eng.wait_ge(LN1["xn"], GB * g + GB)
                    eng.tensor_tensor(xb[:, :, :], x_in[:, :, :],
                                      bob[:, :].rearrange("p (o d) -> p o d", o=1).broadcast_to([P, GB, D]),
                                      ALU.add).then_inc(xb_done, 1)

                def third(name, g, rest, parts):
                    _, rested, part2, part3, stored_, _ = PART[name]
                    eng.wait_ge(part2, g + 1)
                    eng.tensor_tensor(parts[:, 2, :, :], rest[:, :, :], parts[:, 1, :, :], ALU.subtract).then_inc(part3, 1)

                def body(kind, i):
                    for step, n in steps(kind, "gpsimd"):
                        if step == "lin_scores":
                            masked(i + 1, n)
                        elif step == "ln1_stats":
                            ln_rstd(LN1, 0, i + 2, n)
                        elif step == "out_project":
                            ln_rstd(LN2, 1, i + 1, n)
                        elif step == "x_divide":
                            ln_rstd(LN3, 2, i, n)
                        elif step == "xb":
                            residual_bias(i + 2)
                        elif step == "xk_split2":
                            third("xk", i + 1, kf, kp)
                        elif step == "xq_split2":
                            third("xq", i + 1, qf, qp)
                        elif step == "q_split2":
                            third("q", i + 2, qf, qp)
                        elif step == "k_split2":
                            third("k", i + 2, kf, kp)

                each_turn(eng, body)

            @block.scalar
            def _(eng):
                eng.wait_ge(weights, NW)
                eng.preload_act_table(ACT.Exp)
                eng.activation(identb[:, :], ident, ACT.Copy).then_inc(act_const, 1)
                def turned(kind, c, g, ln, name, dst, last_use, per):
                    eng.wait_ge(ln["turned"], C * g + c + 1)
                    if c == 0:
                        wait_count(eng, last_use, per * g)
                    eng.activation(dst[:, c, :], pbank(kind, f"{name}{c}")[:, :], ACT.Copy).then_inc(ln["xnT"], 1)

                def qk_exp_(kind, g, t, c):
                    n = "qk".index(t) * C + c
                    eng.wait_ge(qk_psum, 2 * C * g + n + 1)
                    wait_count(eng, qk_done, 2 * C * g + n - 1)
                    eng.activation(ex[:, c, :], pbank(kind, f"{t}{c}")[:, :], ACT.Exp,
                                   bias=(bqc if t == "q" else bkc)[:, c:c + 1]).then_inc(qk_exp, 1)

                def scores_out(g, n):
                    eng.wait_ge(lin_s, NU * g + n + 1)
                    wait_count(eng, av_done[0], NU * g + n - NA + 1)
                    eng.activation(att[:, 0, n % NA, :, :], lin_bank[:, :].rearrange("p (j s) -> p j s", j=4), ACT.Copy)\
                       .then_inc(lin_c, 1)

                def free_parts(name, g):
                    prev, count = before_in_buffer(name, g)
                    if not (isinstance(count, int) and count <= 0):
                        eng.wait_ge(PART[prev][4], 16 * count)

                def first_part(name, g, src, parts):
                    part1, _, _, _, _, _ = PART[name]
                    eng.wait_ge(qk_done, 2 * C * g + C * "qk".index(name) + C)
                    free_parts(name, g)
                    eng.activation(parts[:, 0, :, :], src[:, :, :], ACT.Copy).then_inc(part1, 1)

                def first_part_psum(kind, name, g, ready, parts, c):
                    if c == 0:
                        free_parts(name, g)
                    eng.wait_ge(ready, C * g + c + 1)
                    eng.activation(parts[:, 0, c, :], pbank(kind, f"{name}{c}")[:, :], ACT.Copy).then_inc(PART[name][0], 1)

                def second_part(name, g, rest, parts):
                    _, rested, part2, _, _, _ = PART[name]
                    eng.wait_ge(rested, (g + 1) * (C if name[0] == "x" else 1))
                    eng.activation(parts[:, 1, :, :], rest[:, :, :], ACT.Copy).then_inc(part2, 1)

                def sums_out(g, part, b):
                    eng.wait_ge(av_done[part], NU * g + 4 * b + 4)
                    wait_count(eng, turned_sums[part], GB * g + b)
                    eng.activation(sums[:, part, :, :], ob[part][:, :].rearrange("p (u s) -> p u s", u=4), ACT.Copy)\
                       .then_inc(sums_done[part], 1)

                def oT_out(kind, i, b):
                    eng.wait_ge(on_turned, GB * i + b + 1)
                    if not (isinstance(i, int) and i == 0 and b < 2):
                        eng.wait_ge(wo_psum, GB * i + b - 1)
                    eng.activation(oT[:, b % 2, :, :], pbank(kind, f"on{b}")[:, 0:D].rearrange("p (c s) -> p c s", c=C),
                                   ACT.Copy).then_inc(oT_done, 1)

                def xv_out(kind, g, n):
                    eng.wait_ge(xv_psum, 2 * g + n + 1)
                    if n == 0:
                        wait_count(eng, av_done[1], NU * g)
                    if n == 0 and isinstance(g, int) and g == 0:
                        eng.wait_ge(const_ready, 5)
                    eng.activation(xv[:, 2 * n:2 * n + 2, :, 0:HD].rearrange("p b h d -> p (b h) d"),
                                   pbank(kind, f"xv{n}")[:, :].rearrange("p (h d) -> p h d", d=HD), ACT.Copy)\
                       .then_inc(xv_done, 1)

                def shift_out(kind, i, b):
                    eng.wait_ge(sh_psum, GB * i + b + 1)
                    wait_count(eng, sh_rows[b % 2], 32 * (2 * i + b // 2))
                    eng.activation(shiftT[:, b % 2, :],
                                   pbank(kind, f"sh{b}")[0:32, 0:S // 2].bitcast(BF16), ACT.Copy)\
                       .then_inc(sh_done, 1)
                    eng.wait_ge(sh_done, GB * i + b + 1)
                    for part in range(2):
                        eng.dma_start(xqs[KR + part:KR + part + 1, :, b * S:(b + 1) * S],
                                      shiftT[H * part:H * part + H, b % 2, :]).then_inc(sh_rows[b % 2], 16)

                def exponentials(i, n):
                    eng.wait_ge(x_s, NU * i + n + 1)
                    wait_count(eng, av_done[1], NU * i + n - NA + 1)
                    eng.activation(att[:, 1, n % NA, :, :],
                                   sbank("x_scores", n)[:, :].rearrange("p (j s) -> p j s", j=4), ACT.Exp, scale=SCALE)\
                       .then_inc(x_e, 1)

                def body(kind, i):
                    for step, n in steps(kind, "scalar"):
                        if step == "lin_scores":
                            scores_out(i + 1, n)
                        elif step == "ln1T":
                            turned(kind, n, i + 2, LN1, "ln1T", xn1T, v_psum, 2)
                        elif step == "q" or step == "k":
                            qk_exp_(kind, i + 2, step, n)
                        elif step == "q_split":
                            first_part("q", i + 2, qf, qp)
                        elif step == "k_split":
                            first_part("k", i + 2, kf, kp)
                        elif step == "q_split2":
                            second_part("q", i + 2, qf, qp)
                        elif step == "k_split2":
                            second_part("k", i + 2, kf, kp)
                        elif step == "xk":
                            first_part_psum(kind, "xk", i + 1, xk_psum, kp, n)
                        elif step == "xk_split2":
                            second_part("xk", i + 1, kf, kp)
                        elif step == "xq":
                            first_part_psum(kind, "xq", i + 1, xq_psum, qp, n)
                        elif step == "xq_split2":
                            second_part("xq", i + 1, qf, qp)
                        elif step == "xv":
                            xv_out(kind, i + 1, n)
                        elif step == "lin_sums_out":
                            sums_out(i + 1, 0, n)
                        elif step == "lin_turn":
                            oT_out(kind, i + 1, n)
                        elif step == "ln2T":
                            turned(kind, n, i + 1, LN2, "ln2T", xn2T, xq_psum, C)
                        elif step == "keep_x1":
                            eng.wait_ge(x1_done, GB * i + GB)
                            wait_count(eng, x2T_psum, 2 * C * i)
                            wait_count(eng, LN3["xn"], GB * i)
                            eng.activation(x2[:, :, :], x1[:, :, :], ACT.Copy).then_inc(kept, 1)
                        elif step == "shift":
                            shift_out(kind, i, n)
                        elif step == "x_scores":
                            exponentials(i, n)
                        elif step == "x_sums_out":
                            sums_out(i, 1, n)
                        elif step == "x2T":
                            eng.wait_ge(x2T_psum, 2 * C * (i - 1) + n + 1)
                            if n == 0:
                                wait_count(eng, stored, 32 * (i - 1))
                            eng.activation((x2T, xn3T)[n // C][:, n % C, :], pbank(kind, f"x2T{n}")[:, :], ACT.Copy)\
                               .then_inc(x2T_done, 1)

                each_turn(eng, body)

            @block.vector
            def _(eng):
                eng.memset(xks[KR:KR + 2, :, :], 1.0).then_inc(const_ready, 1)
                eng.wait_ge(weights, NW)
                eng.tensor_scalar(bq1[:, :], bqc[:, :], 1.0, None, ALU.add).then_inc(bias_ready, 1)
                eng.tensor_scalar(bk1[:, :], bkc[:, :], 1.0, None, ALU.add).then_inc(bias_ready, 1)
                eng.wait_ge(bias_ready, 2)

                def mean_var(ln, n, src, g, b):
                    eng.bn_stats(stats[:, n, b, :], src[:, b, :]).then_inc(ln["stats"], 1)
                    eng.wait_ge(ln["stats"], GB * g + b + 1)
                    eng.memset(unused[0:1, :], 0.0)
                    eng.bn_aggr(mv[:, n, b, :], stats[:, n, b, :]).then_inc(ln["mean_var"], 1)

                def normalise(ln, n, dst, src, g, b, per, last):
                    eng.wait_ge(ln["rstd"], GB * g + b + 1)
                    if b == 0 and not (isinstance(g, int) and g == 0):
                        eng.wait_ge(last, per * g)
                    eng.tensor_scalar(dst[:, b, :], src[:, b, :], mv[:, n, b, 0:1], rstd[:, n, b:b + 1],
                                      ALU.subtract, ALU.mult).then_inc(ln["xn"], 1)

                def ln1(g, b):
                    if b == 0:
                        eng.wait_ge(x_loaded, 16 * g + 16)
                    mean_var(LN1, 0, x_in, g, b)

                def qk_out(kind, g, t, c):
                    n = "qk".index(t) * C + c
                    eng.wait_ge(qk_exp, 2 * C * g + n + 1)
                    eng.tensor_scalar(ex[:, c, :], ex[:, c, :], 1.0, None, ALU.min).then_inc(qk_min, 1)
                    eng.wait_ge(qk_min, 2 * C * g + n + 1)
                    if c == 0:
                        free_rest(eng, t, g)
                    eng.scalar_tensor_tensor((qf if t == "q" else kf)[:, c, :], pbank(kind, f"{t}{c}")[:, :],
                                             (bq1 if t == "q" else bk1)[:, c:c + 1], ex[:, c, :],
                                             ALU.add, ALU.max).then_inc(qk_done, 1)

                def rest(name, g, src, parts):
                    part1, rested, _, _, _, _ = PART[name]
                    eng.wait_ge(part1, g + 1)
                    eng.tensor_tensor(src[:, :, :], src[:, :, :], parts[:, 0, :, :], ALU.subtract).then_inc(rested, 1)

                def rest_psum(kind, name, g, dst, parts, c):
                    part1, rested, _, _, _, _ = PART[name]
                    eng.wait_ge(part1, C * g + c + 1)
                    if c == 0:
                        free_rest(eng, name, g)
                    eng.tensor_tensor(dst[:, c, :], pbank(kind, f"{name}{c}")[:, :], parts[:, 0, c, :], ALU.subtract)\
                       .then_inc(rested, 1)

                def v_out(kind, g, n):
                    eng.wait_ge(v_psum, 2 * g + n + 1)
                    if n == 0 and isinstance(g, int) and g == 0:
                        eng.wait_ge(const_ready, 5)
                    if n == 0:
                        wait_count(eng, av_done[0], NU * g)
                    for b in range(2):
                        last = eng.tensor_tensor(v[:, 2 * n + b, :, 0:HD], heads(pbank(kind, f"v{n}"), b * H, H, HD),
                                                 heads(bvb, 0, H, HD), ALU.add)
                    last.then_inc(v_done, 1)

                def divide(kind, use, g, part, b):
                    bank_ = heads(pbank(kind, use), 0, H, 2 * HD)
                    count = GB * g + b + 1
                    eng.wait_ge(turned_sums[part], count)
                    eng.tensor_scalar(denom[:, part, :], bank_[:, :, HD], (ATT_EPS, 0.0)[part], None, ALU.add)\
                       .then_inc(den_done[part], 1)
                    eng.wait_ge(den_done[part], count)
                    eng.reciprocal(rec[:, part, :], denom[:, part, :]).then_inc(rec_done[part], 1)
                    eng.wait_ge(rec_done[part], count)
                    if part == 0:
                        wait_count(eng, on_turned, count - 1)
                    eng.tensor_tensor(heads(o[:, part, :], 0, H, HD), bank_[:, :, 0:HD],
                                      rec[:, part, :].rearrange("p (h o) -> p h o", o=1).broadcast_to([P, H, HD]),
                                      ALU.mult).then_inc(divided[part], 1)

                def residual1(kind, g, b):
                    eng.wait_ge(wo_psum, GB * g + b + 1)
                    eng.wait_ge(xb_done, g + 1)
                    if b == 0:
                        wait_count(eng, kept, g)
                    eng.tensor_tensor(x1[:, b, :], pbank(kind, f"wo{b}")[:, 0:D], xb[:, b, :], ALU.add)\
                       .then_inc(x1_done, 1)
                    eng.wait_ge(x1_done, GB * g + b + 1)
                    mean_var(LN2, 1, x1, g, b)

                def maximum(i, n):
                    b, h = n // 4, 4 * (n % 4)
                    eng.wait_ge(max_psum, NU * i + n + 1)
                    eng.tensor_reduce(mx[:, b % 2, h:h + 4], sbank("max_scores", n)[:, :].rearrange("p (j t) -> p j t", j=4),
                                      AX.X, ALU.max).then_inc(max_done, 1)

                def shift(i, b):
                    eng.wait_ge(max_done, NU * i + 4 * b + 4)
                    if not (isinstance(i, int) and i == 0 and b < 2):
                        eng.wait_ge(sh_psum, GB * i + b - 1)
                    eng.tensor_scalar(nshift[:, b % 2, 0, :], mx[:, b % 2, :], -1.0, None, ALU.mult).then_inc(sh_hi, 1)
                    eng.wait_ge(sh_hi, GB * i + b + 1)
                    eng.scalar_tensor_tensor(nshift[:, b % 2, 1, :], mx[:, b % 2, :], -1.0, nshift[:, b % 2, 0, :],
                                             ALU.mult, ALU.subtract).then_inc(sh_lo, 1)

                def residual2(kind, g, b):
                    divide(kind, f"sx{b}", g, 1, b)
                    eng.wait_ge(divided[1], GB * g + b + 1)
                    if b == 0:
                        eng.wait_ge(kept, g + 1)
                    eng.tensor_tensor(x2[:, b, :], x2[:, b, :], o[:, 1, :], ALU.add).then_inc(x2_done, 1)
                    eng.wait_ge(x2_done, GB * g + b + 1)
                    mean_var(LN3, 2, x2, g, b)

                def low_bits_of(i, n):
                    if n == 0:
                        eng.wait_ge(wbits_loaded, 64 * i + 64)
                    part = wbits[:, n * NX // NB:(n + 1) * NX // NB]
                    eng.tensor_scalar(part, part, 0xFFF, None, ALU.bitwise_and).then_inc(low_done, 1)
                    eng.wait_ge(low_done, NB * i + n + 1)
                    at = NB * i + n
                    out = low[:, at:at + 1] if isinstance(i, int) else low[:, bass.ds(at, 1)]
                    eng.tensor_reduce(out, part, AX.X, ALU.max).then_inc(wbits_read, 1)

                def body(kind, i):
                    for step, n in steps(kind, "vector"):
                        if step == "ln1_stats":
                            ln1(i + 2, n)
                        elif step == "ln1":
                            normalise(LN1, 0, xn1, x_in, i + 2, n, C, LN1["turned"])
                        elif step == "q" or step == "k":
                            qk_out(kind, i + 2, step, n)
                        elif step == "q_split":
                            rest("q", i + 2, qf, qp)
                        elif step == "k_split":
                            rest("k", i + 2, kf, kp)
                        elif step == "v":
                            v_out(kind, i + 2, n)
                        elif step == "xk":
                            rest_psum(kind, "xk", i + 1, kf, kp, n)
                        elif step == "xq":
                            rest_psum(kind, "xq", i + 1, qf, qp, n)
                        elif step == "lin_divide":
                            divide(kind, f"sl{n}", i + 1, 0, n)
                        elif step == "out_project":
                            residual1(kind, i + 1, n)
                        elif step == "ln2":
                            normalise(LN2, 1, xn2, x1, i + 1, n, C, LN2["turned"])
                        elif step == "max_scores":
                            maximum(i, n)
                        elif step == "shift":
                            shift(i, n)
                        elif step == "x_divide":
                            residual2(kind, i, n)
                        elif step == "ln3":
                            normalise(LN3, 2, xn3, x2, i - 1 if n == 3 else i, n, 2 * C, x2T_psum)
                        elif step == "low_bits":
                            low_bits_of(i, n)

                each_turn(eng, body)
                eng.wait_ge(wbits_read, NB * G)
                eng.tensor_reduce(low[:, NB * G:NB * G + 1], low[:, 0:NB * G], AX.X, ALU.max).then_inc(low_done, 1)
                eng.wait_ge(low_psum, 1)
                eng.tensor_scalar(flag[:, :], lin_bank[0:1, 0:1], 1.0, None, ALU.min).then_inc(flag_ready, 1)

            @block.tensor
            def _(eng):
                eng.wait_ge(weights, NW)
                eng.wait_ge(act_const, 1)
                eng.wait_ge(const_ready, 5)

                def turn(kind, i, g, src, name, ready, done, n, c):
                    eng.wait_ge(ready, GB * g + GB)
                    wait_pbank(eng, kind, i, f"{name}{n}")
                    for b in range(GB):
                        mm = eng.transpose(pbank(kind, f"{name}{n}")[:, b * S:(b + 1) * S], src[:, b, c * P:(c + 1) * P], ident)
                    mm.then_inc(done, 1)

                def project(kind, i, name, w, src, done, m):
                    wait_pbank(eng, kind, i, f"{name}{m}")
                    for c in range(C):
                        mm = eng.matmul(pbank(kind, f"{name}{m}")[:, :], w[:, c, m * P:(m + 1) * P], src[:, c, :],
                                        start=(c == 0), stop=(c == C - 1))
                    mm.then_inc(done, 1)

                def values(kind, i, name, w, src, done, n):
                    wait_pbank(eng, kind, i, f"{name}{n}")
                    for b in (2 * n, 2 * n + 1):
                        for c in range(C):
                            mm = eng.matmul(pbank(kind, f"{name}{n}")[:, b % 2 * D:b % 2 * D + D],
                                            src[:, c, b * S:(b + 1) * S], w[:, c, :],
                                            start=(c == 0), stop=(c == C - 1))
                    mm.then_inc(done, 1)

                def lin_scores(i, n):
                    b, h = n // 4, 4 * (n % 4)
                    if n == 0:
                        eng.wait_ge(PART["q"][5], 96 * i + 96)
                        eng.wait_ge(PART["k"][5], 96 * i + 96)
                    wait_count(eng, lin_c, NU * i + n)
                    for j in range(4):
                        mm = eng.matmul(lin_bank[:, j * S:(j + 1) * S], ks[:, h + j, b * S:(b + 1) * S],
                                        qs[:, h + j, b * S:(b + 1) * S], start=True, stop=True)
                    mm.then_inc(lin_s, 1)

                def add_up(g, part, n, vt, ready):
                    b, h = n // 4, 4 * (n % 4)
                    eng.wait_ge(ready, NU * g + n + 1)
                    if n % 4 == 0:
                        wait_count(eng, sums_done[part], GB * g + b)
                    for r in range(4):
                        mm = eng.matmul(ob[part][32 * r:32 * r + 32, n % 4 * S:(n % 4 + 1) * S], vt[:, b, h + r, :],
                                        att[:, part, n % NA, r, :], start=True, stop=True, tile_position=(0, 32 * r))
                    mm.then_inc(av_done[part], 1)

                def turn_sums(kind, use, i, g, part, b):
                    eng.wait_ge(sums_done[part], GB * g + b + 1)
                    wait_pbank(eng, kind, i, use)
                    for u in range(4):
                        mm = eng.transpose(pbank(kind, use)[:, u * P:(u + 1) * P], sums[:, part, u, :], ident)
                    mm.then_inc(turned_sums[part], 1)

                def turn_o(kind, i, g, b):
                    eng.wait_ge(divided[0], GB * g + b + 1)
                    wait_pbank(eng, kind, i, f"on{b}")
                    for c in range(C):
                        mm = eng.transpose(pbank(kind, f"on{b}")[:, c * S:(c + 1) * S], o[:, 0, c * P:(c + 1) * P], ident)
                    mm.then_inc(on_turned, 1)

                def out_project(kind, i, g, b):
                    eng.wait_ge(oT_done, GB * g + b + 1)
                    wait_pbank(eng, kind, i, f"wo{b}")
                    for c in range(C):
                        mm = eng.matmul(pbank(kind, f"wo{b}")[:, 0:D], oT[:, b % 2, c, :], wo[:, c, :],
                                        start=(c == 0), stop=(c == C - 1))
                    mm.then_inc(wo_psum, 1)

                def max_scores(i, n):
                    b, h = n // 4, 4 * (n % 4)
                    if n == 0:
                        eng.wait_ge(PART["xq"][5], 96 * i + 96)
                        eng.wait_ge(PART["xk"][5], 96 * i + 96)
                    wait_sbank(eng, i, "max_scores", n)
                    for j in range(4):
                        mm = eng.matmul(sbank("max_scores", n)[:, j * S:(j + 1) * S], xqs[0:KR, h + j, b * S:(b + 1) * S],
                                        xks[0:KR, h + j, b * S:(b + 1) * S], start=True, stop=True)
                    mm.then_inc(max_psum, 1)

                def turn_shift(kind, i, b):
                    eng.wait_ge(sh_lo, GB * i + b + 1)
                    wait_pbank(eng, kind, i, f"sh{b}")
                    eng.transpose(pbank(kind, f"sh{b}")[0:32, 0:S // 2].bitcast(BF16),
                                  nshift[:, b % 2, :, :].rearrange("p a h -> p (a h)"), identb[:, :]).then_inc(sh_psum, 1)

                def x_scores(i, n):
                    b, h = n // 4, 4 * (n % 4)
                    if n % 4 == 0:
                        eng.wait_ge(sh_rows[b % 2], 32 * (2 * i + b // 2) + 32)
                    wait_sbank(eng, i, "x_scores", n)
                    for j in range(4):
                        mm = eng.matmul(sbank("x_scores", n)[:, j * S:(j + 1) * S], xks[:, h + j, b * S:(b + 1) * S],
                                        xqs[:, h + j, b * S:(b + 1) * S], start=True, stop=True)
                    mm.then_inc(x_s, 1)

                def body(kind, i):
                    for step, n in steps(kind, "tensor"):
                        if step == "ln1T":
                            turn(kind, i, i + 2, xn1, "ln1T", LN1["xn"], LN1["turned"], n, n)
                        elif step == "q":
                            eng.wait_ge(LN1["xnT"], C * (i + 2) + C)
                            project(kind, i, "q", wq, xn1T, qk_psum, n)
                        elif step == "k":
                            project(kind, i, "k", wk, xn1T, qk_psum, n)
                        elif step == "v":
                            values(kind, i, "v", wv, xn1T, v_psum, n)
                        elif step == "xk":
                            eng.wait_ge(ctx_loaded, 16 * (i + 1) + 16)
                            project(kind, i, "xk", xwk, ctxs, xk_psum, n)
                        elif step == "xv":
                            values(kind, i, "xv", xwv, ctxs, xv_psum, n)
                        elif step == "lin_scores":
                            lin_scores(i + 1, n)
                        elif step == "lin_sums":
                            if n == 0:
                                eng.wait_ge(v_done, 2 * (i + 1) + 2)
                            add_up(i + 1, 0, n, v, lin_a)
                        elif step == "lin_divide":
                            turn_sums(kind, f"sl{n}", i, i + 1, 0, n)
                        elif step == "lin_turn":
                            turn_o(kind, i, i + 1, n)
                        elif step == "out_project":
                            out_project(kind, i, i + 1, n)
                        elif step == "ln2T":
                            turn(kind, i, i + 1, xn2, "ln2T", LN2["xn"], LN2["turned"], n, n)
                        elif step == "xq":
                            eng.wait_ge(LN2["xnT"], C * (i + 1) + C)
                            project(kind, i, "xq", xwq, xn2T, xq_psum, n)
                        elif step == "max_scores":
                            max_scores(i, n)
                        elif step == "shift":
                            turn_shift(kind, i, n)
                        elif step == "x_scores":
                            x_scores(i, n)
                        elif step == "x_sums":
                            if n == 0:
                                eng.wait_ge(xv_done, 2 * i + 2)
                            add_up(i, 1, n, xv, x_e)
                        elif step == "x_divide":
                            turn_sums(kind, f"sx{n}", i, i, 1, n)
                        elif step == "x2T":
                            src, ready = ((x2, x2_done), (xn3, LN3["xn"]))[n // C]
                            turn(kind, i, i - 1, src, "x2T", ready, x2T_psum, n, n % C)

                each_turn(eng, body)
                eng.wait_ge(low_done, NB * G + 1)
                eng.matmul(lin_bank[0:1, 0:1], low[:, NB * G:NB * G + 1], causal[:, P - 1:P], start=True, stop=True).then_inc(low_psum, 1)

        ctx = ExitStack()
        with ctx:
            base = (nc.sbuf_base + 31) // 32 * 32

            def sb(name, shape, dt=F32):
                return ctx.enter_context(nc.sbuf_tensor(name, shape, dt))

            FA = nc.alloc_sbuf_tensor_at("general_hidden_a", [P, KH, T], F32, offset=base)
            FB = nc.alloc_sbuf_tensor_at("general_hidden_b", [P, KH, T], F32, offset=base + KH * T * 4)
            FW = nc.alloc_sbuf_tensor_at("general_weights", [P, 2, KH, P], F32, offset=base + 2 * KH * T * 4)
            w12r = sb("w12_r", [P, KH, 2, C, P], F32R)
            h1r = sb("h1_r", [P, KH, KH, P], F32R)
            h2r = sb("h2_r", [P, KH, KH, P], F32R)
            w3r = sb("w3_r", [P, C, KH, P], F32R)
            HA = sb("hidden_a", [P, 2, KH, T], F32R)
            HB = sb("hidden_b", [P, 2, KH, T], F32R)
            xin = sb("ffn_in", [P, C, T])
            xhl = sb("ffn_in_parts", [P, 2, C, T], F32R)
            res = sb("ffn_residual", [P, C, T])
            gate = sb("gate", [P, T])
            full = sb("hidden_full", [P, 2, T])
            s1c, s2c, sh1c, sh2c = (sb(n, [P, KH]) for n in ("s1c", "s2c", "sh1c", "sh2c"))
            s3c, s1h, s12 = sb("s3c", [P, C]), sb("s1h", [P, KH]), sb("s12", [P, KH])

            bank = [ctx.enter_context(nc.psum_tensor(f"ffn_bank{n}", [P, T], F32)) for n in range(8)]
            scales, s1h_done, s12_done = sem("scales_loaded"), sem("s1h_done"), sem("s12_done")
            w_loaded = {n: sem(f"{n}_loaded") for n in ("w12a", "w12b", "h1a", "h1b", "h2", "w3")}
            in_loaded, res_loaded = sem("ffn_in_loaded"), sem("residual_loaded")
            hi_done, in_done = sem("in_hi"), sem("in_parts")
            gate_psum, gate_act, gate_mul, gate_full = (sem(n) for n in ("gate_psum", "gate_act", "gate_mul", "gate_full"))
            gate_hi, gate_lo = sem("gate_hi"), sem("gate_lo")
            h_psum, h_full, h_hi, h_lo = sem("h_psum"), sem("h_full"), sem("h_hi"), sem("h_lo")
            o_psum, o_done, o_stored = sem("o_psum"), sem("o_done"), sem("o_stored")
            g_loaded = [sem(f"general_weights_loaded{n}") for n in range(2)]
            out_t = sb("out_tile", [P, C, T])

            def some(n):
                return not isinstance(n, int) or n > 0

            def exact_gpsimd(eng):
                half = KH // 2
                for dst, src, s in ((w12r[:, 0:half], w12[:, 0:half], "w12a"), (w12r[:, half:KH], w12[:, half:KH], "w12b"),
                                    (h1r[:, 0:half], h1[:, 0:half], "h1a"), (h1r[:, half:KH], h1[:, half:KH], "h1b"),
                                    (h2r[:, :], h2[:, :], "h2"), (w3r[:, :], w3[:, :], "w3")):
                    eng.dma_start(dst, src).then_inc(w_loaded[s], 16)

            def exact_sync(eng):
                eng.dma_start(xin[:, :, :], tokens(xnT_d, 0)).then_inc(in_loaded, 16)
                eng.dma_start(res[:, :, :], tokens(x2T_d, 0)).then_inc(res_loaded, 16)
                with nc.allow_non_contiguous_dma(reason="scales, once"):
                    for dst, src in ((s1c, s1), (s2c, s2), (sh1c, sh1), (sh2c, sh2), (s3c, s3)):
                        eng.dma_start(dst[:, :], src.rearrange("(c p) -> p c", p=P)).then_inc(scales, 16)

                def store(i):
                    eng.wait_ge(o_done, C * i + C)
                    eng.dma_start(tokens(outT, i), out_t[:, :, :]).then_inc(o_stored, 16)

                with eng.Fori(1, G) as i:
                    eng.wait_ge(in_done, i)
                    eng.dma_start(xin[:, :, :], tokens(xnT_d, i)).then_inc(in_loaded, 16)
                    store(i - 1)
                    eng.dma_start(res[:, :, :], tokens(x2T_d, i)).then_inc(res_loaded, 16)
                store(G - 1)
                eng.wait_ge(o_stored, 16 * G)

            def exact_scalar(eng):
                eng.wait_ge(scales, 16 * 5)
                eng.preload_act_table(ACT.Gelu)
                eng.activation(s1h[:, :], s1c[:, :], ACT.Copy, scale=0.5).then_inc(s1h_done, 1)
                eng.wait_ge(s1h_done, 1)

                def split_in(i):
                    eng.wait_ge(in_loaded, 16 * i + 16)
                    if some(i):
                        eng.wait_ge(gate_psum, KH * i)
                    eng.activation(xhl[:, 0, :, :], xin[:, :, :], ACT.Copy).then_inc(hi_done, 1)

                def gates(i, m):
                    eng.wait_ge(gate_psum, KH * i + m + 1)
                    if some(KH * i + m):
                        eng.wait_ge(gate_mul, KH * i + m)
                    eng.activation(gate[:, :], bank[2 * m % 4][:, :], ACT.Tanh, scale=s1h[:, m:m + 1])\
                       .then_inc(gate_act, 1)

                def gate_round(i, m):
                    eng.wait_ge(gate_full, KH * i + m + 1)
                    if m == 0 and some(i):
                        eng.wait_ge(o_psum, C * i)
                    eng.activation(HA[:, 0, m, :], full[:, m % 2, :], ACT.Copy).then_inc(gate_hi, 1)

                def hidden(i, n):
                    m, layer = n % KH, n // KH
                    src, dst, sc = bank[4 + n % 4], (HB, HA)[layer], (sh1c, sh2c)[layer][:, m:m + 1]
                    eng.wait_ge(h_psum, 2 * KH * i + n + 1)
                    if n >= 2:
                        eng.wait_ge(h_lo, 2 * KH * i + n - 1)
                    else:
                        eng.wait_ge(gate_lo, KH * i + KH - 1 + n)
                    eng.activation(full[:, n % 2, :], src[:, :], ACT.Gelu, scale=sc).then_inc(h_full, 1)
                    if n == 0 and some(i):
                        eng.wait_ge(h_psum, 2 * KH * i)
                    eng.activation(dst[:, 0, m, :], src[:, :], ACT.Gelu, scale=sc).then_inc(h_hi, 1)

                split_in(0)

                def body(i, last=False):
                    for m in range(KH):
                        gates(i, m)
                        if m >= 1:
                            gate_round(i, m - 1)
                    gate_round(i, KH - 1)
                    for n in range(2 * KH):
                        hidden(i, n)
                        if n == 2 and not last:
                            split_in(i + 1)

                body(0)
                with eng.Fori(1, G - 1) as i:
                    body(i)
                body(G - 1, last=True)

            def exact_vector(eng):
                eng.wait_ge(scales, 16 * 5)
                eng.scalar_tensor_tensor(s12[:, :], s1c[:, :], 0.5, s2c[:, :], ALU.mult, ALU.mult).then_inc(s12_done, 1)
                eng.wait_ge(s12_done, 1)

                def rest_in(i):
                    eng.wait_ge(hi_done, i + 1)
                    eng.tensor_tensor(xhl[:, 1, :, :], xin[:, :, :], xhl[:, 0, :, :].bitcast(F32), ALU.subtract)\
                       .then_inc(in_done, 1)

                def gated(i, m):
                    eng.wait_ge(gate_act, KH * i + m + 1)
                    f = full[:, m % 2, :]
                    if m < 2:
                        if some(i):
                            eng.wait_ge(h_lo, 2 * KH * i)
                    else:
                        eng.wait_ge(gate_lo, KH * i + m - 1)
                    eng.scalar_tensor_tensor(f, gate[:, :], 1.0, bank[2 * m % 4][:, :], ALU.add, ALU.mult)\
                       .then_inc(gate_mul, 1)
                    eng.wait_ge(gate_mul, KH * i + m + 1)
                    eng.scalar_tensor_tensor(f, bank[2 * m % 4 + 1][:, :], s12[:, m:m + 1], f, ALU.mult, ALU.mult)\
                       .then_inc(gate_full, 1)

                def gate_rest(i, m):
                    eng.wait_ge(gate_hi, KH * i + m + 1)
                    eng.tensor_tensor(HA[:, 1, m, :], full[:, m % 2, :], HA[:, 0, m, :].bitcast(F32), ALU.subtract)\
                       .then_inc(gate_lo, 1)

                def hidden_rest(i, n):
                    m, dst = n % KH, (HB, HA)[n // KH]
                    eng.wait_ge(h_hi, 2 * KH * i + n + 1)
                    eng.tensor_tensor(dst[:, 1, m, :], full[:, n % 2, :], dst[:, 0, m, :].bitcast(F32), ALU.subtract)\
                       .then_inc(h_lo, 1)

                def output(i, c):
                    eng.wait_ge(o_psum, C * i + c + 1)
                    eng.wait_ge(res_loaded, 16 * i + 16)
                    if c == 0 and some(i):
                        eng.wait_ge(o_stored, 16 * i)
                    eng.scalar_tensor_tensor(out_t[:, c, :], bank[c][:, :], s3c[:, c:c + 1], res[:, c, :],
                                             ALU.mult, ALU.add).then_inc(o_done, 1)

                rest_in(0)

                def body(i, last=False):
                    for m in range(KH):
                        gated(i, m)
                        if m >= 1:
                            gate_rest(i, m - 1)
                    gate_rest(i, KH - 1)
                    for n in range(2 * KH):
                        hidden_rest(i, n)
                        if n == 2 and not last:
                            rest_in(i + 1)
                    for c in range(C):
                        output(i, c)

                body(0)
                with eng.Fori(1, G - 1) as i:
                    body(i)
                body(G - 1, last=True)

            def exact_tensor(eng):
                def products(out, w, src, n):
                    for kk in range(n):
                        for part in range(2):
                            mm = eng.matmul(out[:, :], w(kk), src[:, part, kk, :],
                                            start=(kk == 0 and part == 0), stop=(kk == n - 1 and part == 1))
                    return mm

                def body(i):
                    eng.wait_ge(in_done, i + 1)
                    for m in range(KH):
                        if m == 0:
                            eng.wait_ge(w_loaded["w12a"], 16)
                            if some(i):
                                eng.wait_ge(o_done, C * i)
                        if m == KH // 2:
                            eng.wait_ge(w_loaded["w12b"], 16)
                        if m >= 2:
                            eng.wait_ge(gate_full, KH * i + m - 1)
                        for z in range(2):
                            mm = products(bank[2 * m % 4 + z], lambda kk: w12r[:, m, z, kk, :], xhl, C)
                        mm.then_inc(gate_psum, 1)
                    for n in range(2 * KH):
                        m, w, src = n % KH, (h1r, h2r)[n // KH], (HA, HB)[n // KH]
                        if n == 0:
                            eng.wait_ge(w_loaded["h1a"], 16)
                        if n == KH // 2:
                            eng.wait_ge(w_loaded["h1b"], 16)
                        if n == KH:
                            eng.wait_ge(w_loaded["h2"], 16)
                        if some(2 * KH * i + n - 3):
                            eng.wait_ge(h_hi, 2 * KH * i + n - 3)
                        for kk in range(KH):
                            if m == 0:
                                if n == 0:
                                    eng.wait_ge(gate_lo, KH * i + kk + 1)
                                else:
                                    eng.wait_ge(h_lo, 2 * KH * i + kk + 1)
                            for part in range(2):
                                mm = eng.matmul(bank[4 + n % 4][:, :], w[:, m, kk, :], src[:, part, kk, :],
                                                start=(kk == 0 and part == 0), stop=(kk == KH - 1 and part == 1))
                        mm.then_inc(h_psum, 1)
                    eng.wait_ge(w_loaded["w3"], 16)
                    eng.wait_ge(gate_full, KH * i + KH - 1)
                    for c in range(C):
                        for kk in range(KH):
                            if c == 0:
                                eng.wait_ge(h_lo, 2 * KH * i + KH + kk + 1)
                            for part in range(2):
                                mm = eng.matmul(bank[c][:, :], w3r[:, c, kk, :], HA[:, part, kk, :],
                                                start=(kk == 0 and part == 0), stop=(kk == KH - 1 and part == 1))
                        mm.then_inc(o_psum, 1)

                body(0)
                with eng.Fori(1, G) as i:
                    body(i)

            NT = KH + 2 * KH + C

            def general_sync(eng):
                def body(i):
                    if some(i):
                        eng.wait_ge(o_done, C * i)
                    eng.dma_start(xin[:, :, :], tokens(xnT_d, i)).then_inc(in_loaded, 16)
                    eng.dma_start(res[:, :, :], tokens(x2T_d, i)).then_inc(res_loaded, 16)
                    for j in range(NT):
                        used = j - 2
                        if 0 <= used < KH:
                            eng.wait_ge(gate_psum, KH * i + used + 1)
                        elif KH <= used < 3 * KH:
                            eng.wait_ge(h_psum, 2 * KH * i + used - KH + 1)
                        if j < KH:
                            src = w12[:, j].rearrange("p z k o -> p (z k) o")
                        elif j < 2 * KH:
                            src = h1[:, j - KH]
                        elif j < 3 * KH:
                            src = h2[:, j - 2 * KH]
                        else:
                            src = w3[:, j - 3 * KH]
                        eng.dma_start(FW[:, j % 2, 0:src.shape[1], :], src).then_inc(g_loaded[j % 2], 16)
                    eng.wait_ge(o_done, C * i + C)
                    eng.dma_start(tokens(outT, i), out_t[:, :, :]).then_inc(o_stored, 16)

                with nc.allow_non_contiguous_dma(reason="scales, once"):
                    for dst, src in ((s1c, s1), (s2c, s2), (sh1c, sh1), (sh2c, sh2), (s3c, s3)):
                        eng.dma_start(dst[:, :], src.rearrange("(c p) -> p c", p=P)).then_inc(scales, 16)
                body(0)
                with eng.Fori(1, G) as i:
                    body(i)
                eng.wait_ge(o_stored, 16 * G)

            def general_scalar(eng):
                eng.wait_ge(scales, 16 * 5)
                eng.activation(s1h[:, :], s1c[:, :], ACT.Copy, scale=0.5).then_inc(s1h_done, 1)
                eng.wait_ge(s1h_done, 1)

                def body(i):
                    for m in range(KH):
                        eng.wait_ge(gate_psum, KH * i + m + 1)
                        if some(KH * i + m):
                            eng.wait_ge(gate_mul, KH * i + m)
                        eng.activation(gate[:, :], bank[2 * m % 4][:, :], ACT.Tanh, scale=s1h[:, m:m + 1])\
                           .then_inc(gate_act, 1)
                    for n in range(2 * KH):
                        m, dst, sc = n % KH, (FB, FA)[n // KH], (sh1c, sh2c)[n // KH]
                        eng.wait_ge(h_psum, 2 * KH * i + n + 1)
                        eng.activation(dst[:, m, :], bank[4 + n % 4][:, :], ACT.Gelu, scale=sc[:, m:m + 1])\
                           .then_inc(h_full, 1)

                body(0)
                with eng.Fori(1, G) as i:
                    body(i)

            def general_vector(eng):
                eng.wait_ge(scales, 16 * 5)
                eng.scalar_tensor_tensor(s12[:, :], s1c[:, :], 0.5, s2c[:, :], ALU.mult, ALU.mult).then_inc(s12_done, 1)
                eng.wait_ge(s12_done, 1)

                def body(i):
                    for m in range(KH):
                        eng.wait_ge(gate_act, KH * i + m + 1)
                        eng.scalar_tensor_tensor(FA[:, m, :], gate[:, :], 1.0, bank[2 * m % 4][:, :], ALU.add, ALU.mult)\
                           .then_inc(gate_mul, 1)
                        eng.wait_ge(gate_mul, KH * i + m + 1)
                        eng.scalar_tensor_tensor(FA[:, m, :], bank[2 * m % 4 + 1][:, :], s12[:, m:m + 1], FA[:, m, :],
                                                 ALU.mult, ALU.mult).then_inc(gate_full, 1)
                    eng.wait_ge(res_loaded, 16 * i + 16)
                    if some(i):
                        eng.wait_ge(o_stored, 16 * i)
                    for c in range(C):
                        eng.wait_ge(o_psum, C * i + c + 1)
                        eng.scalar_tensor_tensor(out_t[:, c, :], bank[c][:, :], s3c[:, c:c + 1], res[:, c, :],
                                                 ALU.mult, ALU.add).then_inc(o_done, 1)

                body(0)
                with eng.Fori(1, G) as i:
                    body(i)

            def general_tensor(eng):
                def body(i):
                    eng.wait_ge(in_loaded, 16 * i + 16)
                    for j in range(NT):
                        eng.wait_ge(g_loaded[j % 2], 16 * (NT // 2 * i + j // 2) + 16)
                        if j < KH:
                            if j == 0 and some(i):
                                eng.wait_ge(o_done, C * i)
                            if j >= 2:
                                eng.wait_ge(gate_full, KH * i + j - 1)
                            for z in range(2):
                                for kk in range(C):
                                    mm = eng.matmul(bank[2 * j % 4 + z][:, :], FW[:, j % 2, C * z + kk, :], xin[:, kk, :],
                                                    start=(kk == 0), stop=(kk == C - 1))
                            mm.then_inc(gate_psum, 1)
                        elif j < 3 * KH:
                            n = j - KH
                            if n == 0:
                                eng.wait_ge(gate_full, KH * i + KH)
                            if n == KH:
                                eng.wait_ge(h_full, 2 * KH * i + KH)
                            if some(2 * KH * i + n - 3):
                                eng.wait_ge(h_full, 2 * KH * i + n - 3)
                            for kk in range(KH):
                                mm = eng.matmul(bank[4 + n % 4][:, :], FW[:, j % 2, kk, :], (FA, FB)[n // KH][:, kk, :],
                                                start=(kk == 0), stop=(kk == KH - 1))
                            mm.then_inc(h_psum, 1)
                        else:
                            c = j - 3 * KH
                            if c == 0:
                                eng.wait_ge(h_full, 2 * KH * i + 2 * KH)
                            for kk in range(KH):
                                mm = eng.matmul(bank[c][:, :], FW[:, j % 2, kk, :], FA[:, kk, :],
                                                start=(kk == 0), stop=(kk == KH - 1))
                            mm.then_inc(o_psum, 1)

                body(0)
                with eng.Fori(1, G) as i:
                    body(i)

            block = ctx.enter_context(nc.Block())

            def inexact(eng):
                eng.wait_ge(flag_ready, 1)
                return eng.value_load(flag[0:1, 0:1], min_val=0, max_val=1) != 0

            @block.gpsimd
            def _(eng):
                with eng.If(inexact(eng)):
                    pass
                with eng.Else():
                    exact_gpsimd(eng)

            @block.sync
            def _(eng):
                with eng.If(inexact(eng)):
                    general_sync(eng)
                with eng.Else():
                    exact_sync(eng)

            @block.scalar
            def _(eng):
                with eng.If(inexact(eng)):
                    general_scalar(eng)
                with eng.Else():
                    exact_scalar(eng)

            @block.vector
            def _(eng):
                with eng.If(inexact(eng)):
                    general_vector(eng)
                with eng.Else():
                    exact_vector(eng)

            @block.tensor
            def _(eng):
                with eng.If(inexact(eng)):
                    general_tensor(eng)
                with eng.Else():
                    exact_tensor(eng)


_INS = ["x", "ctxT", "wqT", "wkT", "wvT", "woT", "bq", "bk", "bv", "bo", "xqT", "xkT", "xvT",
        "w12", "h1", "h2", "w3", "s1", "s2", "sh1", "sh2", "s3", "consts"]


def constants():
    import numpy as np
    c = np.zeros((128, 256), np.float32)
    c[:, 0:128] = np.eye(128)
    c[:, 128:256] = np.triu(np.ones((128, 128)))
    return c


def kernel(**inputs):
    import numpy as np
    import concourse.bacc as bacc
    from concourse.bass_utils import run_bass_kernel_spmd

    a = {n: np.asarray(v) for n, v in inputs.items()}
    B, S, D = a["x"].shape

    def turned(w):
        return np.ascontiguousarray(np.transpose(w))

    def by_tile(w, columns):
        o, i = w.shape
        return np.ascontiguousarray(np.transpose(w.reshape(o // columns, columns, i // 128, 128), (3, 0, 2, 1)))

    w1, w2 = by_tile(a["L0_ffn_w1_w"], 128), by_tile(a["L0_ffn_w2_w"], 128)
    arrays = {
        "x": np.ascontiguousarray(a["x"]),
        "ctxT": turned(a["ctx_1024"].reshape(B * S, D)),
        "wqT": turned(a["L0_attn_Wq"]), "wkT": turned(a["L0_attn_Wk"]),
        "wvT": turned(a["L0_attn_Wv"]), "woT": turned(a["L0_attn_Wo"]),
        "bq": a["L0_attn_bq"], "bk": a["L0_attn_bk"], "bv": a["L0_attn_bv"], "bo": a["L0_attn_bo"],
        "xqT": turned(a["L0_xattn_Wq"]), "xkT": turned(a["L0_xattn_Wk"]), "xvT": turned(a["L0_xattn_Wv"]),
        "w12": np.ascontiguousarray(np.stack([w1, w2], axis=2)),
        "h1": by_tile(a["L0_ffn_h1_w"], 128), "h2": by_tile(a["L0_ffn_h2_w"], 128),
        "w3": by_tile(a["L0_ffn_w3_w"], 128),
        "s1": a["L0_ffn_w1_s"], "s2": a["L0_ffn_w2_s"],
        "sh1": a["L0_ffn_h1_s"], "sh2": a["L0_ffn_h2_s"], "s3": a["L0_ffn_w3_s"],
        "consts": constants(),
    }
    nc = bacc.Bacc("TRN2", target_bir_lowering=False, num_devices=1)
    args = [nc.dram_tensor(f"in_{n}", arrays[n].shape, mybir.dt.from_np(arrays[n].dtype), kind="ExternalInput").ap()
            for n in _INS]
    out = nc.dram_tensor("out_T", (D, B * S), mybir.dt.float32, kind="ExternalOutput").ap()
    decoder_layer_program(nc, *args, out)
    r = run_bass_kernel_spmd(nc, [{f"in_{n}": arrays[n] for n in _INS}], core_ids=[0])
    return np.ascontiguousarray(np.transpose(r.results[0]["out_T"])).reshape(B, S, D)
```

```python
import concourse.bass as bass
from concourse import mybir
from contextlib import ExitStack


def decoder_layer_program(nc, x, ctxT, wqT, wkT, wvT, woT, bv, bo, xqT, xkT, xvT,
                          w12, h1, h2, w3, columns, consts, outT):
    F32, F32R, BF16, I32 = mybir.dt.float32, mybir.dt.float32r, mybir.dt.bfloat16, mybir.dt.int32
    ALU, ACT, AX = mybir.AluOpType, mybir.ActivationFunctionType, mybir.AxisListType

    P = 128
    B, S, D = x.shape
    H, HD = 16, 16
    HID = w12.shape[1] * 128
    C = D // P
    GB = 4
    T = GB * S
    G = B // GB
    KH = HID // P
    LN_EPS, ATT_EPS, SCALE = 1e-5, 1e-6, HD ** -0.5
    NU = 4 * GB

    x2T_d = nc.dram_tensor("x2T_scratch", [D, B * S], F32, kind="Internal").ap()
    xnT_d = nc.dram_tensor("xn3T_scratch", [D, B * S], F32, kind="Internal").ap()

    parts_d = nc.dram_tensor("parts_scratch", [4, 3, P, C * T], BF16, kind="Internal").ap()

    def tokens(ap, g):
        v = ap.rearrange("(c p) t -> p c t", p=P)
        if isinstance(g, int):
            return v[:, :, g * T:(g + 1) * T]
        return v[:, :, bass.ds(g * T, T)]

    outer = ExitStack()

    def sem(name):
        return outer.enter_context(nc.semaphore(name))

    with outer:
        flag = outer.enter_context(nc.sbuf_tensor("inexact_flag", [1, 1], I32))
        flag_ready = sem("flag_ready")
        cols = outer.enter_context(nc.sbuf_tensor("columns_sb", [P, 4 * KH + 3 * C], F32))
        s1c, s2c, sh1c, sh2c = (cols[:, n * KH:(n + 1) * KH] for n in range(4))
        s3c, bqc, bkc = (cols[:, 4 * KH + n * C:4 * KH + (n + 1) * C] for n in range(3))
        stored = sem("scratch_stored")

        base = (nc.sbuf_base + 31) // 32 * 32
        half = KH // 2
        w12r = nc.alloc_sbuf_tensor_at("w12_r", [P, KH, 2, C, P], F32R, offset=base)
        h1r = nc.alloc_sbuf_tensor_at("h1_r", [P, KH, KH, P], F32R, offset=base + KH * 2 * C * P * 4)
        w_loaded = {n: sem(f"{n}_loaded") for n in ("w12a", "w12b", "h1a", "h1b", "h2", "w3")}
        EARLY = ((w12r[:, 0:half], w12[:, 0:half], "w12a"), (w12r[:, half:KH], w12[:, half:KH], "w12b"),
                 (h1r[:, 0:half], h1[:, 0:half], "h1a"))

        ctx = ExitStack()
        with ctx:
            def sb(name, shape, dt=F32):
                return ctx.enter_context(nc.sbuf_tensor(name, shape, dt))

            Q_PARTS, K_PARTS = (0, 1, 2, 0, 1, 0), (0, 0, 0, 1, 1, 2)
            KR = HD * len(Q_PARTS)

            def runs(order):
                out = []
                for j, part in enumerate(order):
                    if out and part == order[j - 1] + 1:
                        out[-1][2] += 1
                    else:
                        out.append([j, part, 1])
                return out

            ROWS = {"q": runs(Q_PARTS), "xq": runs(Q_PARTS), "k": runs(K_PARTS), "xk": runs(K_PARTS)}
            qs, ks = sb("qs", [KR, H, T], BF16), sb("ks", [KR, H, T], BF16)
            wq, wk, wv, wo = (sb(n, [P, C, D]) for n in ("wq", "wk", "wv", "wo"))
            xwq, xwk, xwv = (sb(n, [P, C, D]) for n in ("xwq", "xwk", "xwv"))
            NC_ = consts.shape[1]
            cst = sb("cst", [P, NC_])
            ident = cst[:, 0:128]
            causal = cst[:, 128:256]
            bq1, bk1 = (sb(n, [P, C]) for n in ("bq1", "bk1"))
            bvb, bob = sb("bvb", [P, D]), sb("bob", [P, D])
            identb = sb("identb", [P, P], BF16)
            unused = sb("unused", [P, 1])
            mhalf, eps = sb("mhalf", [P, 1]), sb("eps", [P, 1])

            x_in = sb("x_in", [P, GB, D])
            xn1 = sb("xn1", [P, GB, D])
            xn1T = sb("xn1T", [P, C, T])
            xb = sb("xb", [P, GB, D])
            x1 = sb("x1", [P, GB, D])
            xn2 = sb("xn2", [P, GB, D])
            xn2T = sb("xn2T", [P, C, T])
            x2 = sb("x2", [P, GB, D])
            xn3 = sb("xn3", [P, GB, D])
            x2T = sb("x2T", [P, C, T])
            xn3T = sb("xn3T", [P, C, T])
            ctxs = sb("ctxs", [P, C, T])
            stats = sb("stats", [P, 3, GB, 6])
            mv = sb("mv", [P, 3, GB, 2])
            ve = sb("ve", [P, 3, GB])
            rstd = sb("rstd", [P, 3, GB])

            ex = sb("ex", [P, 2, T])
            qf = sb("qf", [P, C, T])
            kf = sb("kf", [P, C, T])
            qp = sb("qp", [P, 3, C, T], BF16)
            kp = sb("kp", [P, 3, C, T], BF16)
            xqs, xks = sb("xqs", [KR + 2, H, T], BF16), sb("xks", [KR + 2, H, T], BF16)
            v = sb("v", [P, GB, H, 2 * HD])
            xv = sb("xv", [P, GB, H, 2 * HD])
            NA = 4
            att = sb("att", [P, 2, NA, 4, S])
            sums = sb("sums", [P, 2, 4, S])
            denom = sb("denom", [P, 2, H])
            rec = sb("rec", [P, 2, H])
            o = sb("o", [P, 2, D])
            oT = sb("oT", [P, 2, C, S])
            mx = sb("mx", [P, 2, H])
            nshift = sb("nshift", [P, 2, 2, H], BF16)
            shiftT = sb("shiftT", [32, 2, S], BF16)
            NX = 2 * C * P + 2 * KH * P + C * P
            wbits = sb("weight_bits", [P, NX], I32)
            NB = 4
            assert NX % NB == 0
            low = sb("low_bits", [P, NB * G + 1])

            bank = [ctx.enter_context(nc.psum_tensor(f"bank{n}", [P, 512], F32)) for n in range(8)]
            NP = 3
            pb, lin_bank, sbk, ob = bank[0:NP], bank[3], bank[4:6], bank[6:8]

            consts_loaded, weights = sem("consts_loaded"), sem("weights_loaded")
            ln_const, const_ready = sem("ln_const"), sem("const_ready")
            act_const = sem("act_const")
            x_loaded, ctx_loaded = sem("x_loaded"), sem("ctx_loaded")
            bias_ready = sem("bias_ready")
            LNS = [dict((w, sem(f"ln{n + 1}_{w}")) for w in ("stats", "mean_var", "ve", "rstd", "xn", "turned", "xnT"))
                   for n in range(3)]
            xb_done = sem("xb_done")
            qk_psum, qk_exp, qk_min, qk_done = sem("qk_psum"), sem("qk_exp"), sem("qk_min"), sem("qk_done")
            PART = {n: [sem(f"{n}_{w}") for w in ("part1", "rest", "part2", "part3", "parts_stored", "rows_loaded", "rows_loaded1", "parts_stored1")]
                    for n in ("q", "k", "xq", "xk")}
            v_psum, v_done = sem("v_psum"), sem("v_done")
            lin_s, lin_c, lin_a = sem("lin_scores"), sem("lin_scores_out"), sem("lin_masked")
            av_done, sums_done, turned_sums, den_done, rec_done, divided = (
                [sem(f"{which}_{w}") for which in ("lin", "x")]
                for w in ("sums", "sums_out", "sums_turned", "denominator", "reciprocal", "divided"))
            on_turned, oT_done, wo_psum, x1_done = sem("o_turned"), sem("oT_done"), sem("wo_psum"), sem("x1_done")
            kept = sem("x1_kept")
            xq_psum, xk_psum = sem("xq_psum"), sem("xk_psum")
            xv_psum, xv_done = sem("xv_psum"), sem("xv_done")
            max_psum, max_done = sem("max_psum"), sem("max_done")
            sh_hi, sh_lo = sem("shift_hi"), sem("shift_lo")
            sh_psum, sh_done = sem("shift_turned"), sem("shift_done")
            sh_rows = [sem(f"shift_rows{n}") for n in range(2)]
            x_s, x_e = sem("x_scores"), sem("x_exp")
            x2_done = sem("x2_done")
            x2T_psum, x2T_done = sem("x2T_psum"), sem("x2T_done")
            LN1, LN2, LN3 = LNS
            wbits_loaded, wbits_read, low_done, low_psum = (
                sem(n) for n in ("wbits_loaded", "wbits_read", "low_done", "low_psum"))

            streams = {"start": "Q", "fill": "LQ", "first": "LQX", "mid": "TLQX", "drain": "TLX", "last": "TX", "end": "T"}

            plan = [("Q", "load_x", 0, dict(scalar=0.2)), ("X", "load_bits", 0, dict(sync=3.7)), ("L", "load_ctx", 0, dict(sync=5.2)),
                    ("X", "keep_x1", 0, dict(scalar=4.8)),
                    ("Q", "q_split", 0, dict(scalar=13.3, vector=15)),
                    ("Q", "q_split2", 0, dict(scalar=14.9, gpsimd=14.8, sync=15.3)), ("Q", "q_rows", 0, dict(sync=16.7)),
                    ("Q", "k_split", 0, dict(scalar=17.9, vector=18.7)),
                    ("Q", "k_split2", 0, dict(scalar=19.3, gpsimd=19.6, sync=20.1)), ("Q", "k_rows", 0, dict(sync=21.3)),
                    ("Q", "xb", 0, dict(gpsimd=26.5)),
                    ("L", "xk_split2", 0, dict(scalar=24.2, gpsimd=22.2, sync=25.7)), ("L", "xk_rows", 0, dict(sync=26.6)),
                    ("L", "xk_rows", 1, dict(sync=26.7))]
            for n in range(NU):
                plan += [("L", "lin_scores", n, dict(tensor=n, scalar=n + .1, gpsimd=n + .3)), ("L", "lin_sums", n, dict(tensor=n + 2.6)),
                         ("X", "max_scores", n, dict(tensor=n + 3.2, vector=n + 3.5)),
                         ("X", "x_scores", n, dict(tensor=n + 10.3, scalar=n + 10.4)),
                         ("X", "x_sums", n, dict(tensor=n + 11.7))]
            for b in range(GB):
                at = 4 * b
                plan += [("L", "lin_sums_out", b, dict(scalar=at + 5.6)),
                         ("L", "lin_divide", b, dict(tensor=at + 6.5, vector=at + 7.2)),
                         ("L", "lin_turn", b, dict(tensor=at + 8, scalar=at + 8.3)),
                         ("L", "out_project", b, dict(tensor=at + 9.3, vector=at + 10.2, gpsimd=at + 9.6)),
                         ("L", "ln2", b, dict(vector=at + 11.5)),
                         ("Q", "ln1_stats", b, dict(vector=b + 4, gpsimd=b + 4.6)), ("Q", "ln1", b, dict(vector=b + 7.1)),
                         ("X", "shift", b, dict(vector=at + 6.9, tensor=at + 7.4, scalar=at + 7.6)),
                         ("X", "x_sums_out", b, dict(scalar=at + 14.6)),
                         ("X", "x_divide", b, dict(tensor=at + 16.6, vector=at + 17.2, gpsimd=at + 17.3)),
                         ("T", "ln3", b, dict(vector=1.1)) if b == 3 else ("X", "ln3", b, dict(vector=at + 18.8)),
                         ("T", "x2T", b, dict(tensor=.7 * b - 0.2, scalar=.7 * b + 0.8, sync=.7 * b - 1.3))]
            for n in range(NB):
                plan += [("X", "low_bits", n, dict(vector=1.5 * n + 20.3))]
            for c in range(C):
                plan += [("Q", "ln1T", c, dict(tensor=9.6 + c, scalar=9.9 + c)),
                         ("Q", "q", c, dict(tensor=11.5 + c, scalar=12 + c, vector=c + 12.3)),
                         ("Q", "k", c, dict(tensor=15.5 + c, scalar=16 + c, vector=c + 16)),
                         ("Q", "v", c, dict(tensor=c + 18.8, vector=c + 19.9)),
                         ("L", "xk", c, dict(tensor=21 + c, scalar=21.6 + c, vector=c + 23.3)),
                         ("L", "ln2T", c, dict(tensor=17 + 7.2 * c, scalar=17.3 + 7.2 * c)),
                         ("L", "xq", c, dict(tensor=18.4 + 7.2 * c, scalar=19.1 + 7.2 * c, vector=19.5 + 7.2 * c)),
                         ("L", "xq_split2", c, dict(scalar=20.2 + 7.2 * c, gpsimd=20.5 + 7.2 * c, sync=20.9 + 7.2 * c)),
                         ("L", "xq_rows", c, dict(sync=21.7 + 6.5 * c)),
                         ("L", "xv", c, dict(tensor=c + 28.1, scalar=c + 30.3))]

            def steps(kind, engine):
                mine = [(slots[engine], step, n) for stream, step, n, slots in plan
                        if stream in streams[kind] and engine in slots]
                return [(step, n) for _, step, n in sorted(mine, key=lambda entry: entry[0])]

            def each_turn(eng, body):
                body("start", -2)
                body("fill", -1)
                body("first", 0)
                with eng.Fori(1, G - 2) as i:
                    body("mid", i)
                body("drain", G - 2)
                body("last", G - 1)
                body("end", G)

            in_banks = {"lin_divide": "sl", "lin_turn": "on", "out_project": "wo", "shift": "sh", "x_divide": "sx",
                        **{name: name for name in ("x2T", "xk", "ln1T", "q", "k", "v", "ln2T", "xq", "xv")}}
            freed = {"sx": (0, divided[1], GB), "x2T": (-1, x2T_done, 2 * C),
                     "ln1T": (2, LN1["xnT"], C), "q": (2, qk_done, 2 * C), "k": (2, qk_done, 2 * C), "v": (2, v_done, 2),
                     "ln2T": (1, LN2["xnT"], C), "xq": (1, PART["xq"][1], C), "xk": (1, PART["xk"][1], C),
                     "xv": (1, xv_done, 2), "sl": (1, divided[0], GB), "on": (1, oT_done, GB), "wo": (1, x1_done, GB),
                     "sh": (0, sh_done, GB)}

            def bank_uses(kind):
                uses = []
                for step, n in steps(kind, "tensor"):
                    if step in in_banks:
                        uses.append(f"{in_banks[step]}{n}")
                    if (step, n) == ("x2T", 3):
                        uses += [None] * PAD
                return uses

            PAD = 0
            PAD = -len(bank_uses("mid")) % NP
            lists = {kind: bank_uses(kind) for kind in streams}
            kinds = list(streams)
            before = dict(zip(kinds[1:], kinds[:-1]))
            assert lists["first"][-2 * NP:] == lists["mid"][-2 * NP:] and len(lists["mid"]) % NP == 0
            begin = {kind: sum(len(lists[k]) for k in kinds[:at]) for at, kind in enumerate(kinds)}

            def pbank(kind, use):
                return pb[(begin[kind] + lists[kind].index(use)) % NP]

            def wait_pbank(eng, kind, i, use):
                pos, turn, prev = lists[kind].index(use), i, None
                while prev is None:
                    pos -= NP
                    while pos < 0:
                        if kind == "start":
                            return
                        kind, turn = before[kind], turn - 1
                        pos += len(lists[kind])
                    prev = lists[kind][pos]
                name, n = prev[:-1], int(prev[-1])
                ahead, s, per = freed[name]
                eng.wait_ge(s, per * (turn + ahead) + (C + n if name == "k" else n) + 1)

            s_order = [step for step in steps("mid", "tensor") if step[0] in ("max_scores", "x_scores")]
            assert len(s_order) % 2 == 0
            s_freed = {"max_scores": max_done, "x_scores": x_e}

            def sbank(step, n):
                return sbk[s_order.index((step, n)) % 2]

            def wait_sbank(eng, i, step, n):
                pos = s_order.index((step, n)) - 2
                step, n = s_order[pos]
                j = i - 1 if pos < 0 else i
                if not (isinstance(j, int) and j < 0):
                    eng.wait_ge(s_freed[step], NU * j + n + 1)

            def wait_count(eng, s, count):
                if not (isinstance(count, int) and count <= 0):
                    eng.wait_ge(s, count)

            def before_in_buffer(name, g):
                last = isinstance(g, int) and g == G - 1
                return ("x" + name, g - 1) if name in "qk" else (name[1], g + 1 if last else g + 2)

            TH = T // 2

            def token_half(n):
                return slice(n * TH, (n + 1) * TH)

            def free_rest(eng, name, g):
                prev, count = before_in_buffer(name, g)
                wait_count(eng, PART[prev][3], count * (2 if prev == "xq" else 1))

            def heads(t, first, n, width):
                return t[:, first * width:(first + n) * width].rearrange("p (h d) -> p h d", d=width)

            def load_x(eng, g):
                x_v = x.rearrange("(g b) s d -> g s b d", b=GB)
                src = x_v[g] if isinstance(g, int) else x_v[bass.ds(g, 1)].rearrange("g s b d -> (g s) b d")
                eng.dma_start(x_in[:, :, :], src).then_inc(x_loaded, 16)

            block = ctx.enter_context(nc.Block())

            @block.sync
            def _(eng):
                def load_bits(g):
                    wait_count(eng, wbits_read, NB * g)
                    at = 0
                    for w in (w12.rearrange("p m z k o -> p m (z k o)"), h1.rearrange("p m k o -> p m (k o)"),
                              h2.rearrange("p m k o -> p m (k o)"),
                              w3.rearrange("p m (k2 k) o -> p (m k2) (k o)", k2=G // C)):
                        n = w.shape[2]
                        src = w[:, g, :] if isinstance(g, int) else w[:, bass.ds(g, 1), :].rearrange("p m n -> p (m n)")
                        eng.dma_start(wbits[:, at:at + n], src.bitcast(I32)).then_inc(wbits_loaded, 16)
                        at += n
                    assert at == NX

                load_x(eng, 0)
                eng.dma_start(cst[:, :], consts).then_inc(consts_loaded, 16)
                eng.dma_start(cols[:, :], columns).then_inc(consts_loaded, 16)
                for dst, src in ((wq, wqT), (wk, wkT), (wv, wvT), (wo, woT), (xwq, xqT), (xwk, xkT), (xwv, xvT)):
                    eng.dma_start(dst[:, :, :], src.rearrange("(c p) o -> p c o", p=P)).then_inc(weights, 16)
                eng.dma_start(bvb[:, :], bv.partition_broadcast(P)).then_inc(weights, 16)
                eng.dma_start(bob[:, :], bo.partition_broadcast(P)).then_inc(weights, 16)
                eng.dma_start(ctxs[:, :, :], tokens(ctxT, 0)).then_inc(ctx_loaded, 16)

                def store_parts(name, g, parts):
                    at = ("q", "k", "xq", "xk").index(name)
                    _, _, _, part3, stored_ = PART[name][:5]
                    eng.wait_ge(part3, g + 1)
                    eng.dma_start(parts_d[at].rearrange("j p n -> p j n"), parts[:, :, :, :].rearrange("p j c t -> p j (c t)"))\
                       .then_inc(stored_, 16)

                def store_xq(g, n):
                    eng.wait_ge(PART["xq"][3], 2 * g + n + 1)
                    for c in range(C):
                        eng.dma_start(parts_d[2].rearrange("j p (c t) -> p j c t", c=C)[:, :, c, token_half(n)],
                                      qp[:, :, c, token_half(n)]).then_inc(PART["xq"][(4, 7)[n]], 16)

                def load_rows(name, g, rows, last, half=0):
                    at = ("q", "k", "xq", "xk").index(name)
                    if name == "xq":
                        eng.wait_ge(PART[name][(4, 7)[half]], 16 * C * g + 16 * C)
                    else:
                        eng.wait_ge(PART[name][4], 16 * g + 16)
                    tokens_ = slice(0, T)
                    if name[0] == "x":
                        tokens_ = token_half(half)
                        wait_count(eng, last, NU * g - (1 - half) * NU // 2)
                    else:
                        wait_count(eng, last, NU * g)
                    for j, part, n in ROWS[name]:
                        eng.dma_start(rows[HD * j:HD * (j + n), :, tokens_],
                                      parts_d[at, part:part + n].rearrange("j (d e) (c t) -> (j d) (e c) t", d=HD, c=C)[:, :, tokens_])\
                           .then_inc(PART[name][5 + half], 16)

                def body(kind, i):
                    for step, n in steps(kind, "sync"):
                        if step == "load_bits":
                            load_bits(i)
                        elif step == "x2T" and n % C == C - 1:
                            eng.wait_ge(x2T_done, 2 * C * (i - 1) + n + 1)
                            dst, src = ((x2T_d, x2T), (xnT_d, xn3T))[n // C]
                            eng.dma_start(tokens(dst, i - 1), src[:, :, :]).then_inc(stored, 16)
                        elif step == "xk_split2":
                            store_parts("xk", i + 1, kp)
                        elif step == "xk_rows":
                            load_rows("xk", i + 1, xks, x_s, n)
                        elif step == "xq_split2":
                            store_xq(i + 1, n)
                        elif step == "xq_rows":
                            load_rows("xq", i + 1, xqs, x_s, n)
                        elif step == "q_split2":
                            store_parts("q", i + 2, qp)
                        elif step == "q_rows":
                            load_rows("q", i + 2, qs, lin_s)
                        elif step == "k_split2":
                            store_parts("k", i + 2, kp)
                        elif step == "k_rows":
                            load_rows("k", i + 2, ks, lin_s)
                        elif step == "load_ctx" and kind != "fill":
                            eng.wait_ge(xv_psum, 2 * (i + 1))
                            eng.dma_start(ctxs[:, :, :], tokens(ctxT, i + 1)).then_inc(ctx_loaded, 16)

                each_turn(eng, body)

            NCON, NW = 16 * 2, 16 * 9

            @block.gpsimd
            def _(eng):
                eng.memset(mhalf[:, :], -0.5).then_inc(ln_const, 1)
                eng.memset(eps[:, :], LN_EPS).then_inc(ln_const, 1)
                eng.wait_ge(ln_const, 2)

                def ln_rstd(ln, n, g, b):
                    eng.wait_ge(ln["mean_var"], GB * g + b + 1)
                    eng.tensor_tensor(ve[:, n, b:b + 1], mv[:, n, b, 1:2], eps[:, 0:1], ALU.add).then_inc(ln["ve"], 1)
                    eng.wait_ge(ln["ve"], GB * g + b + 1)
                    eng.tensor_tensor(rstd[:, n, b:b + 1], ve[:, n, b:b + 1], mhalf[:, 0:1], ALU.pow)\
                       .then_inc(ln["rstd"], 1)

                def masked(g, n):
                    eng.wait_ge(lin_c, NU * g + n + 1)
                    slot = att[:, 0, n % NA, :, :]
                    eng.tensor_tensor(slot, slot, causal.rearrange("p (o s) -> p o s", o=1).broadcast_to([P, 4, S]), ALU.mult)\
                       .then_inc(lin_a, 1)

                def residual_bias(g):
                    eng.wait_ge(x_loaded, 16 * g + 16)
                    if not (isinstance(g, int) and g == 0):
                        eng.wait_ge(x1_done, GB * g)
                    eng.wait_ge(LN1["xn"], GB * g + GB)
                    eng.tensor_tensor(xb[:, :, :], x_in[:, :, :],
                                      bob[:, :].rearrange("p (o d) -> p o d", o=1).broadcast_to([P, GB, D]),
                                      ALU.add).then_inc(xb_done, 1)

                def third(name, g, rest, parts):
                    _, rested, part2, part3, stored_ = PART[name][:5]
                    eng.wait_ge(part2, g + 1)
                    eng.tensor_tensor(parts[:, 2, :, :], rest[:, :, :], parts[:, 1, :, :], ALU.subtract).then_inc(part3, 1)

                def third_xq(g, n):
                    eng.wait_ge(PART["xq"][2], 2 * g + n + 1)
                    eng.tensor_tensor(qp[:, 2, :, token_half(n)], qf[:, :, token_half(n)], qp[:, 1, :, token_half(n)],
                                      ALU.subtract).then_inc(PART["xq"][3], 1)

                def body(kind, i):
                    for step, n in steps(kind, "gpsimd"):
                        if kind == "last" and (step, n) == ("x_divide", 2):
                            eng.wait_ge(lin_s, NU * G)
                            for s in sh_rows:
                                eng.wait_ge(s, 32 * 2 * G)
                            for dst, src, s in EARLY:
                                eng.dma_start(dst, src).then_inc(w_loaded[s], 16)
                        if step == "lin_scores":
                            masked(i + 1, n)
                        elif step == "ln1_stats":
                            ln_rstd(LN1, 0, i + 2, n)
                            if kind == "start" and n == GB - 1:
                                eng.memset(v[:, :, :, :], 1.0).then_inc(const_ready, 1)
                                eng.memset(xv[:, :, :, :], 1.0).then_inc(const_ready, 1)
                                eng.wait_ge(consts_loaded, NCON)
                                eng.wait_ge(weights, NW)
                        elif step == "out_project":
                            ln_rstd(LN2, 1, i + 1, n)
                        elif step == "x_divide":
                            ln_rstd(LN3, 2, i, n)
                        elif step == "xb":
                            residual_bias(i + 2)
                        elif step == "xk_split2":
                            third("xk", i + 1, kf, kp)
                        elif step == "xq_split2":
                            third_xq(i + 1, n)
                        elif step == "q_split2":
                            third("q", i + 2, qf, qp)
                        elif step == "k_split2":
                            third("k", i + 2, kf, kp)

                each_turn(eng, body)

            @block.scalar
            def _(eng):
                eng.wait_ge(consts_loaded, NCON)
                eng.preload_act_table(ACT.Exp)
                eng.activation(identb[:, :], ident, ACT.Copy).then_inc(act_const, 1)
                def turned(kind, c, g, ln, name, dst, last_use, per):
                    eng.wait_ge(ln["turned"], C * g + c + 1)
                    if c == 0:
                        wait_count(eng, last_use, per * g)
                    eng.activation(dst[:, c, :], pbank(kind, f"{name}{c}")[:, :], ACT.Copy).then_inc(ln["xnT"], 1)

                def qk_exp_(kind, g, t, c):
                    n = "qk".index(t) * C + c
                    eng.wait_ge(qk_psum, 2 * C * g + n + 1)
                    wait_count(eng, qk_done, 2 * C * g + n - 1)
                    eng.activation(ex[:, c, :], pbank(kind, f"{t}{c}")[:, :], ACT.Exp,
                                   bias=(bqc if t == "q" else bkc)[:, c:c + 1]).then_inc(qk_exp, 1)

                def scores_out(g, n):
                    eng.wait_ge(lin_s, NU * g + n + 1)
                    wait_count(eng, av_done[0], NU * g + n - NA + 1)
                    eng.activation(att[:, 0, n % NA, :, :], lin_bank[:, :].rearrange("p (j s) -> p j s", j=4), ACT.Copy)\
                       .then_inc(lin_c, 1)

                def free_parts(name, g):
                    prev, count = before_in_buffer(name, g)
                    if not (isinstance(count, int) and count <= 0):
                        if prev == "xq":
                            eng.wait_ge(PART[prev][4], 16 * C * count)
                            eng.wait_ge(PART[prev][7], 16 * C * count)
                        else:
                            eng.wait_ge(PART[prev][4], 16 * count)

                def first_part(name, g, src, parts):
                    part1, _, _, _, _ = PART[name][:5]
                    eng.wait_ge(qk_done, 2 * C * g + C * "qk".index(name) + C)
                    free_parts(name, g)
                    eng.activation(parts[:, 0, :, :], src[:, :, :], ACT.Copy).then_inc(part1, 1)

                def first_part_psum(kind, name, g, ready, parts, c):
                    if c == 0:
                        free_parts(name, g)
                    eng.wait_ge(ready, C * g + c + 1)
                    eng.activation(parts[:, 0, c, :], pbank(kind, f"{name}{c}")[:, :], ACT.Copy).then_inc(PART[name][0], 1)

                def second_part(name, g, rest, parts):
                    _, rested, part2, _, _ = PART[name][:5]
                    eng.wait_ge(rested, (g + 1) * (C if name[0] == "x" else 1))
                    eng.activation(parts[:, 1, :, :], rest[:, :, :], ACT.Copy).then_inc(part2, 1)

                def first_part_xq(kind, g, n):
                    if n == 0:
                        free_parts("xq", g)
                    eng.wait_ge(xq_psum, 2 * g + n + 1)
                    eng.activation(qp[:, 0, :, token_half(n)], pbank(kind, f"xq{n}")[:, :].rearrange("p (c t) -> p c t", c=C),
                                   ACT.Copy).then_inc(PART["xq"][0], 1)

                def second_part_xq(g, n):
                    eng.wait_ge(PART["xq"][1], 2 * g + n + 1)
                    eng.activation(qp[:, 1, :, token_half(n)], qf[:, :, token_half(n)], ACT.Copy).then_inc(PART["xq"][2], 1)

                def turned_ln2(kind, g, n):
                    eng.wait_ge(LN2["turned"], 2 * g + n + 1)
                    if n == 0:
                        wait_count(eng, xq_psum, 2 * g)
                    eng.activation(xn2T[:, :, token_half(n)], pbank(kind, f"ln2T{n}")[:, :].rearrange("p (c t) -> p c t", c=C),
                                   ACT.Copy).then_inc(LN2["xnT"], 1)

                def sums_out(g, part, b):
                    eng.wait_ge(av_done[part], NU * g + 4 * b + 4)
                    wait_count(eng, turned_sums[part], GB * g + b)
                    eng.activation(sums[:, part, :, :], ob[part][:, :].rearrange("p (u s) -> p u s", u=4), ACT.Copy)\
                       .then_inc(sums_done[part], 1)

                def oT_out(kind, i, b):
                    eng.wait_ge(on_turned, GB * i + b + 1)
                    if not (isinstance(i, int) and i == 0 and b < 2):
                        eng.wait_ge(wo_psum, GB * i + b - 1)
                    eng.activation(oT[:, b % 2, :, :], pbank(kind, f"on{b}")[:, 0:D].rearrange("p (c s) -> p c s", c=C),
                                   ACT.Copy).then_inc(oT_done, 1)

                def xv_out(kind, g, n):
                    eng.wait_ge(xv_psum, 2 * g + n + 1)
                    if n == 0:
                        wait_count(eng, av_done[1], NU * g)
                    if n == 0 and isinstance(g, int) and g == 0:
                        eng.wait_ge(const_ready, 3)
                    eng.activation(xv[:, 2 * n:2 * n + 2, :, 0:HD].rearrange("p b h d -> p (b h) d"),
                                   pbank(kind, f"xv{n}")[:, :].rearrange("p (h d) -> p h d", d=HD), ACT.Copy)\
                       .then_inc(xv_done, 1)

                def shift_out(kind, i, b):
                    eng.wait_ge(sh_psum, GB * i + b + 1)
                    wait_count(eng, sh_rows[b % 2], 32 * (2 * i + b // 2))
                    eng.activation(shiftT[:, b % 2, :],
                                   pbank(kind, f"sh{b}")[0:32, 0:S // 2].bitcast(BF16), ACT.Copy)\
                       .then_inc(sh_done, 1)
                    eng.wait_ge(sh_done, GB * i + b + 1)
                    for part in range(2):
                        eng.dma_start(xqs[KR + part:KR + part + 1, :, b * S:(b + 1) * S],
                                      shiftT[H * part:H * part + H, b % 2, :]).then_inc(sh_rows[b % 2], 16)

                def exponentials(i, n):
                    eng.wait_ge(x_s, NU * i + n + 1)
                    wait_count(eng, av_done[1], NU * i + n - NA + 1)
                    eng.activation(att[:, 1, n % NA, :, :],
                                   sbank("x_scores", n)[:, :].rearrange("p (j s) -> p j s", j=4), ACT.Exp, scale=SCALE)\
                       .then_inc(x_e, 1)

                def body(kind, i):
                    for step, n in steps(kind, "scalar"):
                        if step == "load_x" and kind != "start":
                            eng.wait_ge(xb_done, i + 2)
                            load_x(eng, i + 2)
                        elif step == "lin_scores":
                            scores_out(i + 1, n)
                        elif step == "ln1T":
                            turned(kind, n, i + 2, LN1, "ln1T", xn1T, v_psum, 2)
                        elif step == "q" or step == "k":
                            qk_exp_(kind, i + 2, step, n)
                        elif step == "q_split":
                            first_part("q", i + 2, qf, qp)
                        elif step == "k_split":
                            first_part("k", i + 2, kf, kp)
                        elif step == "q_split2":
                            second_part("q", i + 2, qf, qp)
                        elif step == "k_split2":
                            second_part("k", i + 2, kf, kp)
                        elif step == "xk":
                            first_part_psum(kind, "xk", i + 1, xk_psum, kp, n)
                        elif step == "xk_split2":
                            second_part("xk", i + 1, kf, kp)
                        elif step == "xq":
                            first_part_xq(kind, i + 1, n)
                        elif step == "xq_split2":
                            second_part_xq(i + 1, n)
                        elif step == "xv":
                            xv_out(kind, i + 1, n)
                        elif step == "lin_sums_out":
                            sums_out(i + 1, 0, n)
                        elif step == "lin_turn":
                            oT_out(kind, i + 1, n)
                        elif step == "ln2T":
                            turned_ln2(kind, i + 1, n)
                        elif step == "keep_x1":
                            eng.wait_ge(x1_done, GB * i + GB)
                            wait_count(eng, x2T_psum, 2 * C * i)
                            wait_count(eng, LN3["xn"], GB * i)
                            eng.activation(x2[:, :, :], x1[:, :, :], ACT.Copy).then_inc(kept, 1)
                        elif step == "shift":
                            shift_out(kind, i, n)
                        elif step == "x_scores":
                            exponentials(i, n)
                        elif step == "x_sums_out":
                            sums_out(i, 1, n)
                        elif step == "x2T":
                            eng.wait_ge(x2T_psum, 2 * C * (i - 1) + n + 1)
                            if n == 0:
                                wait_count(eng, stored, 32 * (i - 1))
                            eng.activation((x2T, xn3T)[n // C][:, n % C, :], pbank(kind, f"x2T{n}")[:, :], ACT.Copy)\
                               .then_inc(x2T_done, 1)

                each_turn(eng, body)

            @block.vector
            def _(eng):

                def mean_var(ln, n, src, g, b):
                    eng.bn_stats(stats[:, n, b, :], src[:, b, :]).then_inc(ln["stats"], 1)
                    eng.wait_ge(ln["stats"], GB * g + b + 1)
                    eng.memset(unused[0:1, :], 0.0)
                    eng.bn_aggr(mv[:, n, b, :], stats[:, n, b, :]).then_inc(ln["mean_var"], 1)

                def normalise(ln, n, dst, src, g, b, per, last):
                    eng.wait_ge(ln["rstd"], GB * g + b + 1)
                    if b == 0 and not (isinstance(g, int) and g == 0):
                        eng.wait_ge(last, per * g)
                    eng.tensor_scalar(dst[:, b, :], src[:, b, :], mv[:, n, b, 0:1], rstd[:, n, b:b + 1],
                                      ALU.subtract, ALU.mult).then_inc(ln["xn"], 1)

                def ln1(g, b):
                    if b == 0:
                        eng.wait_ge(x_loaded, 16 * g + 16)
                    mean_var(LN1, 0, x_in, g, b)

                def qk_out(kind, g, t, c):
                    n = "qk".index(t) * C + c
                    eng.wait_ge(qk_exp, 2 * C * g + n + 1)
                    eng.tensor_scalar(ex[:, c, :], ex[:, c, :], 1.0, None, ALU.min).then_inc(qk_min, 1)
                    eng.wait_ge(qk_min, 2 * C * g + n + 1)
                    if c == 0:
                        free_rest(eng, t, g)
                    eng.scalar_tensor_tensor((qf if t == "q" else kf)[:, c, :], pbank(kind, f"{t}{c}")[:, :],
                                             (bq1 if t == "q" else bk1)[:, c:c + 1], ex[:, c, :],
                                             ALU.add, ALU.max).then_inc(qk_done, 1)

                def rest(name, g, src, parts):
                    part1, rested, _, _, _ = PART[name][:5]
                    eng.wait_ge(part1, g + 1)
                    eng.tensor_tensor(src[:, :, :], src[:, :, :], parts[:, 0, :, :], ALU.subtract).then_inc(rested, 1)

                def rest_psum(kind, name, g, dst, parts, c):
                    part1, rested, _, _, _ = PART[name][:5]
                    eng.wait_ge(part1, C * g + c + 1)
                    if c == 0:
                        free_rest(eng, name, g)
                    eng.tensor_tensor(dst[:, c, :], pbank(kind, f"{name}{c}")[:, :], parts[:, 0, c, :], ALU.subtract)\
                       .then_inc(rested, 1)

                def rest_xq(kind, g, n):
                    eng.wait_ge(PART["xq"][0], 2 * g + n + 1)
                    if n == 0:
                        free_rest(eng, "xq", g)
                    eng.tensor_tensor(qf[:, :, token_half(n)], pbank(kind, f"xq{n}")[:, :].rearrange("p (c t) -> p c t", c=C),
                                      qp[:, 0, :, token_half(n)], ALU.subtract).then_inc(PART["xq"][1], 1)

                def v_out(kind, g, n):
                    eng.wait_ge(v_psum, 2 * g + n + 1)
                    if n == 0 and isinstance(g, int) and g == 0:
                        eng.wait_ge(const_ready, 3)
                    if n == 0:
                        wait_count(eng, av_done[0], NU * g)
                    for b in range(2):
                        last = eng.tensor_tensor(v[:, 2 * n + b, :, 0:HD], heads(pbank(kind, f"v{n}"), b * H, H, HD),
                                                 heads(bvb, 0, H, HD), ALU.add)
                    last.then_inc(v_done, 1)

                def divide(kind, use, g, part, b):
                    bank_ = heads(pbank(kind, use), 0, H, 2 * HD)
                    count = GB * g + b + 1
                    eng.wait_ge(turned_sums[part], count)
                    eng.tensor_scalar(denom[:, part, :], bank_[:, :, HD], (ATT_EPS, 0.0)[part], None, ALU.add)\
                       .then_inc(den_done[part], 1)
                    eng.wait_ge(den_done[part], count)
                    eng.reciprocal(rec[:, part, :], denom[:, part, :]).then_inc(rec_done[part], 1)
                    eng.wait_ge(rec_done[part], count)
                    if part == 0:
                        wait_count(eng, on_turned, count - 1)
                    eng.tensor_tensor(heads(o[:, part, :], 0, H, HD), bank_[:, :, 0:HD],
                                      rec[:, part, :].rearrange("p (h o) -> p h o", o=1).broadcast_to([P, H, HD]),
                                      ALU.mult).then_inc(divided[part], 1)

                def residual1(kind, g, b):
                    eng.wait_ge(wo_psum, GB * g + b + 1)
                    eng.wait_ge(xb_done, g + 1)
                    if b == 0:
                        wait_count(eng, kept, g)
                    eng.tensor_tensor(x1[:, b, :], pbank(kind, f"wo{b}")[:, 0:D], xb[:, b, :], ALU.add)\
                       .then_inc(x1_done, 1)
                    eng.wait_ge(x1_done, GB * g + b + 1)
                    mean_var(LN2, 1, x1, g, b)

                def maximum(i, n):
                    b, h = n // 4, 4 * (n % 4)
                    eng.wait_ge(max_psum, NU * i + n + 1)
                    eng.tensor_reduce(mx[:, b % 2, h:h + 4], sbank("max_scores", n)[:, :].rearrange("p (j t) -> p j t", j=4),
                                      AX.X, ALU.max).then_inc(max_done, 1)

                def shift(i, b):
                    eng.wait_ge(max_done, NU * i + 4 * b + 4)
                    if not (isinstance(i, int) and i == 0 and b < 2):
                        eng.wait_ge(sh_psum, GB * i + b - 1)
                    eng.tensor_scalar(nshift[:, b % 2, 0, :], mx[:, b % 2, :], -1.0, None, ALU.mult).then_inc(sh_hi, 1)
                    eng.wait_ge(sh_hi, GB * i + b + 1)
                    eng.scalar_tensor_tensor(nshift[:, b % 2, 1, :], mx[:, b % 2, :], -1.0, nshift[:, b % 2, 0, :],
                                             ALU.mult, ALU.subtract).then_inc(sh_lo, 1)

                def residual2(kind, g, b):
                    divide(kind, f"sx{b}", g, 1, b)
                    eng.wait_ge(divided[1], GB * g + b + 1)
                    if b == 0:
                        eng.wait_ge(kept, g + 1)
                    eng.tensor_tensor(x2[:, b, :], x2[:, b, :], o[:, 1, :], ALU.add).then_inc(x2_done, 1)
                    eng.wait_ge(x2_done, GB * g + b + 1)
                    mean_var(LN3, 2, x2, g, b)

                def low_bits_of(i, n):
                    if n == 0:
                        eng.wait_ge(wbits_loaded, 64 * i + 64)
                    part = wbits[:, n * NX // NB:(n + 1) * NX // NB]
                    eng.tensor_scalar(part, part, 0xFFF, None, ALU.bitwise_and).then_inc(low_done, 1)
                    eng.wait_ge(low_done, NB * i + n + 1)
                    at = NB * i + n
                    out = low[:, at:at + 1] if isinstance(i, int) else low[:, bass.ds(at, 1)]
                    eng.tensor_reduce(out, part, AX.X, ALU.max).then_inc(wbits_read, 1)

                def flag_out():
                    eng.wait_ge(wbits_read, NB * G)
                    eng.tensor_reduce(low[:, NB * G:NB * G + 1], low[:, 0:NB * G], AX.X, ALU.max).then_inc(low_done, 1)
                    eng.wait_ge(low_psum, 1)
                    eng.tensor_scalar(flag[:, :], lin_bank[0:1, 0:1], 1.0, None, ALU.min).then_inc(flag_ready, 1)

                def body(kind, i):
                    if kind == "end":
                        flag_out()
                    for step, n in steps(kind, "vector"):
                        if step == "ln1_stats":
                            ln1(i + 2, n)
                        elif step == "ln1":
                            normalise(LN1, 0, xn1, x_in, i + 2, n, C, LN1["turned"])
                            if kind == "start" and n == GB - 1:
                                eng.wait_ge(consts_loaded, NCON)
                                eng.tensor_scalar(bq1[:, :], bqc[:, :], 1.0, None, ALU.add).then_inc(bias_ready, 1)
                                eng.tensor_scalar(bk1[:, :], bkc[:, :], 1.0, None, ALU.add).then_inc(bias_ready, 1)
                                eng.wait_ge(bias_ready, 2)
                                eng.memset(xks[KR:KR + 2, :, :], 1.0).then_inc(const_ready, 1)
                                eng.wait_ge(weights, NW)
                        elif step == "q" or step == "k":
                            qk_out(kind, i + 2, step, n)
                        elif step == "q_split":
                            rest("q", i + 2, qf, qp)
                        elif step == "k_split":
                            rest("k", i + 2, kf, kp)
                        elif step == "v":
                            v_out(kind, i + 2, n)
                        elif step == "xk":
                            rest_psum(kind, "xk", i + 1, kf, kp, n)
                        elif step == "xq":
                            rest_xq(kind, i + 1, n)
                        elif step == "lin_divide":
                            divide(kind, f"sl{n}", i + 1, 0, n)
                        elif step == "out_project":
                            residual1(kind, i + 1, n)
                        elif step == "ln2":
                            normalise(LN2, 1, xn2, x1, i + 1, n, C, LN2["turned"])
                        elif step == "max_scores":
                            maximum(i, n)
                        elif step == "shift":
                            shift(i, n)
                        elif step == "x_divide":
                            residual2(kind, i, n)
                        elif step == "ln3":
                            normalise(LN3, 2, xn3, x2, i - 1 if n == 3 else i, n, 2 * C, x2T_psum)
                        elif step == "low_bits":
                            low_bits_of(i, n)

                each_turn(eng, body)

            @block.tensor
            def _(eng):
                eng.wait_ge(consts_loaded, NCON)
                eng.wait_ge(act_const, 1)

                def turn(kind, i, g, src, name, ready, done, n, c):
                    eng.wait_ge(ready, GB * g + GB)
                    wait_pbank(eng, kind, i, f"{name}{n}")
                    for b in range(GB):
                        mm = eng.transpose(pbank(kind, f"{name}{n}")[:, b * S:(b + 1) * S], src[:, b, c * P:(c + 1) * P], ident)
                    mm.then_inc(done, 1)

                def project(kind, i, name, w, src, done, m):
                    wait_pbank(eng, kind, i, f"{name}{m}")
                    for c in range(C):
                        mm = eng.matmul(pbank(kind, f"{name}{m}")[:, :], w[:, c, m * P:(m + 1) * P], src[:, c, :],
                                        start=(c == 0), stop=(c == C - 1))
                    mm.then_inc(done, 1)

                def turn_ln2(kind, i, g, n):
                    eng.wait_ge(LN2["xn"], GB * g + 2 * n + 2)
                    wait_pbank(eng, kind, i, f"ln2T{n}")
                    for c in range(C):
                        for b in range(2):
                            mm = eng.transpose(pbank(kind, f"ln2T{n}")[:, c * TH + b * S:c * TH + (b + 1) * S],
                                               xn2[:, 2 * n + b, c * P:(c + 1) * P], ident)
                    mm.then_inc(LN2["turned"], 1)

                def project_xq(kind, i, g, n):
                    eng.wait_ge(LN2["xnT"], 2 * g + n + 1)
                    wait_pbank(eng, kind, i, f"xq{n}")
                    for m in range(C):
                        for c in range(C):
                            mm = eng.matmul(pbank(kind, f"xq{n}")[:, m * TH:(m + 1) * TH], xwq[:, c, m * P:(m + 1) * P],
                                            xn2T[:, c, token_half(n)], start=(c == 0), stop=(c == C - 1))
                    mm.then_inc(xq_psum, 1)

                def values(kind, i, name, w, src, done, n):
                    wait_pbank(eng, kind, i, f"{name}{n}")
                    for b in (2 * n, 2 * n + 1):
                        for c in range(C):
                            mm = eng.matmul(pbank(kind, f"{name}{n}")[:, b % 2 * D:b % 2 * D + D],
                                            src[:, c, b * S:(b + 1) * S], w[:, c, :],
                                            start=(c == 0), stop=(c == C - 1))
                    mm.then_inc(done, 1)

                def lin_scores(i, n):
                    b, h = n // 4, 4 * (n % 4)
                    if n == 0:
                        eng.wait_ge(PART["q"][5], 16 * len(ROWS["q"]) * (i + 1))
                        eng.wait_ge(PART["k"][5], 16 * len(ROWS["k"]) * (i + 1))
                    wait_count(eng, lin_c, NU * i + n)
                    for j in range(4):
                        mm = eng.matmul(lin_bank[:, j * S:(j + 1) * S], ks[:, h + j, b * S:(b + 1) * S],
                                        qs[:, h + j, b * S:(b + 1) * S], start=True, stop=True)
                    mm.then_inc(lin_s, 1)

                def add_up(g, part, n, vt, ready):
                    b, h = n // 4, 4 * (n % 4)
                    eng.wait_ge(ready, NU * g + n + 1)
                    if n % 4 == 0:
                        wait_count(eng, sums_done[part], GB * g + b)
                    for r in range(4):
                        mm = eng.matmul(ob[part][32 * r:32 * r + 32, n % 4 * S:(n % 4 + 1) * S], vt[:, b, h + r, :],
                                        att[:, part, n % NA, r, :], start=True, stop=True, tile_position=(0, 32 * r))
                    mm.then_inc(av_done[part], 1)

                def turn_sums(kind, use, i, g, part, b):
                    eng.wait_ge(sums_done[part], GB * g + b + 1)
                    wait_pbank(eng, kind, i, use)
                    for u in range(4):
                        mm = eng.transpose(pbank(kind, use)[:, u * P:(u + 1) * P], sums[:, part, u, :], ident)
                    mm.then_inc(turned_sums[part], 1)

                def turn_o(kind, i, g, b):
                    eng.wait_ge(divided[0], GB * g + b + 1)
                    wait_pbank(eng, kind, i, f"on{b}")
                    for c in range(C):
                        mm = eng.transpose(pbank(kind, f"on{b}")[:, c * S:(c + 1) * S], o[:, 0, c * P:(c + 1) * P], ident)
                    mm.then_inc(on_turned, 1)

                def out_project(kind, i, g, b):
                    eng.wait_ge(oT_done, GB * g + b + 1)
                    wait_pbank(eng, kind, i, f"wo{b}")
                    for c in range(C):
                        mm = eng.matmul(pbank(kind, f"wo{b}")[:, 0:D], oT[:, b % 2, c, :], wo[:, c, :],
                                        start=(c == 0), stop=(c == C - 1))
                    mm.then_inc(wo_psum, 1)

                def max_scores(i, n):
                    b, h = n // 4, 4 * (n % 4)
                    if n % (NU // 2) == 0:
                        half = 2 * n // NU
                        eng.wait_ge(PART["xq"][5 + half], 16 * len(ROWS["xq"]) * (i + 1))
                        eng.wait_ge(PART["xk"][5 + half], 16 * len(ROWS["xk"]) * (i + 1))
                    wait_sbank(eng, i, "max_scores", n)
                    for j in range(4):
                        mm = eng.matmul(sbank("max_scores", n)[:, j * S:(j + 1) * S], xqs[0:KR, h + j, b * S:(b + 1) * S],
                                        xks[0:KR, h + j, b * S:(b + 1) * S], start=True, stop=True)
                    mm.then_inc(max_psum, 1)

                def turn_shift(kind, i, b):
                    eng.wait_ge(sh_lo, GB * i + b + 1)
                    wait_pbank(eng, kind, i, f"sh{b}")
                    eng.transpose(pbank(kind, f"sh{b}")[0:32, 0:S // 2].bitcast(BF16),
                                  nshift[:, b % 2, :, :].rearrange("p a h -> p (a h)"), identb[:, :]).then_inc(sh_psum, 1)

                def x_scores(i, n):
                    b, h = n // 4, 4 * (n % 4)
                    if n % 4 == 0:
                        eng.wait_ge(sh_rows[b % 2], 32 * (2 * i + b // 2) + 32)
                    wait_sbank(eng, i, "x_scores", n)
                    for j in range(4):
                        mm = eng.matmul(sbank("x_scores", n)[:, j * S:(j + 1) * S], xks[:, h + j, b * S:(b + 1) * S],
                                        xqs[:, h + j, b * S:(b + 1) * S], start=True, stop=True)
                    mm.then_inc(x_s, 1)

                def body(kind, i):
                    if kind == "end":
                        eng.wait_ge(low_done, NB * G + 1)
                        eng.matmul(lin_bank[0:1, 0:1], low[:, NB * G:NB * G + 1], causal[:, P - 1:P], start=True, stop=True).then_inc(low_psum, 1)
                    for step, n in steps(kind, "tensor"):
                        if step == "ln1T":
                            turn(kind, i, i + 2, xn1, "ln1T", LN1["xn"], LN1["turned"], n, n)
                        elif step == "q":
                            if kind == "start" and n == 0:
                                eng.wait_ge(weights, NW)
                            eng.wait_ge(LN1["xnT"], C * (i + 2) + C)
                            project(kind, i, "q", wq, xn1T, qk_psum, n)
                        elif step == "k":
                            project(kind, i, "k", wk, xn1T, qk_psum, n)
                        elif step == "v":
                            values(kind, i, "v", wv, xn1T, v_psum, n)
                        elif step == "xk":
                            eng.wait_ge(ctx_loaded, 16 * (i + 1) + 16)
                            project(kind, i, "xk", xwk, ctxs, xk_psum, n)
                        elif step == "xv":
                            values(kind, i, "xv", xwv, ctxs, xv_psum, n)
                        elif step == "lin_scores":
                            lin_scores(i + 1, n)
                        elif step == "lin_sums":
                            if n == 0:
                                eng.wait_ge(v_done, 2 * (i + 1) + 2)
                            add_up(i + 1, 0, n, v, lin_a)
                        elif step == "lin_divide":
                            turn_sums(kind, f"sl{n}", i, i + 1, 0, n)
                        elif step == "lin_turn":
                            turn_o(kind, i, i + 1, n)
                        elif step == "out_project":
                            out_project(kind, i, i + 1, n)
                        elif step == "ln2T":
                            turn_ln2(kind, i, i + 1, n)
                        elif step == "xq":
                            project_xq(kind, i, i + 1, n)
                        elif step == "max_scores":
                            max_scores(i, n)
                        elif step == "shift":
                            turn_shift(kind, i, n)
                        elif step == "x_scores":
                            x_scores(i, n)
                        elif step == "x_sums":
                            if n == 0:
                                eng.wait_ge(xv_done, 2 * i + 2)
                            add_up(i, 1, n, xv, x_e)
                        elif step == "x_divide":
                            turn_sums(kind, f"sx{n}", i, i, 1, n)
                        elif step == "x2T":
                            src, ready = ((x2, x2_done), (xn3, LN3["xn"]))[n // C]
                            turn(kind, i, i - 1, src, "x2T", ready, x2T_psum, n, n % C)

                each_turn(eng, body)

        ctx = ExitStack()
        with ctx:
            def sb(name, shape, dt=F32):
                return ctx.enter_context(nc.sbuf_tensor(name, shape, dt))

            sb("place_of_w12_r_and_h1_r", [P, KH * 2 * C * P + KH * KH * P])
            FA = nc.alloc_sbuf_tensor_at("general_hidden_a", [P, KH, T], F32, offset=base)
            FB = nc.alloc_sbuf_tensor_at("general_hidden_b", [P, KH, T], F32, offset=base + KH * T * 4)
            FW = nc.alloc_sbuf_tensor_at("general_weights", [P, 2, KH, P], F32, offset=base + 2 * KH * T * 4)
            h2r = sb("h2_r", [P, KH, KH, P], F32R)
            w3r = sb("w3_r", [P, C, KH, P], F32R)
            HA = sb("hidden_a", [P, 2, KH, T], F32R)
            HB = sb("hidden_b", [P, 2, KH, T], F32R)
            xin = sb("ffn_in", [P, C, T])
            xhl = sb("ffn_in_parts", [P, 2, C, T], F32R)
            res = sb("ffn_residual", [P, C, T])
            gate = sb("gate", [P, 2, T])
            full = sb("hidden_full", [P, 4, T])
            s1h, s12 = sb("s1h", [P, KH]), sb("s12", [P, KH])

            bank = [ctx.enter_context(nc.psum_tensor(f"ffn_bank{n}", [P, T], F32)) for n in range(8)]
            s1h_done, s12_done = sem("s1h_done"), sem("s12_done")
            in_loaded, res_loaded = sem("ffn_in_loaded"), sem("residual_loaded")
            hi_done, in_done = sem("in_hi"), sem("in_parts")
            gate_psum, gate_act, gate_mul, gate_full = (sem(n) for n in ("gate_psum", "gate_act", "gate_mul", "gate_full"))
            gate_hi, gate_lo = sem("gate_hi"), sem("gate_lo")
            h_psum, h_full, h_hi, h_lo = sem("h_psum"), sem("h_full"), sem("h_hi"), sem("h_lo")
            o_psum, o_done, o_stored = sem("o_psum"), sem("o_done"), sem("o_stored")
            g_loaded = [sem(f"general_weights_loaded{n}") for n in range(2)]
            out_t = sb("out_tile", [P, C, T])

            def some(n):
                return not isinstance(n, int) or n > 0

            def exact_gpsimd(eng):
                for dst, src, s in ((h1r[:, half:KH], h1[:, half:KH], "h1b"),
                                    (h2r[:, :], h2[:, :], "h2"), (w3r[:, :], w3[:, :], "w3")):
                    if s == "w3":
                        eng.wait_ge(stored, 32 * G)
                    eng.dma_start(dst, src).then_inc(w_loaded[s], 16)

                def gate_rest(i, m):
                    eng.wait_ge(gate_hi, KH * i + m + 1)
                    eng.tensor_tensor(HA[:, 1, m, :], full[:, m % 4, :], HA[:, 0, m, :].bitcast(F32), ALU.subtract)\
                       .then_inc(gate_lo, 1)

                def body(i):
                    for m in range(KH):
                        gate_rest(i, m)

                body(0)
                with eng.Fori(1, G) as i:
                    body(i)

            def exact_sync(eng):
                eng.dma_start(xin[:, :, :], tokens(xnT_d, 0)).then_inc(in_loaded, 16)
                eng.dma_start(res[:, :, :], tokens(x2T_d, 0)).then_inc(res_loaded, 16)
                eng.wait_ge(stored, 32 * G)

                def store(i):
                    eng.wait_ge(o_done, C * i + C)
                    eng.dma_start(tokens(outT, i), out_t[:, :, :]).then_inc(o_stored, 16)

                with eng.Fori(1, G) as i:
                    eng.wait_ge(in_done, i)
                    eng.dma_start(xin[:, :, :], tokens(xnT_d, i)).then_inc(in_loaded, 16)
                    store(i - 1)
                    eng.dma_start(res[:, :, :], tokens(x2T_d, i)).then_inc(res_loaded, 16)
                store(G - 1)
                eng.wait_ge(o_stored, 16 * G)

            def exact_scalar(eng):
                eng.preload_act_table(ACT.Gelu)
                eng.activation(s1h[:, :], s1c[:, :], ACT.Copy, scale=0.5).then_inc(s1h_done, 1)
                eng.wait_ge(s1h_done, 1)

                def split_in(i):
                    eng.wait_ge(in_loaded, 16 * i + 16)
                    if some(i):
                        eng.wait_ge(gate_psum, KH * i)
                    eng.activation(xhl[:, 0, :, :], xin[:, :, :], ACT.Copy).then_inc(hi_done, 1)

                def gates(i, m):
                    eng.wait_ge(gate_psum, KH * i + m + 1)
                    if some(KH * i + m - 1):
                        eng.wait_ge(gate_mul, KH * i + m - 1)
                    eng.activation(gate[:, m % 2, :], bank[2 * m % 8][:, :], ACT.Tanh, scale=s1h[:, m:m + 1])\
                       .then_inc(gate_act, 1)

                def gate_round(i, m):
                    eng.wait_ge(gate_full, KH * i + m + 1)
                    if m == 0 and some(i):
                        eng.wait_ge(o_psum, C * i)
                    eng.activation(HA[:, 0, m, :], full[:, m % 4, :], ACT.Copy).then_inc(gate_hi, 1)

                def hidden(i, n):
                    m, layer = n % KH, n // KH
                    src, dst, sc = bank[n % 4], (HB, HA)[layer], (sh1c, sh2c)[layer][:, m:m + 1]
                    eng.wait_ge(h_psum, 2 * KH * i + n + 1)
                    if n >= 4:
                        eng.wait_ge(h_lo, 2 * KH * i + n - 3)
                    else:
                        eng.wait_ge(gate_lo, KH * i + KH - 3 + n)
                    eng.activation(full[:, n % 4, :], src[:, :], ACT.Gelu, scale=sc).then_inc(h_full, 1)
                    if n == 0 and some(i):
                        eng.wait_ge(h_psum, 2 * KH * i)
                    eng.activation(dst[:, 0, m, :], src[:, :], ACT.Gelu, scale=sc).then_inc(h_hi, 1)

                split_in(0)

                def body(i, last=False):
                    for m in range(KH):
                        gates(i, m)
                        if m >= 1:
                            gate_round(i, m - 1)
                    gate_round(i, KH - 1)
                    for n in range(2 * KH):
                        hidden(i, n)
                        if n == 2 and not last:
                            split_in(i + 1)

                body(0)
                with eng.Fori(1, G - 1) as i:
                    body(i)
                body(G - 1, last=True)

            def exact_vector(eng):
                eng.scalar_tensor_tensor(s12[:, :], s1c[:, :], 0.5, s2c[:, :], ALU.mult, ALU.mult).then_inc(s12_done, 1)
                eng.wait_ge(s12_done, 1)

                def rest_in(i):
                    eng.wait_ge(hi_done, i + 1)
                    eng.tensor_tensor(xhl[:, 1, :, :], xin[:, :, :], xhl[:, 0, :, :].bitcast(F32), ALU.subtract)\
                       .then_inc(in_done, 1)

                def gated(i, m):
                    eng.wait_ge(gate_act, KH * i + m + 1)
                    f = full[:, m % 4, :]
                    if m < 4:
                        if some(i):
                            eng.wait_ge(h_lo, 2 * KH * i - 3 + m)
                    else:
                        eng.wait_ge(gate_lo, KH * i + m - 3)
                    eng.scalar_tensor_tensor(f, gate[:, m % 2, :], 1.0, bank[2 * m % 8][:, :], ALU.add, ALU.mult)\
                       .then_inc(gate_mul, 1)
                    eng.wait_ge(gate_mul, KH * i + m + 1)
                    eng.scalar_tensor_tensor(f, bank[2 * m % 8 + 1][:, :], s12[:, m:m + 1], f, ALU.mult, ALU.mult)\
                       .then_inc(gate_full, 1)

                def hidden_rest(i, n):
                    m, dst = n % KH, (HB, HA)[n // KH]
                    eng.wait_ge(h_hi, 2 * KH * i + n + 1)
                    eng.tensor_tensor(dst[:, 1, m, :], full[:, n % 4, :], dst[:, 0, m, :].bitcast(F32), ALU.subtract)\
                       .then_inc(h_lo, 1)

                def output(i, c):
                    eng.wait_ge(o_psum, C * i + c + 1)
                    eng.wait_ge(res_loaded, 16 * i + 16)
                    if c == 0 and some(i):
                        eng.wait_ge(o_stored, 16 * i)
                    eng.scalar_tensor_tensor(out_t[:, c, :], bank[4 + c][:, :], s3c[:, c:c + 1], res[:, c, :],
                                             ALU.mult, ALU.add).then_inc(o_done, 1)

                rest_in(0)

                def body(i, last=False):
                    for m in range(KH):
                        gated(i, m)
                    for n in range(2 * KH):
                        hidden_rest(i, n)
                        if n == 2 and not last:
                            rest_in(i + 1)
                    for c in range(C):
                        output(i, c)

                body(0)
                with eng.Fori(1, G - 1) as i:
                    body(i)
                body(G - 1, last=True)

            def exact_tensor(eng):
                def products(out, w, src, n):
                    for kk in range(n):
                        for part in range(2):
                            mm = eng.matmul(out[:, :], w(kk), src[:, part, kk, :],
                                            start=(kk == 0 and part == 0), stop=(kk == n - 1 and part == 1))
                    return mm

                def hidden(i, n, tiles):
                    m, w, src = n % KH, (h1r, h2r)[n // KH], (HA, HB)[n // KH]
                    for kk in tiles:
                        if n == 0:
                            eng.wait_ge(gate_lo, KH * i + kk + 1)
                        elif n == KH:
                            eng.wait_ge(h_lo, 2 * KH * i + kk + 1)
                        for part in range(2):
                            mm = eng.matmul(bank[n % 4][:, :], w[:, m, kk, :], src[:, part, kk, :],
                                            start=(kk == 0 and part == 0), stop=(kk == KH - 1 and part == 1))
                    if kk == KH - 1:
                        mm.then_inc(h_psum, 1)

                def body(i):
                    eng.wait_ge(in_done, i + 1)
                    for m in range(KH):
                        if m == 0:
                            eng.wait_ge(w_loaded["w12a"], 16)
                        if m == KH // 2:
                            eng.wait_ge(w_loaded["w12b"], 16)
                        if m < 2 and some(i):
                            eng.wait_ge(h_hi, 2 * KH * i - 2 + 2 * m)
                        if m == 2 and some(i):
                            eng.wait_ge(o_done, C * i)
                        if m >= 4:
                            eng.wait_ge(gate_full, KH * i + m - 3)
                        for z in range(2):
                            mm = products(bank[2 * m % 8 + z], lambda kk: w12r[:, m, z, kk, :], xhl, C)
                        mm.then_inc(gate_psum, 1)
                    eng.wait_ge(w_loaded["h1a"], 16)
                    eng.wait_ge(gate_full, KH * i + 5)
                    hidden(i, 0, range(KH - 1))
                    hidden(i, 1, range(KH - 1))
                    hidden(i, 0, [KH - 1])
                    hidden(i, 1, [KH - 1])
                    for n in range(2, 2 * KH):
                        if n == KH // 2:
                            eng.wait_ge(w_loaded["h1b"], 16)
                        if n == KH:
                            eng.wait_ge(w_loaded["h2"], 16)
                        if n >= 4:
                            eng.wait_ge(h_hi, 2 * KH * i + n - 3)
                        else:
                            eng.wait_ge(gate_full, KH * i + 6)
                        hidden(i, n, range(KH))
                    eng.wait_ge(w_loaded["w3"], 16)
                    eng.wait_ge(gate_full, KH * i + KH - 1)
                    for c in range(C):
                        for kk in range(KH):
                            if c == 0:
                                eng.wait_ge(h_lo, 2 * KH * i + KH + kk + 1)
                            for part in range(2):
                                mm = eng.matmul(bank[4 + c][:, :], w3r[:, c, kk, :], HA[:, part, kk, :],
                                                start=(kk == 0 and part == 0), stop=(kk == KH - 1 and part == 1))
                        mm.then_inc(o_psum, 1)

                body(0)
                with eng.Fori(1, G) as i:
                    body(i)

            NT = KH + 2 * KH + C

            def general_sync(eng):
                def body(i):
                    if some(i):
                        eng.wait_ge(o_done, C * i)
                    eng.dma_start(xin[:, :, :], tokens(xnT_d, i)).then_inc(in_loaded, 16)
                    eng.dma_start(res[:, :, :], tokens(x2T_d, i)).then_inc(res_loaded, 16)
                    if not some(i):
                        eng.wait_ge(stored, 32 * G)
                    for j in range(NT):
                        used = j - 2
                        if 0 <= used < KH:
                            eng.wait_ge(gate_psum, KH * i + used + 1)
                        elif KH <= used < 3 * KH:
                            eng.wait_ge(h_psum, 2 * KH * i + used - KH + 1)
                        if j < KH:
                            src = w12[:, j].rearrange("p z k o -> p (z k) o")
                        elif j < 2 * KH:
                            src = h1[:, j - KH]
                        elif j < 3 * KH:
                            src = h2[:, j - 2 * KH]
                        else:
                            src = w3[:, j - 3 * KH]
                        eng.dma_start(FW[:, j % 2, 0:src.shape[1], :], src).then_inc(g_loaded[j % 2], 16)
                    eng.wait_ge(o_done, C * i + C)
                    eng.dma_start(tokens(outT, i), out_t[:, :, :]).then_inc(o_stored, 16)

                body(0)
                with eng.Fori(1, G) as i:
                    body(i)
                eng.wait_ge(o_stored, 16 * G)

            def general_scalar(eng):
                eng.activation(s1h[:, :], s1c[:, :], ACT.Copy, scale=0.5).then_inc(s1h_done, 1)
                eng.wait_ge(s1h_done, 1)

                def body(i):
                    for m in range(KH):
                        eng.wait_ge(gate_psum, KH * i + m + 1)
                        if some(KH * i + m):
                            eng.wait_ge(gate_mul, KH * i + m)
                        eng.activation(gate[:, 0, :], bank[2 * m % 4][:, :], ACT.Tanh, scale=s1h[:, m:m + 1])\
                           .then_inc(gate_act, 1)
                    for n in range(2 * KH):
                        m, dst, sc = n % KH, (FB, FA)[n // KH], (sh1c, sh2c)[n // KH]
                        eng.wait_ge(h_psum, 2 * KH * i + n + 1)
                        eng.activation(dst[:, m, :], bank[4 + n % 4][:, :], ACT.Gelu, scale=sc[:, m:m + 1])\
                           .then_inc(h_full, 1)

                body(0)
                with eng.Fori(1, G) as i:
                    body(i)

            def general_vector(eng):
                eng.scalar_tensor_tensor(s12[:, :], s1c[:, :], 0.5, s2c[:, :], ALU.mult, ALU.mult).then_inc(s12_done, 1)
                eng.wait_ge(s12_done, 1)

                def body(i):
                    for m in range(KH):
                        eng.wait_ge(gate_act, KH * i + m + 1)
                        eng.scalar_tensor_tensor(FA[:, m, :], gate[:, 0, :], 1.0, bank[2 * m % 4][:, :], ALU.add, ALU.mult)\
                           .then_inc(gate_mul, 1)
                        eng.wait_ge(gate_mul, KH * i + m + 1)
                        eng.scalar_tensor_tensor(FA[:, m, :], bank[2 * m % 4 + 1][:, :], s12[:, m:m + 1], FA[:, m, :],
                                                 ALU.mult, ALU.mult).then_inc(gate_full, 1)
                    eng.wait_ge(res_loaded, 16 * i + 16)
                    if some(i):
                        eng.wait_ge(o_stored, 16 * i)
                    for c in range(C):
                        eng.wait_ge(o_psum, C * i + c + 1)
                        eng.scalar_tensor_tensor(out_t[:, c, :], bank[c][:, :], s3c[:, c:c + 1], res[:, c, :],
                                                 ALU.mult, ALU.add).then_inc(o_done, 1)

                body(0)
                with eng.Fori(1, G) as i:
                    body(i)

            def general_tensor(eng):
                def body(i):
                    eng.wait_ge(in_loaded, 16 * i + 16)
                    for j in range(NT):
                        eng.wait_ge(g_loaded[j % 2], 16 * (NT // 2 * i + j // 2) + 16)
                        if j < KH:
                            if j == 0 and some(i):
                                eng.wait_ge(o_done, C * i)
                            if j >= 2:
                                eng.wait_ge(gate_full, KH * i + j - 1)
                            for z in range(2):
                                for kk in range(C):
                                    mm = eng.matmul(bank[2 * j % 4 + z][:, :], FW[:, j % 2, C * z + kk, :], xin[:, kk, :],
                                                    start=(kk == 0), stop=(kk == C - 1))
                            mm.then_inc(gate_psum, 1)
                        elif j < 3 * KH:
                            n = j - KH
                            if n == 0:
                                eng.wait_ge(gate_full, KH * i + KH)
                            if n == KH:
                                eng.wait_ge(h_full, 2 * KH * i + KH)
                            if some(2 * KH * i + n - 3):
                                eng.wait_ge(h_full, 2 * KH * i + n - 3)
                            for kk in range(KH):
                                mm = eng.matmul(bank[4 + n % 4][:, :], FW[:, j % 2, kk, :], (FA, FB)[n // KH][:, kk, :],
                                                start=(kk == 0), stop=(kk == KH - 1))
                            mm.then_inc(h_psum, 1)
                        else:
                            c = j - 3 * KH
                            if c == 0:
                                eng.wait_ge(h_full, 2 * KH * i + 2 * KH)
                            for kk in range(KH):
                                mm = eng.matmul(bank[c][:, :], FW[:, j % 2, kk, :], FA[:, kk, :],
                                                start=(kk == 0), stop=(kk == KH - 1))
                            mm.then_inc(o_psum, 1)

                body(0)
                with eng.Fori(1, G) as i:
                    body(i)

            block = ctx.enter_context(nc.Block())

            def inexact(eng):
                for _, _, s in EARLY:
                    eng.wait_ge(w_loaded[s], 16)
                eng.wait_ge(flag_ready, 1)
                return eng.value_load(flag[0:1, 0:1], min_val=0, max_val=1) != 0

            @block.gpsimd
            def _(eng):
                with eng.If(inexact(eng)):
                    pass
                with eng.Else():
                    exact_gpsimd(eng)

            @block.sync
            def _(eng):
                with eng.If(inexact(eng)):
                    general_sync(eng)
                with eng.Else():
                    exact_sync(eng)

            @block.scalar
            def _(eng):
                with eng.If(inexact(eng)):
                    general_scalar(eng)
                with eng.Else():
                    exact_scalar(eng)

            @block.vector
            def _(eng):
                with eng.If(inexact(eng)):
                    general_vector(eng)
                with eng.Else():
                    exact_vector(eng)

            @block.tensor
            def _(eng):
                with eng.If(inexact(eng)):
                    general_tensor(eng)
                with eng.Else():
                    exact_tensor(eng)


_INS = ["x", "ctxT", "wqT", "wkT", "wvT", "woT", "bv", "bo", "xqT", "xkT", "xvT",
        "w12", "h1", "h2", "w3", "columns", "consts"]


def constants():
    import numpy as np
    c = np.zeros((128, 256), np.float32)
    c[:, 0:128] = np.eye(128)
    c[:, 128:256] = np.triu(np.ones((128, 128)))
    return c


def kernel(**inputs):
    import numpy as np
    import concourse.bacc as bacc
    from concourse.bass_utils import run_bass_kernel_spmd

    a = {n: np.asarray(v) for n, v in inputs.items()}
    B, S, D = a["x"].shape

    def turned(w):
        return np.ascontiguousarray(np.transpose(w))

    def by_head(w):
        return np.ascontiguousarray(np.transpose(w.reshape(-1, 8, 2, 16), (0, 2, 3, 1))).reshape(-1, D)

    def by_tile(w, columns):
        o, i = w.shape
        return np.ascontiguousarray(np.transpose(w.reshape(o // columns, columns, i // 128, 128), (3, 0, 2, 1)))

    w1, w2 = by_tile(a["L0_ffn_w1_w"], 128), by_tile(a["L0_ffn_w2_w"], 128)
    arrays = {
        "x": np.ascontiguousarray(a["x"]),
        "ctxT": turned(a["ctx_1024"].reshape(B * S, D)),
        "wqT": by_head(turned(a["L0_attn_Wq"])), "wkT": by_head(turned(a["L0_attn_Wk"])),
        "wvT": turned(a["L0_attn_Wv"]), "woT": turned(a["L0_attn_Wo"]),
        "bv": a["L0_attn_bv"], "bo": a["L0_attn_bo"],
        "xqT": by_head(turned(a["L0_xattn_Wq"])), "xkT": by_head(turned(a["L0_xattn_Wk"])), "xvT": turned(a["L0_xattn_Wv"]),
        "w12": np.ascontiguousarray(np.stack([w1, w2], axis=2)),
        "h1": by_tile(a["L0_ffn_h1_w"], 128), "h2": by_tile(a["L0_ffn_h2_w"], 128),
        "w3": by_tile(a["L0_ffn_w3_w"], 128),
        "columns": np.ascontiguousarray(np.concatenate(
            [np.transpose(w.reshape(-1, 128)) for w in (
                *(a[f"L0_ffn_{n}_s"] for n in ("w1", "w2", "h1", "h2", "w3")),
                by_head(a["L0_attn_bq"][None])[0], by_head(a["L0_attn_bk"][None])[0])], axis=1)),
        "consts": constants(),
    }
    nc = bacc.Bacc("TRN2", target_bir_lowering=False, num_devices=1)
    args = [nc.dram_tensor(f"in_{n}", arrays[n].shape, mybir.dt.from_np(arrays[n].dtype), kind="ExternalInput").ap()
            for n in _INS]
    out = nc.dram_tensor("out_T", (D, B * S), mybir.dt.float32, kind="ExternalOutput").ap()
    decoder_layer_program(nc, *args, out)
    r = run_bass_kernel_spmd(nc, [{f"in_{n}": arrays[n] for n in _INS}], core_ids=[0])
    return np.ascontiguousarray(np.transpose(r.results[0]["out_T"])).reshape(B, S, D)
```
